# Optimizing a Trainium2 kernel written in Bass

```python
import numpy as np
import jax
import jax.numpy as jnp

def _softmax(x, axis=-1):
    return jax.nn.softmax(x, axis=axis)

def _gelu(x):
    return jax.nn.gelu(x, approximate=True)

def _silu(x):
    return jax.nn.silu(x)

def _sigmoid(x):
    return jax.nn.sigmoid(x)

def _layernorm(x, axis=-1, eps=1e-05):
    m = jnp.mean(x, axis=axis, keepdims=True)
    v = jnp.var(x, axis=axis, keepdims=True)
    return (x - m) / jnp.sqrt(v + eps)

def _scatter_add(tgt, idx, src, axis=0):
    return tgt.at[idx].add(src)

def _segment_sum(src, seg, n):
    return jax.ops.segment_sum(src, seg, n)
kernel_name = 'mk_decoder_postln_d2_seqx_r8_0e399c'

def setup_inputs(seed: int=0):
    np.random.seed(seed)
    _w = jnp.asarray

    def _rec_inputs():
        import jax
        import jax.numpy as jnp
        _rk = jax.random.key(seed)
        x = -0.0002928 + 1 * jax.random.normal(jax.random.fold_in(_rk, 1), (4, 256, 128), jnp.float32)
        _lenS = 256 - jax.random.randint(jax.random.fold_in(_rk, 7), (4,), 0, max(1, 256 // 4) + 1, jnp.int32)
        _lenS2 = 64 - jax.random.randint(jax.random.fold_in(_rk, 8), (4,), 0, max(1, 64 // 4) + 1, jnp.int32)
        _ctx_1024P = jax.random.normal(jax.random.fold_in(_rk, 11), (4, 16, 128), jnp.float32)
        _ctx_1024c = jax.random.dirichlet(jax.random.fold_in(_rk, 511), 0.3 * jnp.ones((16,), jnp.float32), (4, 64))
        _ctx_1024t = jnp.einsum('bsk,bkd->bsd', _ctx_1024c, _ctx_1024P)
        _ctx_1024t = _ctx_1024t * jax.lax.rsqrt(jnp.mean(jnp.square(_ctx_1024t)) + 1e-12) * 0.953939
        ctx_1024 = -1.39393e-06 + 0.999914 * (_ctx_1024t + 0.3 * jax.random.normal(jax.random.fold_in(_rk, 611), (4, 64, 128), jnp.float32))
        fside_BxSxS2_0 = -4.48278e-06 + 1.00019 * jax.random.normal(jax.random.fold_in(_rk, 12), (4, 256, 64), jnp.float32)
        _validS = jnp.arange(256)[None, :] < _lenS[:, None]
        _validS2 = jnp.arange(64)[None, :] < _lenS2[:, None]
        _causal = jnp.tril(jnp.ones((256, 256), dtype=bool))
        mask_BxSxS2_ff0 = jnp.where(jnp.ones((4, 256, 64), dtype=bool), 0.0, -1000000000.0).astype(jnp.float32)
        return (x, ctx_1024, fside_BxSxS2_0, mask_BxSxS2_ff0)
    x, ctx_1024, fside_BxSxS2_0, mask_BxSxS2_ff0 = _rec_inputs()

    def _L0_attn_setup():
        import jax, jax.numpy as jnp
        import numpy as np
        MODEL_DIM = 128
        HEADS = 16
        HEAD_DIM = MODEL_DIM // HEADS
        B, T = (2, 256)
        TB_LEN = 500
        key = jax.random.key(seed)
        ks = jax.random.split(key, 12)
        s = 0.02
        d = MODEL_DIM
        return {'x': jax.random.normal(ks[0], (B, T, d), dtype=jnp.float32), 'Wq': jax.random.normal(ks[1], (d, d), dtype=jnp.float32) * s, 'bq': jnp.zeros((d,), jnp.float32), 'Wk': jax.random.normal(ks[2], (d, d), dtype=jnp.float32) * s, 'bk': jnp.zeros((d,), jnp.float32), 'Wv': jax.random.normal(ks[3], (d, d), dtype=jnp.float32) * s, 'bv': jnp.zeros((d,), jnp.float32), 'Wo': jax.random.normal(ks[4], (d, d), dtype=jnp.float32) * s, 'bo': jnp.zeros((d,), jnp.float32), 'et_gate': jax.random.normal(ks[5], (1, 1, 1), dtype=jnp.float32), 'is_gate': jax.random.normal(ks[6], (1, 1, 1), dtype=jnp.float32), 'time_bias': jnp.linspace(-1.0, 1.0, TB_LEN, dtype=jnp.float32).reshape(1, 1, TB_LEN)}
    _L0_attn_all = _L0_attn_setup()
    _L0_attn_in = {k: v for k, v in _L0_attn_all.items() if k in ('Wq', 'bq', 'Wk', 'bk', 'Wv', 'bv', 'Wo', 'bo', 'et_gate', 'is_gate', 'time_bias')}
    del _L0_attn_all

    def _L0_xattn_setup():
        import jax, jax.numpy as jnp
        import numpy as np
        HIDDEN = 128
        HEADS = 16
        DK = HIDDEN // HEADS
        B, N = (2, 256)
        key = jax.random.key(seed)
        ks = jax.random.split(key, 12)
        s = 0.02
        return {'q': jax.random.normal(ks[0], (B, N, HIDDEN), jnp.float32), 'k': jax.random.normal(ks[1], (B, N, HIDDEN), jnp.float32), 'v': jax.random.normal(ks[2], (B, N, HIDDEN), jnp.float32), 'attn_bias': jax.random.normal(ks[3], (B, N, N), jnp.float32), 'attention_mask': jnp.zeros((B, N, N), jnp.float32), 'Wq': jax.random.normal(ks[4], (HIDDEN, HIDDEN), jnp.float32) * s, 'bq': jnp.zeros((HIDDEN,), jnp.float32), 'Wk': jax.random.normal(ks[5], (HIDDEN, HIDDEN), jnp.float32) * s, 'bk': jnp.zeros((HIDDEN,), jnp.float32), 'Wv': jax.random.normal(ks[6], (HIDDEN, HIDDEN), jnp.float32) * s, 'bv': jnp.zeros((HIDDEN,), jnp.float32), 'Wo': jax.random.normal(ks[7], (HIDDEN, HIDDEN), jnp.float32) * s, 'bo': jnp.zeros((HIDDEN,), jnp.float32)}
    _L0_xattn_all = _L0_xattn_setup()
    _L0_xattn_in = {k: v for k, v in _L0_xattn_all.items() if k in ('Wq', 'bq', 'Wk', 'bk', 'Wv', 'bv', 'Wo', 'bo')}
    del _L0_xattn_all

    def _L0_ffn_setup():
        import jax, jax.numpy as jnp
        import numpy as np
        B, S, H, E, K = (4, 256, 128, 8, 2)
        key = jax.random.key(seed)
        k0, k1, k2, k3 = jax.random.split(key, 4)
        x = jax.random.normal(k0, (B, S, H), dtype=jnp.float32)
        router_w = jax.random.normal(k1, (E, H), dtype=jnp.float32) * np.float32(1.0 / np.sqrt(H))
        xav1 = np.float32(np.sqrt(2.0 / (2 * H + H)))
        w1 = jax.random.normal(k2, (E, 2 * H, H), dtype=jnp.float32) * xav1
        w2 = jax.random.normal(k3, (E, H, 2 * H), dtype=jnp.float32) * xav1
        return {'x': x, 'router_w': router_w, 'w1': w1, 'w2': w2}
    _L0_ffn_all = _L0_ffn_setup()
    _L0_ffn_in = {k: v for k, v in _L0_ffn_all.items() if k in ('router_w', 'w1', 'w2')}
    del _L0_ffn_all

    def _L1_attn_setup():
        import jax, jax.numpy as jnp
        import numpy as np
        import math
        DIM = 128
        NUM_HEADS = 16
        HEAD_DIM = DIM // NUM_HEADS
        LAYER_IDX = 12
        LAMBDA_INIT = 0.8 - 0.6 * math.exp(-0.3 * (LAYER_IDX - 1))
        LN_EPS = 1e-05
        key = jax.random.key(seed)
        ks = jax.random.split(key, 11)
        B, S = (2, 256)
        x = jax.random.normal(ks[0], (B, S, DIM), dtype=jnp.float32)
        s = 1.0 / math.sqrt(DIM)
        Wq = jax.random.normal(ks[1], (DIM, 2 * DIM), dtype=jnp.float32) * s
        Wk = jax.random.normal(ks[2], (DIM, 2 * DIM), dtype=jnp.float32) * s
        Wv = jax.random.normal(ks[3], (DIM, DIM), dtype=jnp.float32) * s
        Wo = jax.random.normal(ks[4], (DIM, DIM), dtype=jnp.float32) * s
        lambda_q1 = jax.random.normal(ks[5], (HEAD_DIM,), dtype=jnp.float32) * 0.1
        lambda_k1 = jax.random.normal(ks[6], (HEAD_DIM,), dtype=jnp.float32) * 0.1
        lambda_q2 = jax.random.normal(ks[7], (HEAD_DIM,), dtype=jnp.float32) * 0.1
        lambda_k2 = jax.random.normal(ks[8], (HEAD_DIM,), dtype=jnp.float32) * 0.1
        gamma = jnp.ones((DIM,), dtype=jnp.float32)
        beta = jnp.zeros((DIM,), dtype=jnp.float32)
        return {'x': x, 'Wq': Wq, 'Wk': Wk, 'Wv': Wv, 'Wo': Wo, 'lambda_q1': lambda_q1, 'lambda_k1': lambda_k1, 'lambda_q2': lambda_q2, 'lambda_k2': lambda_k2, 'gamma': gamma, 'beta': beta}
    _L1_attn_all = _L1_attn_setup()
    _L1_attn_in = {k: v for k, v in _L1_attn_all.items() if k in ('Wq', 'Wk', 'Wv', 'Wo', 'lambda_q1', 'lambda_k1', 'lambda_q2', 'lambda_k2', 'gamma', 'beta')}
    del _L1_attn_all

    def _L1_xattn_setup():
        import jax, jax.numpy as jnp
        import numpy as np
        B, N, P, DIM, H = (8, 128, 77, 128, 16)
        HD = DIM // H
        LN_EPS = 1e-05
        key = jax.random.key(seed)
        ks = jax.random.split(key, 8)
        s = 0.02
        return {'x': jax.random.normal(ks[0], (B, N, DIM), jnp.float32), 'x_text': jax.random.normal(ks[1], (B, P, DIM), jnp.float32), 'Wq': jax.random.normal(ks[2], (DIM, DIM), jnp.float32) * s, 'Wk': jax.random.normal(ks[3], (DIM, DIM), jnp.float32) * s, 'Wv': jax.random.normal(ks[4], (DIM, DIM), jnp.float32) * s, 'gate': jax.random.normal(ks[5], (1, H, 1, 1), jnp.float32) * 0.5, 'ln_g': jnp.ones((DIM,), jnp.float32), 'ln_b': jnp.zeros((DIM,), jnp.float32), 'Wp': jax.random.normal(ks[6], (DIM, DIM), jnp.float32) * s, 'bp': jnp.zeros((DIM,), jnp.float32)}
    _L1_xattn_all = _L1_xattn_setup()
    _L1_xattn_in = {k: v for k, v in _L1_xattn_all.items() if k in ('Wq', 'Wk', 'Wv', 'gate', 'ln_g', 'ln_b', 'Wp', 'bp')}
    del _L1_xattn_all

    def _L1_ffn_setup():
        import jax, jax.numpy as jnp
        import numpy as np
        H = 128
        I = 256
        E = 8
        TOP_K = 2
        NUM_SHARED = 1
        key = jax.random.key(seed)
        ks = jax.random.split(key, 9)
        s = 0.02
        x = jax.random.normal(ks[0], (2, 256, H), dtype=jnp.float32)
        sg_w = jax.random.normal(ks[1], (I, H), dtype=jnp.float32) * s
        su_w = jax.random.normal(ks[2], (I, H), dtype=jnp.float32) * s
        sd_w = jax.random.normal(ks[3], (H, I), dtype=jnp.float32) * s
        router_w = jax.random.normal(ks[4], (E, H), dtype=jnp.float32) * s
        routing_bias = jnp.zeros((E,), dtype=jnp.float32)
        wg = jax.random.normal(ks[5], (E, I, H), dtype=jnp.float32) * s
        wu = jax.random.normal(ks[6], (E, I, H), dtype=jnp.float32) * s
        wd = jax.random.normal(ks[7], (E, H, I), dtype=jnp.float32) * s
        return {'x': x, 'sg_w': sg_w, 'su_w': su_w, 'sd_w': sd_w, 'router_w': router_w, 'routing_bias': routing_bias, 'wg': wg, 'wu': wu, 'wd': wd}
    _L1_ffn_all = _L1_ffn_setup()
    _L1_ffn_in = {k: v for k, v in _L1_ffn_all.items() if k in ('sg_w', 'su_w', 'sd_w', 'router_w', 'routing_bias', 'wg', 'wu', 'wd')}
    del _L1_ffn_all
    return {'x': x, 'ctx_1024': ctx_1024, 'fside_BxSxS2_0': fside_BxSxS2_0, 'mask_BxSxS2_ff0': mask_BxSxS2_ff0, 'L0_attn_Wq': _L0_attn_in['Wq'], 'L0_attn_bq': _L0_attn_in['bq'], 'L0_attn_Wk': _L0_attn_in['Wk'], 'L0_attn_bk': _L0_attn_in['bk'], 'L0_attn_Wv': _L0_attn_in['Wv'], 'L0_attn_bv': _L0_attn_in['bv'], 'L0_attn_Wo': _L0_attn_in['Wo'], 'L0_attn_bo': _L0_attn_in['bo'], 'L0_attn_et_gate': _L0_attn_in['et_gate'], 'L0_attn_is_gate': _L0_attn_in['is_gate'], 'L0_attn_time_bias': _L0_attn_in['time_bias'], 'L0_xattn_Wq': _L0_xattn_in['Wq'], 'L0_xattn_bq': _L0_xattn_in['bq'], 'L0_xattn_Wk': _L0_xattn_in['Wk'], 'L0_xattn_bk': _L0_xattn_in['bk'], 'L0_xattn_Wv': _L0_xattn_in['Wv'], 'L0_xattn_bv': _L0_xattn_in['bv'], 'L0_xattn_Wo': _L0_xattn_in['Wo'], 'L0_xattn_bo': _L0_xattn_in['bo'], 'L0_ffn_router_w': _L0_ffn_in['router_w'], 'L0_ffn_w1': _L0_ffn_in['w1'], 'L0_ffn_w2': _L0_ffn_in['w2'], 'L1_attn_Wq': _L1_attn_in['Wq'], 'L1_attn_Wk': _L1_attn_in['Wk'], 'L1_attn_Wv': _L1_attn_in['Wv'], 'L1_attn_Wo': _L1_attn_in['Wo'], 'L1_attn_lambda_q1': _L1_attn_in['lambda_q1'], 'L1_attn_lambda_k1': _L1_attn_in['lambda_k1'], 'L1_attn_lambda_q2': _L1_attn_in['lambda_q2'], 'L1_attn_lambda_k2': _L1_attn_in['lambda_k2'], 'L1_attn_gamma': _L1_attn_in['gamma'], 'L1_attn_beta': _L1_attn_in['beta'], 'L1_xattn_Wq': _L1_xattn_in['Wq'], 'L1_xattn_Wk': _L1_xattn_in['Wk'], 'L1_xattn_Wv': _L1_xattn_in['Wv'], 'L1_xattn_gate': _L1_xattn_in['gate'], 'L1_xattn_ln_g': _L1_xattn_in['ln_g'], 'L1_xattn_ln_b': _L1_xattn_in['ln_b'], 'L1_xattn_Wp': _L1_xattn_in['Wp'], 'L1_xattn_bp': _L1_xattn_in['bp'], 'L1_ffn_sg_w': _L1_ffn_in['sg_w'], 'L1_ffn_su_w': _L1_ffn_in['su_w'], 'L1_ffn_sd_w': _L1_ffn_in['sd_w'], 'L1_ffn_router_w': _L1_ffn_in['router_w'], 'L1_ffn_routing_bias': _L1_ffn_in['routing_bias'], 'L1_ffn_wg': _L1_ffn_in['wg'], 'L1_ffn_wu': _L1_ffn_in['wu'], 'L1_ffn_wd': _L1_ffn_in['wd']}

def reference(x, ctx_1024, fside_BxSxS2_0, mask_BxSxS2_ff0, L0_attn_Wq, L0_attn_bq, L0_attn_Wk, L0_attn_bk, L0_attn_Wv, L0_attn_bv, L0_attn_Wo, L0_attn_bo, L0_attn_et_gate, L0_attn_is_gate, L0_attn_time_bias, L0_xattn_Wq, L0_xattn_bq, L0_xattn_Wk, L0_xattn_bk, L0_xattn_Wv, L0_xattn_bv, L0_xattn_Wo, L0_xattn_bo, L0_ffn_router_w, L0_ffn_w1, L0_ffn_w2, L1_attn_Wq, L1_attn_Wk, L1_attn_Wv, L1_attn_Wo, L1_attn_lambda_q1, L1_attn_lambda_k1, L1_attn_lambda_q2, L1_attn_lambda_k2, L1_attn_gamma, L1_attn_beta, L1_xattn_Wq, L1_xattn_Wk, L1_xattn_Wv, L1_xattn_gate, L1_xattn_ln_g, L1_xattn_ln_b, L1_xattn_Wp, L1_xattn_bp, L1_ffn_sg_w, L1_ffn_su_w, L1_ffn_sd_w, L1_ffn_router_w, L1_ffn_routing_bias, L1_ffn_wg, L1_ffn_wu, L1_ffn_wd):
    import jax
    import jax.numpy as jnp

    def _L0_attn_ref(x, Wq, bq, Wk, bk, Wv, bv, Wo, bo, et_gate, is_gate, time_bias):
        import jax, jax.numpy as jnp
        import numpy as np
        MODEL_DIM = 128
        HEADS = 16
        HEAD_DIM = MODEL_DIM // HEADS
        B, T = (2, 256)
        TB_LEN = 500
        Bb, Tt, D = x.shape
        H, hd = (HEADS, HEAD_DIM)
        Q = (x @ Wq.T + bq).reshape(Bb, Tt, H, hd).transpose(0, 2, 1, 3)
        K = (x @ Wk.T + bk).reshape(Bb, Tt, H, hd).transpose(0, 2, 1, 3)
        V = (x @ Wv.T + bv).reshape(Bb, Tt, H, hd).transpose(0, 2, 1, 3)
        scores = jnp.einsum('bhqd,bhkd->bhqk', Q, K) / jnp.sqrt(jnp.float32(hd))
        pos = jnp.arange(Tt)[None, :] - jnp.arange(Tt)[:, None]
        idx = jnp.clip(pos + TB_LEN // 2, 0, TB_LEN - 1)
        tp = time_bias[:, :, idx]
        tp = jnp.squeeze(tp, axis=1)[None, None]
        scores = scores + jax.nn.sigmoid(et_gate) * tp + is_gate
        attn = jax.nn.softmax(scores, axis=-1)
        context = jnp.matmul(attn, V)
        context = context.transpose(0, 2, 1, 3, 4).reshape(Bb, Tt, D)
        return context @ Wo.T + bo

    def _L0_xattn_ref(q, k, v, attn_bias, attention_mask, Wq, bq, Wk, bk, Wv, bv, Wo, bo):
        import jax, jax.numpy as jnp
        import numpy as np
        HIDDEN = 128
        HEADS = 16
        DK = HIDDEN // HEADS
        B, N = (2, 256)
        b, n, _ = q.shape
        scale = DK ** (-0.5)
        qh = (q @ Wq + bq).reshape(b, n, HEADS, DK).transpose(0, 2, 1, 3)
        kh = (k @ Wk + bk).reshape(b, -1, HEADS, DK).transpose(0, 2, 1, 3)
        vh = (v @ Wv + bv).reshape(b, -1, HEADS, DK).transpose(0, 2, 1, 3)
        scores = jnp.einsum('bhnd,bhmd->bhnm', qh * scale, kh)
        scores = scores + attn_bias[:, None, :, :] + attention_mask[:, None, :, :]
        probs = jax.nn.softmax(scores, axis=-1)
        ctx = jnp.einsum('bhnm,bhmd->bhnd', probs, vh)
        ctx = ctx.transpose(0, 2, 1, 3).reshape(b, n, HEADS * DK)
        return ctx @ Wo + bo

    def _L0_ffn_ref(x, router_w, w1, w2):
        import jax, jax.numpy as jnp
        import numpy as np
        B, S, H, E, K = (4, 256, 128, 8, 2)
        bsz, seq, hidden = x.shape
        n_experts = w1.shape[0]
        tokens = x.reshape(-1, hidden)
        T = tokens.shape[0]
        logits = tokens @ router_w.T
        topv, topi = jax.lax.top_k(logits, K)
        w = jax.nn.softmax(topv, axis=-1).astype(tokens.dtype)
        gate = jnp.zeros((T, n_experts), tokens.dtype).at[jnp.arange(T)[:, None], topi].add(w)
        out = jnp.zeros_like(tokens)
        for e in range(n_experts):
            h = jax.nn.gelu(tokens @ w1[e].T, approximate=False)
            y = h @ w2[e].T
            out = out + gate[:, e:e + 1] * y
        return out.reshape(bsz, seq, hidden)

    def _L1_attn_ref(x, Wq, Wk, Wv, Wo, lambda_q1, lambda_k1, lambda_q2, lambda_k2, gamma, beta):
        import jax, jax.numpy as jnp
        import numpy as np
        import math
        DIM = 128
        NUM_HEADS = 16
        HEAD_DIM = DIM // NUM_HEADS
        LAYER_IDX = 12
        LAMBDA_INIT = 0.8 - 0.6 * math.exp(-0.3 * (LAYER_IDX - 1))
        LN_EPS = 1e-05
        B, S, _ = x.shape
        scaling = HEAD_DIM ** (-0.5)
        Q = (x @ Wq).reshape(B, S, NUM_HEADS, 2 * HEAD_DIM).transpose(0, 2, 1, 3)
        K = (x @ Wk).reshape(B, S, NUM_HEADS, 2 * HEAD_DIM).transpose(0, 2, 1, 3)
        V = (x @ Wv).reshape(B, S, NUM_HEADS, HEAD_DIM).transpose(0, 2, 1, 3)
        lamb = jnp.exp(jnp.sum(lambda_q1 * lambda_k1)) - jnp.exp(jnp.sum(lambda_q2 * lambda_k2)) + LAMBDA_INIT
        Q1, Q2 = jnp.split(Q, 2, axis=-1)
        K1, K2 = jnp.split(K, 2, axis=-1)
        A1 = jnp.einsum('bhqd,bhkd->bhqk', Q1, K1) * scaling
        A2 = jnp.einsum('bhqd,bhkd->bhqk', Q2, K2) * scaling
        attn = jax.nn.softmax(A1, axis=-1) - lamb * jax.nn.softmax(A2, axis=-1)
        out = jnp.einsum('bhqk,bhkd->bhqd', attn, V)
        out = out.transpose(0, 2, 1, 3).reshape(B, S, DIM)
        out = out @ Wo
        mu = jnp.mean(out, axis=-1, keepdims=True)
        var = jnp.var(out, axis=-1, keepdims=True)
        out = (out - mu) * jax.lax.rsqrt(var + LN_EPS) * gamma + beta
        return out

    def _L1_xattn_ref(x, x_text, Wq, Wk, Wv, gate, ln_g, ln_b, Wp, bp):
        import jax, jax.numpy as jnp
        import numpy as np
        B, N, P, DIM, H = (8, 128, 77, 128, 16)
        HD = DIM // H
        LN_EPS = 1e-05
        b, n, c = x.shape
        h = gate.shape[1]
        q = x @ Wq.T
        k = jnp.concatenate([x_text @ Wk.T, x @ Wk.T], axis=1)
        v = jnp.concatenate([x_text @ Wv.T, x @ Wv.T], axis=1)
        kv = k.shape[1]
        q = q.reshape(b, n, h, -1).transpose(0, 2, 1, 3)
        k = k.reshape(b, kv, h, -1).transpose(0, 2, 1, 3)
        v = v.reshape(b, kv, h, -1).transpose(0, 2, 1, 3)
        d = q.shape[-1]
        scores = jnp.einsum('bhnd,bhkd->bhnk', q, k) / jnp.sqrt(jnp.float32(d))
        first = jnp.tanh(gate) * jnp.ones_like(scores[..., :1])
        rest = jax.nn.softmax(scores[..., 1:], axis=-1)
        attn = jnp.concatenate([first, rest], axis=-1)
        out = jnp.einsum('bhnk,bhkd->bhnd', attn, v)
        out = out.transpose(0, 2, 1, 3).reshape(b, n, -1)
        out = out.astype(jnp.bfloat16).astype(jnp.float32)
        mu = jnp.mean(out, axis=-1, keepdims=True)
        var = jnp.var(out, axis=-1, keepdims=True)
        out = (out - mu) / jnp.sqrt(var + LN_EPS) * ln_g + ln_b
        return out @ Wp.T + bp

    def _L1_ffn_ref(x, sg_w, su_w, sd_w, router_w, routing_bias, wg, wu, wd):
        import jax, jax.numpy as jnp
        import numpy as np
        H = 128
        I = 256
        E = 8
        TOP_K = 2
        NUM_SHARED = 1
        orig_shape = x.shape
        xt = x.reshape(-1, H)
        T = xt.shape[0]
        shared = jax.nn.silu(xt @ sg_w.T) * (xt @ su_w.T) @ sd_w.T
        shared = shared / NUM_SHARED
        logits = xt @ router_w.T + routing_bias
        probs = jax.nn.sigmoid(logits)
        topk_p, topk_idx = jax.lax.top_k(probs, TOP_K)
        topk_p = topk_p / jnp.sum(topk_p, axis=-1, keepdims=True)
        w = jnp.zeros((T, E), dtype=xt.dtype)
        w = w.at[jnp.arange(T)[:, None], topk_idx].add(topk_p)
        g = jnp.einsum('th,eih->tei', xt, wg)
        u = jnp.einsum('th,eih->tei', xt, wu)
        h = jax.nn.silu(g) * u
        y = jnp.einsum('tei,ehi->teh', h, wd)
        routed = jnp.einsum('te,teh->th', w, y)
        return (shared + routed).reshape(orig_shape)
    x = _layernorm(x + _L0_attn_ref(x, L0_attn_Wq, L0_attn_bq, L0_attn_Wk, L0_attn_bk, L0_attn_Wv, L0_attn_bv, L0_attn_Wo, L0_attn_bo, L0_attn_et_gate, L0_attn_is_gate, L0_attn_time_bias), axis=-1)
    x = _layernorm(x + _L0_xattn_ref(x, ctx_1024, ctx_1024, fside_BxSxS2_0, mask_BxSxS2_ff0, L0_xattn_Wq, L0_xattn_bq, L0_xattn_Wk, L0_xattn_bk, L0_xattn_Wv, L0_xattn_bv, L0_xattn_Wo, L0_xattn_bo), axis=-1)
    x = _layernorm(x + _L0_ffn_ref(x, L0_ffn_router_w, L0_ffn_w1, L0_ffn_w2), axis=-1)
    x = _layernorm(x + _L1_attn_ref(x, L1_attn_Wq, L1_attn_Wk, L1_attn_Wv, L1_attn_Wo, L1_attn_lambda_q1, L1_attn_lambda_k1, L1_attn_lambda_q2, L1_attn_lambda_k2, L1_attn_gamma, L1_attn_beta), axis=-1)
    x = _layernorm(x + _L1_xattn_ref(x, ctx_1024, L1_xattn_Wq, L1_xattn_Wk, L1_xattn_Wv, L1_xattn_gate, L1_xattn_ln_g, L1_xattn_ln_b, L1_xattn_Wp, L1_xattn_bp), axis=-1)
    x = _layernorm(x + _L1_ffn_ref(x, L1_ffn_sg_w, L1_ffn_su_w, L1_ffn_sd_w, L1_ffn_router_w, L1_ffn_routing_bias, L1_ffn_wg, L1_ffn_wu, L1_ffn_wd), axis=-1)
    return x

_drawn_inputs = setup_inputs


def setup_inputs(seed=0):
    import zlib

    import numpy as np

    out = dict(_drawn_inputs(seed))
    spreads = {'L0_attn_bq': (0.0, 0.8),
     'L0_attn_bk': (0.0, 0.8),
     'L0_attn_bv': (0.0, 0.1),
     'L0_attn_bo': (0.0, 0.1),
     'L0_xattn_bq': (0.0, 0.369),
     'L0_xattn_bk': (0.0, 0.8),
     'L0_xattn_bv': (0.0, 0.1),
     'L0_xattn_bo': (0.0, 0.1),
     'L1_attn_gamma': (1.0, 0.2),
     'L1_attn_beta': (0.0, 0.1),
     'L1_xattn_ln_g': (1.0, 0.2),
     'L1_xattn_ln_b': (0.0, 0.34),
     'L1_xattn_bp': (0.0, 0.1),
     'L1_ffn_routing_bias': (0.0, 0.8)}
    factors = {'L0_attn_Wq': 3.996,
     'L0_attn_Wk': 4.084,
     'L0_attn_Wv': 3.53,
     'L0_attn_time_bias': 4.278,
     'L0_xattn_Wq': 8.0,
     'L0_xattn_Wk': 8.0,
     'L1_attn_lambda_q1': 3.531,
     'L1_xattn_Wq': 8.0,
     'L1_xattn_Wk': 8.0,
     'L1_ffn_sg_w': 6.66,
     'L1_ffn_su_w': 6.403,
     'L1_ffn_sd_w': 6.327,
     'L1_ffn_router_w': 8.0,
     'L1_ffn_wg': 8.0,
     'L1_ffn_wu': 8.0,
     'L1_ffn_wd': 8.0}
    for name, (base, spread) in spreads.items():
        noise = np.random.default_rng([zlib.crc32(name.encode()), seed]).standard_normal(out[name].shape)
        drawn = base * np.exp(spread * noise) if base else spread * noise
        out[name] = jnp.asarray(drawn.astype(out[name].dtype))
    for name, factor in factors.items():
        out[name] = (out[name] * factor).astype(out[name].dtype)
    return out
```

```python
from contextlib import ExitStack

import concourse.bass as bass
from concourse import mybir

F32 = mybir.dt.float32
BF16 = mybir.dt.bfloat16
U32 = mybir.dt.uint32
ACT = mybir.ActivationFunctionType
ALU = mybir.AluOpType
AX = mybir.AxisListType

P = 128
B, T, D = 4, 256, 128
TC = 64
H, HD = 16, 8
QT = T // P
E, HID = 8, 256
HH = HID // P
STRIP = 32
G4 = P // STRIP
NPROD = 6
KPART = (0, 0, 1, 0, 2, 1)
QPART = (0, 1, 0, 2, 0, 1)
SROWS = NPROD * HD
MROWS = 3
SCALE = float(HD) ** -0.5
LAMBDA_INIT = 0.8 - 0.6 * 2.718281828459045 ** (-0.3 * 11)
EPS = 1e-5
TB = 500
TOP = -1.0

KINDS = ("a0", "x0", "f0", "d1", "x1", "f1")
UNITS = [(kind, b) for kind in KINDS for b in range(B)]
HEADS = {"a0": H, "x0": H, "d1": 2 * H, "x1": H}
KEYS = {"a0": T, "x0": TC, "d1": T, "x1": TC + T}
ATT = [u for u, (k, _) in enumerate(UNITS) if k[0] != "f"]
ORDER_A = {u: n for n, u in enumerate(ATT)}


def a_items(kind):
    if kind == "x0":
        return [(g, 0) for g in range(H // G4)]
    if kind == "x1":
        return [(s, qt) for s in range(H) for qt in range(QT)]
    return [(s, 0) for s in range(HEADS[kind])]


def b_items(kind, g):
    s0 = G4 * g
    if kind == "x0":
        return [("c", s0), ("c", s0 + 2)]
    if kind == "x1":
        return [("c", s0), ("c", s0 + 2)] + [("s", s0 + j) for j in range(G4)]
    return [("s", s0 + j) for j in range(G4)]


def groups(kind):
    return HEADS[kind] // G4


def order():
    def chain(us):
        yield "prep", us[0], 0
        yield "amax", us[0], (0, 1)
        yield "mneg", us[0], 0
        yield "vprep", us[0], 0
        yield "prep", us[1], 0
        yield "vprep", us[1], 0
        for n, u in enumerate(us):
            G = groups(UNITS[u][0])
            if n:
                yield "post", us[n - 1], 0
                if UNITS[u][0] != "a0":
                    yield "finish", us[n - 1], 0
            for g in range(G):
                yield "bexp", u, g
                if n + 1 < len(us) and g:
                    yield "amax", us[n + 1], (g - 1, G - 1)
                if g:
                    yield "pv", u, g - 1
                if g == 1 and n + 2 < len(us):
                    yield "prep", us[n + 2], 0
            if n + 1 < len(us):
                yield "mneg", us[n + 1], 0
            yield "pv", u, G - 1
            if n + 2 < len(us):
                yield "vprep", us[n + 2], 0
        yield "post", us[-1], 0
        for u in us if UNITS[us[0]][0] == "a0" else us[-1:]:
            yield "finish", u, 0

    for kinds in (("a0",), ("x0",), ("f0",), ("d1", "x1"), ("f1",)):
        us = [u for u, (k, _) in enumerate(UNITS) if k in kinds]
        if kinds[0][0] == "f":
            for u in us:
                yield "ffn", u, 0
        else:
            yield from chain(us)


def part_of(u, part):
    n, m = part
    items = len(a_items(UNITS[u][0]))
    return items * n // m, items * (n + 1) // m


class Banks:

    def __init__(self, ctx, nc):
        self.full = [ctx.enter_context(nc.semaphore(f"bank{i}_full")) for i in range(8)]
        self.free = [ctx.enter_context(nc.semaphore(f"bank{i}_free")) for i in range(8)]
        self.uses = [0] * 8
        self.place = {}
        self.turn = {}

    def take(self, pe, key, pool):
        t = self.turn.get(pool, 0)
        self.turn[pool] = t + 1
        i = pool[t % len(pool)]
        n = self.uses[i]
        self.uses[i] = n + 1
        self.place[key] = (i, n)
        if n:
            pe.wait_ge(self.free[i], n)
        return i

    def await_full(self, eng, key):
        i, n = self.place[key]
        eng.wait_ge(self.full[i], n + 1)
        return i

    def await_read(self, eng, key):
        i, n = self.place[key]
        eng.wait_ge(self.free[i], n + 1)


POOL_A, POOL_B, POOL_O, POOL_M = (0, 1), (2, 3), (4, 5), (6, 7)


def decoder(nc, I, out):
    with ExitStack() as ctx:
        def sb(name, shape, dt=F32):
            return ctx.enter_context(nc.sbuf_tensor(name, shape, dt))

        def sem(name):
            return ctx.enter_context(nc.semaphore(name))

        banks = Banks(ctx, nc)
        PS = ctx.enter_context(nc.psum_tensor("PS", [P, 8, 512], F32))
        scr = nc.dram_tensor("parts_scratch", (4, 3, 2 * P, TC + T), BF16).ap()
        mix = nc.dram_tensor("mix_scratch", (H, B, T, HD), F32)
        ext_d = nc.dram_tensor("bias_scratch", (1, 512), F32)

        X = sb("X", [P, B, QT, D])
        C = sb("C", [TC, B, D])
        ctxT = sb("ctxT", [P, B, TC])
        ident = sb("ident", [P, P])
        identb = sb("identb", [P, P], BF16)
        flip = sb("flip", [P, P])
        W = {}
        for n, w in (("a0_q", D), ("a0_k", D), ("a0_v", D), ("a0_o", D), ("x0_q", D), ("x0_k", D), ("x0_v", D),
                     ("x0_o", D), ("d1_q", 2 * D), ("d1_k", 2 * D), ("d1_v", D), ("d1_o", D), ("x1_q", D),
                     ("x1_k", D), ("x1_v", D), ("x1_o", D), ("f0_r", E), ("f1_r", E)):
            W[n] = sb("w_" + n, [P, w])
        FW = sb("FW", [P, 2 * (E + 1) * HID])
        w1 = FW[:, 0:E * HID].rearrange("p (e i) -> p e i", i=HID)
        w2 = FW[:, E * HID:2 * E * HID].rearrange("p (e t d) -> p e t d", t=HH, d=D)
        wg = FW[:, 0:(E + 1) * HID].rearrange("p (e i) -> p e i", i=HID)
        wu = FW[:, (E + 1) * HID:2 * (E + 1) * HID].rearrange("p (e i) -> p e i", i=HID)
        wd = sb("wd", [P, E + 1, HH, D])
        cols = {n: sb("c_" + n, [P, 1]) for n in ("a0_q", "a0_k", "x0_q", "x0_k")}
        rows = {n: sb("r_" + n, [P, D]) for n in ("a0_v", "a0_o", "x0_v", "x0_o", "d1_g", "d1_b", "x1_g",
                                                   "x1_b", "x1_o")}
        rbias = sb("rbias", [P, E])
        gate_t = sb("gate_t", [P, H])
        gates = sb("gates", [P, 2])
        lam4 = sb("lam4", [P, 4, HD])
        lam = sb("lam", [P, 8])
        neghalf = sb("neghalf", [P, 2])
        iota8 = sb("iota8", [P, E])
        ones3 = sb("ones3", [MROWS, 512], BF16)

        PR = sb("PR", [P, 12, 512])
        win = PR[:, 0, :].rearrange("p (q t) -> p q t", t=T)
        bias_n = PR[:, 1, :]
        bias_t = PR[:, 2, :]
        fs = PR[:, 3, :].rearrange("p (b q t) -> p b q t", b=B, t=TC)
        fm = PR[:, 4, :].rearrange("p (b q t) -> p b q t", b=B, t=TC)
        fst = PR[0:TC, 5:7, :].rearrange("p x (b t) -> p (x b) t", t=T)
        hs = PR[:, 0:2, :]
        sg = PR[:, 2:4, :]
        bias_np = sb("bias_np", [P, 3, QT * T], BF16)
        bias_tp = sb("bias_tp", [P, 3, QT * T], BF16)
        fsp = sb("fsp", [P, B, 3, QT * TC], BF16)
        fstp = sb("fstp", [TC, B, 3, T], BF16)

        xT = sb("xT", [P, 2, T])
        ctx0 = sb("ctx0", [P, B, P])
        qf = sb("qf", [P, 2, 2 * T])
        kf = sb("kf", [P, 2, 2 * T])
        rf = sb("rf", [P, 2 * T])
        qp = sb("qp", [P, 3, 2 * T], BF16)
        kp = sb("kp", [P, 3, 2 * T], BF16)
        QS = sb("QS", [P, 2, 2 * H, T], BF16)
        KS = sb("KS", [P, 2, 2 * H * T], BF16)
        VX = sb("VX", [P, 2, 3, H, STRIP])
        v0 = sb("v0", [P, B, D])
        mx = sb("mx", [P, 2, 2 * H])
        mf = sb("mf", [2 * H, T])
        mr = sb("mr", [2 * H, T])
        mp = sb("mp", [2 * H, 3, T], BF16)
        OR = sb("OR", [P, 8, T])
        on = sb("on", [P, QT, D])
        cm = sb("cm", [P, QT, D])
        onb = sb("onb", [P, QT, D], BF16)
        tmp = sb("tmp", [P, H, HD])
        rs = sb("rs", [P, H])
        OT = sb("OT", [P, QT, P])
        y = sb("y", [P, QT, D])
        st = sb("st", [P, 6])
        mv = sb("mv", [P, QT, 2])
        ve = sb("ve", [P, QT])
        rstd = sb("rstd", [P, QT])
        acc = sb("acc", [P, QT, D])
        lg = sb("lg", [P, QT, E])
        le = sb("le", [P, QT, E])
        top = sb("top", [P, QT, 8])
        topi = sb("topi", [P, QT, 8], U32)
        topf = sb("topf", [P, QT, 8])
        gt = sb("gt", [P, QT, 8])
        gate = sb("gate", [P, QT, E])

        loaded = sem("loaded")
        late_in = sem("late_in")
        ext_done = sem("ext_done")
        win_in = sem("win_in")
        consts = sem("consts")
        zeroed = sem("zeroed")
        ones_in = sem("ones_in")
        bias_sum = sem("bias_sum")
        setup_v = sem("setup_v")
        lam_sums = sem("lam_sums")
        act_set = sem("act_set")
        v_chain = sem("v_chain")
        p_chain = sem("p_chain")
        x_new = sem("x_new")
        q_ready = sem("q_ready")
        k_ready = sem("k_ready")
        qp_ready = sem("qp_ready")
        kp_ready = sem("kp_ready")
        qp_out = sem("qp_out")
        kp_out = sem("kp_out")
        qs_in = sem("qs_in")
        ks_in = sem("ks_in")
        mp_ready = sem("mp_ready")
        m_in = sem("m_in")
        on_ready = sem("on_ready")
        mix_out = sem("mix_out")
        mix_in = sem("mix_in")
        var_ready = sem("var_ready")
        rstd_ready = sem("rstd_ready")
        rt_in = sem("rt_in")
        rt_exp = sem("rt_exp")
        stored = sem("stored")

        ks_view = [KS[:, par, :] for par in range(2)]

        def kstack(u):
            kind, _ = UNITS[u]
            n = KEYS[kind]
            return ks_view[ORDER_A[u] % 2][:, 0:HEADS[kind] * n].rearrange("p (s t) -> p s t", t=n)

        AU = ORDER_A
        groups_before = {}
        pbanks_before = {}
        gsum = psum_ = 0
        for u in ATT:
            groups_before[u], pbanks_before[u] = gsum, psum_
            for g in range(groups(UNITS[u][0])):
                gsum += 1
                psum_ += len(b_items(UNITS[u][0], g))

        def p_slot(u, g, i):
            return ((groups_before[u] + g) % 2) * 6 + i

        def p_count(u, g):
            return pbanks_before[u] + sum(len(b_items(UNITS[u][0], x)) for x in range(g + 1))

        f_units = [u for u, (k, _) in enumerate(UNITS) if k[0] == "f"]
        experts = {"f0": E, "f1": E + 1}
        e_before, n = {}, 0
        for u in f_units:
            e_before[u] = n
            n += experts[UNITS[u][0]]
        flat_e = [(u, e) for u in f_units for e in range(experts[UNITS[u][0]])]
        widths = {"a0": T, "x0": T, "d1": 2 * T, "x1": T}
        kwidths = {"a0": T, "x0": TC, "d1": 2 * T, "x1": TC + T}
        kdmas, n = {}, 0
        for u in ATT:
            n += 1
            kdmas[u] = 16 * NPROD * n

        def ks_count(u):
            return kdmas[u]

        def last_b(u):
            g = groups(UNITS[u][0]) - 1
            return ("b", u, g, len(b_items(UNITS[u][0], g)) - 1)

        def prev(u, k=1):
            return ATT[AU[u] - k] if AU[u] >= k else None

        def sent_dmas(u):
            return sum(3 * (HEADS[UNITS[v][0]] // H) for v in ATT if v <= u)

        def last_t(u):
            return ("t", u, QT - 1, groups(UNITS[u][0]) // 4 - 1)

        block = ctx.enter_context(nc.Block())
        loads = [
            (X[:, :, :, :], I["x"].rearrange("b (t p) d -> p b t d", p=P)),
            (C[:, :, :], I["ctx_1024"].rearrange("b t d -> t b d")),
            (fs[:, :, :, :], I["fside_BxSxS2_0"].rearrange("b (t p) k -> p b t k", p=P)),
            (fm[:, :, :, :], I["mask_BxSxS2_ff0"].rearrange("b (t p) k -> p b t k", p=P)),
        ]
        loads += [(W[n][:, :], I["w_" + n]) for n in W]
        loads += [(cols[n][:, :], I["c_" + n]) for n in cols]
        loads += [(rows[n][:, :], I["r_" + n].partition_broadcast(P)) for n in rows]
        loads += [(rbias[:, :], I["rbias"].partition_broadcast(P)), (gate_t[:, :], I["gate"].partition_broadcast(P)),
                  (gates[:, 0:1], I["et_gate"].partition_broadcast(P)),
                  (gates[:, 1:2], I["is_gate"].partition_broadcast(P))]
        loads += [(lam4[:, i, :], I[n].partition_broadcast(P)) for i, n in enumerate(("lq1", "lk1", "lq2", "lk2"))]
        loads += [(w1[:, :, :], I["w1"].rearrange("e h i -> h e i")),
                  (w2[:, :, :, :], I["w2"].rearrange("e (t p) d -> p e t d", p=P)),
                  (wd[:, 0:E, :, :], I["wd"].rearrange("e (t p) d -> p e t d", p=P)),
                  (wd[:, E, :, :], I["sd"].rearrange("(t p) d -> p t d", p=P))]
        NLOAD = len(loads)
        late = [(wg[:, 0:E, :], I["wg"].rearrange("e h i -> h e i")), (wg[:, E, :], I["sg"]),
                (wu[:, 0:E, :], I["wu"].rearrange("e h i -> h e i")), (wu[:, E, :], I["su"])]

        @block.tensor
        def _(pe):
            def mm(o, l, r, start, stop):
                return pe.matmul(o, l, r, start=start, stop=stop, skip_group_check=True)

            pe.wait_ge(loaded, 16 * NLOAD)
            pe.wait_ge(consts, 1)
            i = banks.take(pe, "ctxT", POOL_M)
            for b in range(B):
                last = pe.transpose(PS[:, i, b * TC:(b + 1) * TC], C[:, b, :], ident[0:TC, 0:TC])
            last.then_inc(banks.full[i], 1)
            pe.wait_ge(win_in, 16 * QT)
            i = banks.take(pe, "bn", POOL_M)
            for qt in range(QT):
                last = mm(PS[:, i, qt * T:(qt + 1) * T], flip[:, :], win[:, qt, :], True, True)
            last.then_inc(banks.full[i], 1)
            i = banks.take(pe, "bt", POOL_M)
            for kt in range(QT):
                for qt in range(QT):
                    last = mm(PS[:, i, kt * T + qt * P:kt * T + (qt + 1) * P], win[:, qt, kt * P:(kt + 1) * P],
                              flip[:, :], True, True)
            last.then_inc(banks.full[i], 1)
            pe.wait_ge(bias_sum, 1)
            for h in range(2):
                i = banks.take(pe, ("ft", h), POOL_M)
                for b2 in range(2):
                    for qt in range(QT):
                        last = pe.transpose(PS[0:TC, i, b2 * T + qt * P:b2 * T + (qt + 1) * P],
                                            fs[:, 2 * h + b2, qt, :], ident[:, :])
                last.then_inc(banks.full[i], 1)
            pe.wait_ge(setup_v, 1)
            pe.wait_ge(ones_in, 32)

            def tokens(u):
                kind, b = UNITS[u]
                if kind != "a0":
                    pe.wait_ge(x_new, u - B + 1)
                i = banks.take(pe, ("xt", u), POOL_M)
                for qt in range(QT):
                    last = pe.transpose(PS[:, i, qt * P:(qt + 1) * P], X[:, b, qt, :], ident[:, :])
                last.then_inc(banks.full[i], 1)
                banks.await_read(pe, ("xt", u))
                return xT[:, u % 2, :]

            def prep(u):
                kind, b = UNITS[u]
                x = tokens(u)
                nq = HEADS[kind] // H
                i = banks.take(pe, ("q", u), POOL_M)
                for c in range(nq):
                    last = mm(PS[:, i, c * T:(c + 1) * T], W[kind + "_q"][:, c * D:(c + 1) * D], x, True, True)
                last.then_inc(banks.full[i], 1)
                i = banks.take(pe, ("k", u), POOL_M)
                at = 0
                if kind in ("x0", "x1"):
                    last = mm(PS[:, i, 0:TC], W[kind + "_k"][:, :], ctxT[:, b, :], True, True)
                    at = TC
                if kind != "x0":
                    for c in range(nq):
                        last = mm(PS[:, i, at + c * T:at + (c + 1) * T], W[kind + "_k"][:, c * D:(c + 1) * D], x,
                                  True, True)
                last.then_inc(banks.full[i], 1)

            def vprep(u):
                kind, b = UNITS[u]
                x = xT[:, u % 2, :]
                i = banks.take(pe, ("v", u), POOL_M)
                w = W[kind + "_v"][:, :]
                if kind != "x0":
                    for qt in range(QT):
                        last = mm(PS[:, i, qt * D:(qt + 1) * D], x[:, qt * P:(qt + 1) * P], w, True, True)
                if kind == "x0":
                    last = mm(PS[0:TC, i, 0:D], ctxT[:, b, :], w, True, True)
                if kind == "x1":
                    mm(PS[0:TC - 1, i, 2 * D:3 * D], ctxT[:, b, 1:TC], w, True, True)
                    last = mm(PS[:, i, 3 * D:4 * D], ctx0[:, b, :], w, True, True)
                last.then_inc(banks.full[i], 1)

            def amax(u, lo, hi):
                kind, b = UNITS[u]
                items = a_items(kind)
                if lo == 0:
                    pe.wait_ge(qs_in, 16 * NPROD * (AU[u] + 1))
                    pe.wait_ge(ks_in, ks_count(u))
                q, k = QS[0:SROWS, AU[u] % 2], kstack(u)[0:SROWS]
                for it in range(lo, hi):
                    s, qt1 = items[it]
                    i = banks.take(pe, ("a", u, it), POOL_A)
                    if kind == "x1":
                        last = mm(PS[:, i, 0:TC + T - 1], q[:, s, qt1 * P:(qt1 + 1) * P], k[:, s, 1:TC + T], True, True)
                    elif kind == "x0":
                        for p in range(3):
                            r = fsp[:, b, p, :].unsqueeze(1).to_broadcast([P, G4, QT * TC])
                            mm(PS[:, i, :], identb[:, :], r, p == 0, False)
                        for j in range(G4):
                            for qt in range(QT):
                                o = (j * QT + qt) * TC
                                last = mm(PS[:, i, o:o + TC], q[:, G4 * s + j, qt * P:(qt + 1) * P],
                                          k[:, G4 * s + j, :], False, j == G4 - 1 and qt == QT - 1)
                    else:
                        if kind == "a0":
                            for p in range(3):
                                mm(PS[:, i, :], identb[:, :], bias_np[:, p, :], p == 0, False)
                        for qt in range(QT):
                            last = mm(PS[:, i, qt * T:(qt + 1) * T], q[:, s, qt * P:(qt + 1) * P], k[:, s, :],
                                      kind == "d1", True)
                    last.then_inc(banks.full[i], 1)

            def mneg(u):
                n = HEADS[UNITS[u][0]]
                banks.await_read(pe, ("a", u, len(a_items(UNITS[u][0])) - 1))
                i = banks.take(pe, ("m", u), POOL_M)
                for qt in range(QT):
                    last = pe.transpose(PS[0:n, i, qt * P:(qt + 1) * P], mx[:, qt, 0:n], ident[:, :])
                last.then_inc(banks.full[i], 1)

            def bexp(u, g):
                kind, b = UNITS[u]
                if g == 0:
                    pe.wait_ge(m_in, 16 * MROWS * (AU[u] + 1))
                q, k = QS[:, AU[u] % 2], kstack(u)
                off = TC if kind == "x1" else 0
                c0 = 1 if kind == "x1" else 0
                for n, (what, s) in enumerate(b_items(kind, g)):
                    i = banks.take(pe, ("b", u, g, n), POOL_B)
                    if what == "c":
                        if kind == "x0":
                            for p in range(3):
                                r = fstp[:, b, p, :].unsqueeze(1).to_broadcast([TC, 2, T])
                                mm(PS[0:TC, i, :], identb[0:TC, 0:TC], r, p == 0, False)
                        for j in range(2):
                            last = mm(PS[0:TC - c0, i, j * T:(j + 1) * T], k[:, s + j, c0:TC], q[:, s + j, :],
                                      kind == "x1", True)
                    else:
                        if kind == "a0":
                            for p in range(3):
                                mm(PS[:, i, :], identb[:, :], bias_tp[:, p, :], p == 0, False)
                        for kt in range(QT):
                            last = mm(PS[:, i, kt * T:(kt + 1) * T], k[:, s, off + kt * P:off + (kt + 1) * P],
                                      q[:, s, :], kind != "a0", True)
                    last.then_inc(banks.full[i], 1)

            def pv(u, g):
                kind, b = UNITS[u]
                for n in range(len(b_items(kind, g))):
                    banks.await_read(pe, ("b", u, g, n))
                if g == 0:
                    banks.await_read(pe, ("v", u))
                i = banks.take(pe, ("o", u, g), POOL_O)
                V = VX[:, AU[u] % 2]
                terms = []
                nc0 = 2 if kind in ("x0", "x1") else 0
                if nc0:
                    rowsc = TC - (kind == "x1")
                    terms.append([(V[0:rowsc, 2], PR[0:rowsc, p_slot(u, g, j // 2), (j % 2) * T:(j % 2 + 1) * T])
                                  for j in range(G4)])
                if kind != "x0":
                    for kt in range(QT):
                        terms.append([(V[:, kt], PR[:, p_slot(u, g, nc0 + j), kt * T:(kt + 1) * T])
                                      for j in range(G4)])
                for n, term in enumerate(terms):
                    for j, (v, p) in enumerate(term):
                        s = G4 * g + j
                        h = s // 2 if kind == "d1" else s
                        last = mm(PS[STRIP * j:STRIP * (j + 1), i, 0:T], v[:, h, :], p, n == 0, n == len(terms) - 1)
                last.then_inc(banks.full[i], 1)

            def post(u):
                kind, b = UNITS[u]
                gs = groups(kind)
                for g in range(gs):
                    banks.await_read(pe, ("o", u, g))
                for qt in range(QT):
                    for half in range(gs // 4):
                        i = banks.take(pe, ("t", u, qt, half), POOL_M)
                        for g in range(4):
                            last = pe.transpose(PS[:, i, g * P:(g + 1) * P], OR[:, 4 * half + g, qt * P:(qt + 1) * P],
                                                ident[:, :])
                        last.then_inc(banks.full[i], 1)

            def finish(u):
                kind, b = UNITS[u]
                if kind == "a0":
                    pe.wait_ge(mix_in, 16 * (u + 1))
                else:
                    pe.wait_ge(on_ready, AU[u] + 1)
                src = cm if kind == "a0" else on
                i = banks.take(pe, ("ont", u), POOL_M)
                for qt in range(QT):
                    last = pe.transpose(PS[:, i, qt * P:(qt + 1) * P], src[:, qt, :], ident[:, :])
                last.then_inc(banks.full[i], 1)
                banks.await_read(pe, ("ont", u))
                i = banks.take(pe, ("wo", u), POOL_M)
                for qt in range(QT):
                    last = mm(PS[:, i, qt * D:(qt + 1) * D], OT[:, qt, :], W[kind + "_o"][:, :], True, True)
                last.then_inc(banks.full[i], 1)

            def ffn(u):
                kind, b = UNITS[u]
                x = tokens(u)
                if kind == "f1":
                    pe.wait_ge(late_in, 16 * len(late))
                i = banks.take(pe, ("r", u), POOL_M)
                for qt in range(QT):
                    last = mm(PS[:, i, qt * E:(qt + 1) * E], x[:, qt * P:(qt + 1) * P], W[kind + "_r"][:, :], True, True)
                last.then_inc(banks.full[i], 1)
                up = [("h", w1)] if kind == "f0" else [("g", wg), ("u", wu)]
                n = experts[kind]
                down = w2 if kind == "f0" else wd

                def second(e):
                    ne = e_before[u] + e
                    banks.await_read(pe, (up[-1][0], u, e))
                    i = banks.take(pe, ("y", u, e), POOL_O)
                    for qt in range(QT):
                        for t in range(HH):
                            last = mm(PS[:, i, qt * D:(qt + 1) * D],
                                      hs[:, ne % 2, t * T + qt * P:t * T + (qt + 1) * P], down[:, e, t, :],
                                      t == 0, t == HH - 1)
                    last.then_inc(banks.full[i], 1)
                for e in range(n):
                    for j, (name, w) in enumerate(up):
                        i = banks.take(pe, (name, u, e), (POOL_A, POOL_B)[j])
                        for t in range(HH):
                            last = mm(PS[:, i, t * T:(t + 1) * T], w[:, e, t * P:(t + 1) * P], x, True, True)
                        last.then_inc(banks.full[i], 1)
                    if e:
                        second(e - 1)
                second(n - 1)

            for step, u, a in order():
                if step == "prep":
                    prep(u)
                elif step == "vprep":
                    vprep(u)
                elif step == "amax":
                    lo, hi = part_of(u, a)
                    amax(u, lo, hi)
                elif step == "mneg":
                    mneg(u)
                elif step == "bexp":
                    bexp(u, a)
                elif step == "pv":
                    pv(u, a)
                elif step == "post":
                    post(u)
                elif step == "finish":
                    finish(u)
                else:
                    ffn(u)

        @block.scalar
        def _(act):
            act.wait_ge(loaded, 16 * NLOAD)
            act.activation(lam[:, 4:5], gates[:, 0:1], ACT.Exp, scale=-1.0).then_inc(act_set, 1)
            act.activation(gate_t[:, :], gate_t[:, :], ACT.Tanh).then_inc(act_set, 1)
            act.wait_ge(lam_sums, 1)
            act.activation(lam[:, 2:4], lam[:, 0:2], ACT.Exp).then_inc(act_set, 1)

            def bexp(u, g):
                kind, b = UNITS[u]
                if groups_before[u] + g >= 2:
                    u2, g2 = (u, g - 2) if g >= 2 else (prev(u), groups(UNITS[prev(u)][0]) + g - 2)
                    banks.await_full(act, ("o", u2, g2))
                for n, (what, s) in enumerate(b_items(kind, g)):
                    i = banks.await_full(act, ("b", u, g, n))
                    pr = P if what == "s" else TC - (kind == "x1")
                    act.activation(PR[0:pr, p_slot(u, g, n), :], PS[0:pr, i, :], ACT.Exp).then_inc(banks.free[i], 1)

            def pv(u, g):
                if g == 0 and prev(u) is not None:
                    banks.await_full(act, last_t(prev(u)))
                i = banks.await_full(act, ("o", u, g))
                act.copy(OR[:, g, :], PS[:, i, 0:T]).then_inc(banks.free[i], 1)

            def finish(u):
                i = banks.await_full(act, ("ont", u))
                act.copy(OT[:, :, :], PS[:, i, 0:QT * P].rearrange("p (q t) -> p q t", t=P)).then_inc(banks.free[i], 1)

            def ffn(u):
                kind, b = UNITS[u]
                act.wait_ge(rt_in, f_units.index(u) + 1)
                if kind == "f0":
                    act.activation(gt[:, :, 1], gt[:, :, 0], ACT.Tanh, scale=0.5).then_inc(rt_exp, 1)
                else:
                    act.activation(le[:, :, :], lg[:, :, :], ACT.Exp, scale=-1.0).then_inc(rt_exp, 1)
                for e in range(experts[kind]):
                    ne = e_before[u] + e
                    if kind == "f0":
                        i = banks.await_full(act, ("h", u, e))
                        if ne >= 2:
                            banks.await_full(act, ("y",) + flat_e[ne - 2])
                        act.activation(hs[:, ne % 2, :], PS[:, i, :], ACT.Gelu).then_inc(banks.free[i], 1)
                    else:
                        i = banks.await_full(act, ("g", u, e))
                        if ne - 2 >= e_before[B * 5]:
                            banks.await_read(act, ("u",) + flat_e[ne - 2])
                        act.activation(sg[:, ne % 2, :], PS[:, i, :], ACT.Silu).then_inc(banks.free[i], 1)

            for step, u, a in order():
                if step in ("prep", "ffn"):
                    i = banks.await_full(act, ("xt", u))
                    act.copy(xT[:, u % 2, :], PS[:, i, 0:T]).then_inc(banks.free[i], 1)
                if step == "bexp":
                    bexp(u, a)
                elif step == "pv":
                    pv(u, a)
                elif step == "finish":
                    finish(u)
                elif step == "ffn":
                    ffn(u)

        @block.gpsimd
        def _(pool):
            nlink = [0]

            def link(ins):
                nlink[0] += 1
                ins.then_inc(p_chain, 1)
                pool.wait_ge(p_chain, nlink[0])

            link(pool.memset(ident[:, :], 0.0))
            link(pool.affine_select(out=ident[:, :], in_=ident[:, :], compare_op=ALU.not_equal, fill=1.0, base=0,
                                    pattern=[[-1, P]], channel_multiplier=1))
            link(pool.memset(flip[:, :], 0.0))
            link(pool.affine_select(out=flip[:, :], in_=flip[:, :], compare_op=ALU.not_equal, fill=1.0,
                                    base=1 - P, pattern=[[1, P]], channel_multiplier=1))
            link(pool.tensor_copy(identb[:, :], ident[:, :]))
            link(pool.iota(iota8[:, :], pattern=[[1, E]], base=0, channel_multiplier=0,
                           allow_small_or_imprecise_dtypes=True))
            link(pool.memset(ones3[:, :], 1.0))
            pool.memset(neghalf[:, :], -0.5).then_inc(consts, 1)
            pool.memset(VX[:, :, :, :, :], 1.0).then_inc(zeroed, 1)
            pool.memset(QS[:, :, :, :].bitcast(F32), 0.0).then_inc(zeroed, 1)
            pool.memset(KS[:, :, :].bitcast(F32), 0.0).then_inc(zeroed, 1)

            def parts(u, src, dst, w, ready, done, sent):
                n = AU[u]
                pool.wait_ge(ready, n + 1)
                if n:
                    pool.wait_ge(sent, 16 * sent_dmas(prev(u)))
                x = src[:, n % 2, 0:w]
                link(pool.tensor_copy(dst[:, 0, 0:w], x))
                link(pool.tensor_tensor(rf[:, 0:w], x, dst[:, 0, 0:w], ALU.subtract))
                link(pool.tensor_copy(dst[:, 1, 0:w], rf[:, 0:w]))
                pool.tensor_tensor(dst[:, 2, 0:w], rf[:, 0:w], dst[:, 1, 0:w], ALU.subtract).then_inc(done, 1)
                pool.wait_ge(done, n + 1)

            npow = [0]

            def power():
                npow[0] += 1
                pool.wait_ge(var_ready, npow[0])
                pool.tensor_tensor(rstd[:, :], ve[:, :], neghalf[:, :], ALU.pow).then_inc(rstd_ready, 1)

            for step, u, a in order():
                kind, b = UNITS[u]
                if step == "prep":
                    parts(u, qf, qp, widths[kind], q_ready, qp_ready, qp_out)
                    parts(u, kf, kp, kwidths[kind], k_ready, kp_ready, kp_out)
                elif step == "post" and kind == "x1" or step == "finish" and kind == "d1":
                    power()
                if step in ("finish", "ffn"):
                    power()

        @block.sync
        def _(sp):
            for dst, src in loads:
                sp.dma_start(dst, src).then_inc(loaded, 16)
            off = T - 1 - TB // 2
            tb, ext = I["time_bias"].tensor, ext_d
            sp.dma_start(bass.AP(tensor=ext, offset=0, ap=[[1, off], [1, 1]]),
                         bass.AP(tensor=tb, offset=0, ap=[[0, off], [1, 1]])).then_inc(ext_done, 16)
            sp.dma_start(bass.AP(tensor=ext, offset=off, ap=[[1, 1], [1, TB]]),
                         bass.AP(tensor=tb, offset=0, ap=[[1, 1], [1, TB]])).then_inc(ext_done, 16)
            end = 2 * T - off - TB
            sp.dma_start(bass.AP(tensor=ext, offset=off + TB, ap=[[1, end], [1, 1]]),
                         bass.AP(tensor=tb, offset=TB - 1, ap=[[0, end], [1, 1]])).then_inc(ext_done, 16)
            sp.wait_ge(ext_done, 48)
            for qt in range(QT):
                sp.dma_start(win[:, qt, :], bass.AP(tensor=ext, offset=P - P * qt, ap=[[1, P], [1, T]])).then_inc(win_in, 16)
            sp.wait_ge(consts, 1)
            sp.wait_ge(zeroed, 3)
            for par in range(2):
                sp.dma_start(KS[SROWS:SROWS + MROWS, par, :].rearrange("p (n w) -> p n w", w=512),
                             ones3[:, :].unsqueeze(1).to_broadcast([MROWS, 2 * H * T // 512, 512])).then_inc(ones_in, 16)

            def stack(u, par, parts_sb, ready, out_sem, dst, which, in_sem, tiles, n, c0):
                sp.wait_ge(ready, AU[u] + 1)
                if AU[u] >= 2:
                    sp.wait_ge(in_sem, 16 * NPROD * (AU[u] - 1))
                    banks.await_full(sp, last_b(prev(u, 2)))
                d = scr[2 * par + which]
                k = 0
                for (t0, tn, row, col) in tiles:
                    for p in range(3):
                        sp.dma_start(d[p, row:row + P, col:col + tn], parts_sb[:, p, t0:t0 + tn]).then_inc(out_sem, 16)
                sp.wait_ge(out_sem, 16 * sent_dmas(u))
                for j, p in enumerate((QPART, KPART)[which]):
                    src = d[p, 0:n * HD, 0:c0].rearrange("(s d) t -> d s t", d=HD)
                    sp.dma_start(dst[j * HD:(j + 1) * HD], src).then_inc(in_sem, 16)

            for step, u, a in order():
                kind, b = UNITS[u]
                if step == "prep":
                    par, n = AU[u] % 2, HEADS[kind]
                    tiles = [(c * T, T, c * P, 0) for c in range(n // H)]
                    stack(u, par, qp, qp_ready, qp_out, QS[:, par, 0:n, :], 0, qs_in, tiles, n, T)
                    if kind == "x0":
                        tiles = [(0, TC, 0, 0)]
                    elif kind == "x1":
                        tiles = [(0, TC + T, 0, 0)]
                    stack(u, par, kp, kp_ready, kp_out, kstack(u), 1, ks_in, tiles, n, KEYS[kind])
                elif step == "post" and kind == "a0":
                    sp.wait_ge(on_ready, AU[u] + 1)
                    for qt in range(QT):
                        sp.dma_start(bass.AP(tensor=mix, offset=(b * T + qt * P) * HD, ap=[[HD, P], [B * T * HD, H], [1, HD]]),
                                     on[:, qt, :].rearrange("p (h d) -> p h d", d=HD)).then_inc(mix_out, 16)
                elif step == "finish" and kind == "a0":
                    sp.wait_ge(mix_out, 16 * QT * B)
                    if u:
                        banks.await_full(sp, ("ont", u - 1))
                    sp.dma_start(cm[:, :, :], bass.AP(tensor=mix, offset=u * T * D, ap=[[D, P], [P * D, QT], [1, D]])).then_inc(mix_in, 16)
                elif step == "mneg":
                    par, n = AU[u] % 2, HEADS[kind]
                    sp.wait_ge(mp_ready, AU[u] + 1)
                    for p in range(MROWS):
                        sp.dma_start(QS[SROWS + p:SROWS + p + 1, par, 0:n, :],
                                     mp[0:n, p, :]).then_inc(m_in, 16)
                    if kind == "d1" and b == 0:
                        sp.wait_ge(x_new, u)
                        for dst, src in late:
                            sp.dma_start(dst, src).then_inc(late_in, 16)
            for n, u in enumerate(range(len(UNITS) - B, len(UNITS))):
                sp.wait_ge(x_new, u + 1)
                sp.dma_start(out[UNITS[u][1]].rearrange("(t p) d -> p t d", p=P), X[:, UNITS[u][1], :, :]).then_inc(stored, 16)
            sp.wait_ge(stored, 16 * B)

        @block.vector
        def _(dve):
            nlink = [0]

            def link(ins):
                nlink[0] += 1
                ins.then_inc(v_chain, 1)
                dve.wait_ge(v_chain, nlink[0])

            def parts(src, dst, tmp_, last=None):
                link(dve.tensor_copy(dst[0], src))
                link(dve.tensor_tensor(tmp_, src, dst[0], ALU.subtract))
                link(dve.tensor_copy(dst[1], tmp_))
                ins = dve.tensor_tensor(dst[2], tmp_, dst[1], ALU.subtract)
                if last is None:
                    link(ins)
                else:
                    ins.then_inc(last, 1)

            dve.wait_ge(loaded, 16 * NLOAD)
            dve.tensor_tensor(fs[:, :, :, :], fs[:, :, :, :], fm[:, :, :, :], ALU.add).then_inc(bias_sum, 1)
            dve.wait_ge(bias_sum, 1)
            link(dve.tensor_tensor(lam4[:, 0, :], lam4[:, 0, :], lam4[:, 1, :], ALU.mult))
            link(dve.tensor_tensor(lam4[:, 2, :], lam4[:, 2, :], lam4[:, 3, :], ALU.mult))
            dve.tensor_reduce(lam[:, 0:2], lam4[:, 0:4:2, :], AX.X, ALU.add).then_inc(lam_sums, 1)
            dve.wait_ge(act_set, 3)
            link(dve.tensor_scalar(lam[:, 5:6], lam[:, 3:4], -LAMBDA_INIT, None, ALU.add))
            link(dve.tensor_tensor(lam[:, 5:6], lam[:, 5:6], lam[:, 2:3], ALU.subtract))
            link(dve.tensor_scalar(lam[:, 6:7], lam[:, 4:5], 1.0, None, ALU.add))
            link(dve.reciprocal(lam[:, 6:7], lam[:, 6:7]))
            i = banks.await_full(dve, "ctxT")
            dve.tensor_copy(ctxT[:, :, :], PS[:, i, 0:B * TC].rearrange("p (b t) -> p b t", t=TC)).then_inc(banks.free[i], 1)
            banks.await_read(dve, "ctxT")
            link(dve.tensor_copy(ctx0[:, :, :], ctxT[:, :, 0:1].to_broadcast([P, B, P])))
            for key, raw, p3 in (("bn", bias_n, bias_np), ("bt", bias_t, bias_tp)):
                i = banks.await_full(dve, key)
                dve.tensor_scalar(raw[:, :], PS[:, i, :], lam[:, 6:7], gates[:, 1:2], ALU.mult, ALU.add).then_inc(banks.free[i], 1)
                banks.await_read(dve, key)
                parts(raw[:, :], [p3[:, p, :] for p in range(3)], rf[:, 0:QT * T])
            for h in range(2):
                i = banks.await_full(dve, ("ft", h))
                dve.tensor_copy(fst[:, 2 * h:2 * h + 2, :], PS[0:TC, i, :].rearrange("p (b t) -> p b t", t=T)).then_inc(banks.free[i], 1)
            banks.await_read(dve, ("ft", 1))
            for b in range(B):
                f = fs[:, b, :, :].rearrange("p q t -> p (q t)")
                parts(f, [fsp[:, b, p, :] for p in range(3)], rf[:, 0:QT * TC])
                parts(fst[:, b, :], [fstp[:, b, p, :] for p in range(3)], rf[0:TC, 0:T], setup_v if b == B - 1 else None)
            dve.wait_ge(setup_v, 1)
            dve.wait_ge(zeroed, 1)

            def prep(u):
                kind, b = UNITS[u]
                par, n = AU[u] % 2, AU[u]
                for which, dst, w, ready, taken in (("q", qf, widths[kind], q_ready, qp_ready),
                                                    ("k", kf, kwidths[kind], k_ready, kp_ready)):
                    i = banks.await_full(dve, (which, u))
                    if n >= 2:
                        dve.wait_ge(taken, n - 1)
                    bias = cols[kind + "_" + which][:, 0:1] if kind in ("a0", "x0") else 0.0
                    dve.tensor_scalar(dst[:, par, 0:w], PS[:, i, 0:w], bias, SCALE if which == "q" else 1.0,
                                      ALU.add, ALU.mult).then_inc(ready, 1)
                    dve.wait_ge(ready, n + 1)
                    dve.sem_inc(banks.free[i], 1)

            def vprep(u):
                kind, b = UNITS[u]
                par, n = AU[u] % 2, AU[u]
                i = banks.await_full(dve, ("v", u))
                if n >= 2:
                    u2 = prev(u, 2)
                    banks.await_full(dve, ("o", u2, groups(UNITS[u2][0]) - 1))

                def to_vx(rows_, kt, c):
                    o = VX[0:rows_, par, kt, :, 0:HD]
                    src = PS[0:rows_, i, c * D:(c + 1) * D].rearrange("p (h d) -> p h d", d=HD)
                    if kind in ("a0", "x0"):
                        return dve.tensor_tensor(o, src, rows[kind + "_v"][0:rows_, :].rearrange("p (h d) -> p h d", d=HD),
                                                 ALU.add)
                    return dve.tensor_copy(o, src)
                if kind == "x0":
                    last = to_vx(TC, 2, 0)
                else:
                    for kt in range(QT):
                        last = to_vx(P, kt, kt)
                if kind == "x1":
                    to_vx(TC - 1, 2, 2)
                    last = dve.tensor_tensor(v0[:, b, :].rearrange("p (h d) -> p h d", d=HD),
                                             PS[:, i, 3 * D:4 * D].rearrange("p (h d) -> p h d", d=HD),
                                             gate_t[:, :].unsqueeze(2).to_broadcast([P, H, HD]), ALU.mult)
                last.then_inc(banks.free[i], 1)

            def amax(u, lo, hi):
                kind, b = UNITS[u]
                items = a_items(kind)
                if lo == 0 and AU[u]:
                    banks.await_full(dve, ("m", prev(u)))
                for it in range(lo, hi):
                    s, qt = items[it]
                    i = banks.await_full(dve, ("a", u, it))
                    if kind == "x1":
                        o, src = mx[:, qt, s:s + 1], PS[:, i, 0:TC + T - 1]
                    elif kind == "x0":
                        o = mx[:, :, G4 * s:G4 * s + G4].rearrange("p q s -> p s q")
                        src = PS[:, i, :].rearrange("p (s q t) -> p s q t", q=QT, t=TC)
                    else:
                        o, src = mx[:, :, s], PS[:, i, :].rearrange("p (q t) -> p q t", t=T)
                    dve.tensor_reduce(o, src, AX.X, ALU.max).then_inc(banks.free[i], 1)

            def mneg(u):
                n = HEADS[UNITS[u][0]]
                i = banks.await_full(dve, ("m", u))
                if AU[u]:
                    dve.wait_ge(m_in, 16 * MROWS * AU[u])
                dve.tensor_scalar(mf[0:n, :], PS[0:n, i, 0:T], -1.0, TOP, ALU.mult, ALU.add).then_inc(banks.free[i], 1)
                banks.await_read(dve, ("m", u))
                parts(mf[0:n, :], [mp[0:n, p, :] for p in range(3)], mr[0:n, :], mp_ready)
                dve.wait_ge(mp_ready, AU[u] + 1)

            nvar = [0]

            def norm(src, dst, gain=None, offset=None, done=None, add=None):
                for qt in range(QT):
                    link(dve.bn_stats(st[:, :], src[qt]))
                    link(dve.bn_aggr(mv[:, qt, :], st[:, :]))
                nvar[0] += 1
                dve.tensor_scalar(ve[:, :], mv[:, :, 1], EPS, None, ALU.add).then_inc(var_ready, 1)
                dve.wait_ge(rstd_ready, nvar[0])
                for qt in range(QT):
                    ins = dve.tensor_scalar(dst[qt], src[qt], mv[:, qt, 0:1], rstd[:, qt:qt + 1], ALU.subtract, ALU.mult)
                    if gain is not None:
                        link(ins)
                        link(dve.tensor_tensor(dst[qt], dst[qt], gain, ALU.mult))
                        ins = dve.tensor_tensor(dst[qt], dst[qt], offset, ALU.add)
                    if qt == QT - 1 and done is not None:
                        ins.then_inc(done, 1)
                    else:
                        link(ins)

            def post(u):
                kind, b = UNITS[u]
                gs = groups(kind)
                if AU[u] and kind == "a0":
                    dve.wait_ge(mix_out, 16 * QT * AU[u])
                elif kind != "a0":
                    banks.await_full(dve, ("ont", prev(u)))
                for qt in range(QT):
                    for half in range(gs // 4):
                        key = ("t", u, qt, half)
                        i = banks.await_full(dve, key)
                        t = PS[:, i, :].rearrange("p (s w) -> p s w", w=STRIP)
                        link(dve.reciprocal(rs[:, :], t[:, :, HD]))
                        if kind == "d1":
                            link(dve.tensor_scalar(rs[:, 1:H:2], rs[:, 1:H:2], lam[:, 5:6], None, ALU.mult))
                            o = tmp[:, :, :]
                        else:
                            o = on[:, qt, :].rearrange("p (h d) -> p h d", d=HD)
                        dve.tensor_tensor(o, t[:, :, 0:HD], rs[:, :].unsqueeze(2).to_broadcast([P, H, HD]),
                                          ALU.mult).then_inc(banks.free[i], 1)
                        banks.await_read(dve, key)
                        if kind == "d1":
                            link(dve.tensor_tensor(on[:, qt, half * D // 2:(half + 1) * D // 2].rearrange("p (h d) -> p h d", d=HD),
                                                   tmp[:, 0:H:2, :], tmp[:, 1:H:2, :], ALU.add))
                if kind == "x1":
                    for qt in range(QT):
                        link(dve.tensor_tensor(onb[:, qt, :], on[:, qt, :], v0[:, b, :], ALU.add))
                    norm([onb[:, qt, :] for qt in range(QT)], [on[:, qt, :] for qt in range(QT)],
                         rows["x1_g"][:, :], rows["x1_b"][:, :], on_ready)
                    dve.wait_ge(on_ready, AU[u] + 1)
                else:
                    dve.sem_inc(on_ready, 1)

            def finish(u):
                kind, b = UNITS[u]
                i = banks.await_full(dve, ("wo", u))
                x = X[:, b, :, :]
                ps = PS[:, i, 0:QT * D].rearrange("p (q d) -> p q d", d=D)
                yq = [y[:, qt, :] for qt in range(QT)]
                xq = [x[:, qt, :] for qt in range(QT)]
                if kind == "d1":
                    dve.tensor_copy(y[:, :, :], ps).then_inc(banks.free[i], 1)
                    banks.await_read(dve, ("wo", u))
                    norm(yq, yq, rows["d1_g"][:, :], rows["d1_b"][:, :])
                    link(dve.tensor_tensor(y[:, :, :], y[:, :, :], x, ALU.add))
                else:
                    dve.tensor_tensor(y[:, :, :], ps, x, ALU.add).then_inc(banks.free[i], 1)
                    banks.await_read(dve, ("wo", u))
                    link(dve.tensor_tensor(y[:, :, :], y[:, :, :],
                                           rows[kind + "_o"][:, :].unsqueeze(1).to_broadcast([P, QT, D]), ALU.add))
                norm(yq, xq, done=x_new)
                dve.wait_ge(x_new, u + 1)

            def ffn(u):
                kind, b = UNITS[u]
                nf = f_units.index(u)
                i = banks.await_full(dve, ("r", u))
                ps = PS[:, i, 0:QT * E].rearrange("p (q e) -> p q e", e=E)
                if kind == "f0":
                    dve.tensor_copy(lg[:, :, :], ps).then_inc(banks.free[i], 1)
                    banks.await_read(dve, ("r", u))
                else:
                    dve.tensor_tensor(lg[:, :, :], ps, rbias[:, :].unsqueeze(1).to_broadcast([P, QT, E]),
                                      ALU.add).then_inc(rt_in, 1)
                    dve.wait_ge(rt_in, nf + 1)
                    dve.sem_inc(banks.free[i], 1)
                    dve.wait_ge(rt_exp, nf + 1)
                    link(dve.tensor_scalar(le[:, :, :], le[:, :, :], 1.0, None, ALU.add))
                    link(dve.reciprocal(lg[:, :, :], le[:, :, :]))
                for qt in range(QT):
                    link(dve.max(top[:, qt, :], lg[:, qt, :]))
                    link(dve.max_index(topi[:, qt, :], top[:, qt, :], lg[:, qt, :]))
                link(dve.tensor_copy(topf[:, :, 0:2], topi[:, :, 0:2]))
                if kind == "f0":
                    dve.tensor_tensor(gt[:, :, 0], top[:, :, 0], top[:, :, 1], ALU.subtract).then_inc(rt_in, 1)
                    dve.wait_ge(rt_exp, nf + 1)
                    link(dve.tensor_scalar(gt[:, :, 2], gt[:, :, 1], 0.5, 0.5, ALU.mult, ALU.add))
                    link(dve.tensor_scalar(gt[:, :, 3], gt[:, :, 1], -0.5, 0.5, ALU.mult, ALU.add))
                else:
                    link(dve.tensor_tensor(gt[:, :, 0], top[:, :, 0], top[:, :, 1], ALU.add))
                    link(dve.reciprocal(gt[:, :, 1], gt[:, :, 0]))
                    link(dve.tensor_tensor(gt[:, :, 2], top[:, :, 0], gt[:, :, 1], ALU.mult))
                    link(dve.tensor_tensor(gt[:, :, 3], top[:, :, 1], gt[:, :, 1], ALU.mult))
                for qt in range(QT):
                    link(dve.tensor_scalar(gate[:, qt, :], iota8[:, :], topf[:, qt, 0:1], gt[:, qt, 2:3], ALU.is_equal, ALU.mult))
                    link(dve.tensor_scalar(le[:, qt, :], iota8[:, :], topf[:, qt, 1:2], gt[:, qt, 3:4], ALU.is_equal, ALU.mult))
                    link(dve.tensor_tensor(gate[:, qt, :], gate[:, qt, :], le[:, qt, :], ALU.add))

                def add_expert(e):
                    key = ("y", u, e)
                    i = banks.await_full(dve, key)
                    for qt in range(QT):
                        ps, a_ = PS[:, i, qt * D:(qt + 1) * D], acc[:, qt, :]
                        if e == 0:
                            ins = dve.tensor_scalar(a_, ps, gate[:, qt, 0:1], None, ALU.mult)
                        elif e < E:
                            ins = dve.scalar_tensor_tensor(out=a_, in0=ps, scalar=gate[:, qt, e:e + 1], in1=a_,
                                                           op0=ALU.mult, op1=ALU.add)
                        else:
                            ins = dve.tensor_tensor(a_, ps, a_, ALU.add)
                    ins.then_inc(banks.free[i], 1)
                    banks.await_read(dve, key)

                for e in range(experts[kind]):
                    ne = e_before[u] + e
                    if kind == "f1":
                        i = banks.await_full(dve, ("u", u, e))
                        banks.await_read(dve, ("g", u, e))
                        if ne >= 2:
                            banks.await_full(dve, ("y",) + flat_e[ne - 2])
                        dve.tensor_tensor(hs[:, ne % 2, :], PS[:, i, :], sg[:, ne % 2, :], ALU.mult).then_inc(banks.free[i], 1)
                    if e:
                        add_expert(e - 1)
                add_expert(experts[kind] - 1)
                link(dve.tensor_tensor(y[:, :, :], acc[:, :, :], X[:, b, :, :], ALU.add))
                norm([y[:, qt, :] for qt in range(QT)], [X[:, b, qt, :] for qt in range(QT)], done=x_new)
                dve.wait_ge(x_new, u + 1)

            for step, u, a in order():
                if step == "prep":
                    prep(u)
                elif step == "vprep":
                    vprep(u)
                elif step == "amax":
                    amax(u, *part_of(u, a))
                elif step == "mneg":
                    mneg(u)
                elif step == "post":
                    post(u)
                elif step == "finish":
                    finish(u)
                elif step == "ffn":
                    ffn(u)


def kernel(**inputs):
    import numpy as np
    import concourse.bacc as bacc
    from concourse.bass_utils import run_bass_kernel_spmd as run

    g = {k: np.asarray(v) for k, v in inputs.items()}
    t = np.transpose
    a = {
        "x": g["x"], "ctx_1024": g["ctx_1024"], "fside_BxSxS2_0": g["fside_BxSxS2_0"],
        "mask_BxSxS2_ff0": g["mask_BxSxS2_ff0"],
        "w_a0_q": g["L0_attn_Wq"].T, "w_a0_k": g["L0_attn_Wk"].T, "w_a0_v": g["L0_attn_Wv"].T,
        "w_a0_o": g["L0_attn_Wo"].T, "w_x0_q": g["L0_xattn_Wq"], "w_x0_k": g["L0_xattn_Wk"],
        "w_x0_v": g["L0_xattn_Wv"], "w_x0_o": g["L0_xattn_Wo"], "w_d1_q": g["L1_attn_Wq"],
        "w_d1_k": g["L1_attn_Wk"], "w_d1_v": g["L1_attn_Wv"], "w_d1_o": g["L1_attn_Wo"],
        "w_x1_q": g["L1_xattn_Wq"].T, "w_x1_k": g["L1_xattn_Wk"].T, "w_x1_v": g["L1_xattn_Wv"].T,
        "w_x1_o": g["L1_xattn_Wp"].T, "w_f0_r": g["L0_ffn_router_w"].T, "w_f1_r": g["L1_ffn_router_w"].T,
        "c_a0_q": g["L0_attn_bq"].reshape(D, 1), "c_a0_k": g["L0_attn_bk"].reshape(D, 1),
        "c_x0_q": g["L0_xattn_bq"].reshape(D, 1), "c_x0_k": g["L0_xattn_bk"].reshape(D, 1),
        "r_a0_v": g["L0_attn_bv"], "r_a0_o": g["L0_attn_bo"], "r_x0_v": g["L0_xattn_bv"], "r_x0_o": g["L0_xattn_bo"],
        "r_d1_g": g["L1_attn_gamma"], "r_d1_b": g["L1_attn_beta"], "r_x1_g": g["L1_xattn_ln_g"],
        "r_x1_b": g["L1_xattn_ln_b"], "r_x1_o": g["L1_xattn_bp"], "rbias": g["L1_ffn_routing_bias"],
        "gate": g["L1_xattn_gate"].reshape(H), "et_gate": g["L0_attn_et_gate"].reshape(1),
        "is_gate": g["L0_attn_is_gate"].reshape(1), "time_bias": g["L0_attn_time_bias"].reshape(1, TB),
        "lq1": g["L1_attn_lambda_q1"], "lk1": g["L1_attn_lambda_k1"], "lq2": g["L1_attn_lambda_q2"],
        "lk2": g["L1_attn_lambda_k2"], "w1": t(g["L0_ffn_w1"], (0, 2, 1)), "w2": t(g["L0_ffn_w2"], (0, 2, 1)),
        "wg": t(g["L1_ffn_wg"], (0, 2, 1)), "wu": t(g["L1_ffn_wu"], (0, 2, 1)), "wd": t(g["L1_ffn_wd"], (0, 2, 1)),
        "sg": g["L1_ffn_sg_w"].T, "su": g["L1_ffn_su_w"].T, "sd": g["L1_ffn_sd_w"].T,
    }
    nc = bacc.Bacc("TRN2", target_bir_lowering=False, num_devices=1)
    arrays, I = {}, {}
    for name, v in a.items():
        v = np.ascontiguousarray(v)
        arrays["in_" + name] = v
        I[name] = nc.dram_tensor("in_" + name, v.shape, mybir.dt.from_np(v.dtype), kind="ExternalInput").ap()
    out = nc.dram_tensor("out_0", (B, T, D), F32, kind="ExternalOutput").ap()
    decoder(nc, I, out)
    r = run(nc, [arrays], core_ids=[0])
    return r.results[0]["out_0"]
```

```python
from contextlib import ExitStack

import concourse.bass as bass
from concourse import mybir

F32 = mybir.dt.float32
BF16 = mybir.dt.bfloat16
U32 = mybir.dt.uint32
ACT = mybir.ActivationFunctionType
ALU = mybir.AluOpType
AX = mybir.AxisListType

P = 128
B, T, D = 4, 256, 128
TC = 64
H, HD = 16, 8
QT = T // P
E, HID = 8, 256
HH = HID // P
STRIP = 32
G4 = P // STRIP
NPROD = 6
KPART = (0, 0, 1, 0, 2, 1)
QPART = (0, 1, 0, 2, 0, 1)
SROWS = NPROD * HD
MROWS = 3
SCALE = float(HD) ** -0.5
EXPERTS = {"f0": E, "f1": E + 1}
AFTER = 8
LAMBDA_INIT = 0.8 - 0.6 * 2.718281828459045 ** (-0.3 * 11)
EPS = 1e-5
TB = 500
TOP = -1.0

KINDS = ("a0", "x0", "f0", "d1", "x1", "f1")
UNITS = [(kind, b) for kind in KINDS for b in range(B)]
HEADS = {"a0": H, "x0": H, "d1": 2 * H, "x1": H}
KEYS = {"a0": T, "x0": TC, "d1": T, "x1": TC + T}
ATT = [u for u, (k, _) in enumerate(UNITS) if k[0] != "f"]
ORDER_A = {u: n for n, u in enumerate(ATT)}


def a_items(kind):
    if kind == "x0":
        return [(g, 0) for g in range(H // G4)]
    if kind == "x1":
        return [(s, qt) for s in range(H) for qt in range(QT)]
    return [(s, 0) for s in range(HEADS[kind])]


def b_items(kind, g):
    s0 = G4 * g
    if kind == "x0":
        return [("c", s0), ("c", s0 + 2)]
    if kind == "x1":
        return [("c", s0), ("c", s0 + 2)] + [("s", s0 + j) for j in range(G4)]
    return [("s", s0 + j) for j in range(G4)]


def groups(kind):
    return HEADS[kind] // G4


def turned(u):
    return QT * groups(UNITS[u][0]) // 4


AT_ONT, AT_WO, AT_XT, AT_PREP = 5, 6, 7, 8
FIRST_EXPERTS, AT_EXPERTS = 20, 8


def order():
    def expert_steps(u):
        return [("route", u, 0)] + [("ffn", u, e) for e in range(EXPERTS[UNITS[u][0]])] + [("ffn_end", u, 0)]

    def chain(us):
        queue = []
        now = [0]

        def due(until=None):
            while queue and (queue[0][0] <= now[0] or until is not None):
                step = queue.pop(0)[1]
                yield step
                if step[:2] == ("ffn_end", until):
                    return

        yield "xt", us[0], 0
        yield "prep", us[0], 0
        if UNITS[us[0]][0] == "a0":
            yield "setup_bias", 0, 0
        yield "amax", us[0], (0, 1)
        yield "mneg", us[0], 0
        yield "vprep", us[0], 0
        yield "xt", us[1], 0
        yield "prep", us[1], 0
        yield "vprep", us[1], 0
        for n, u in enumerate(us):
            kind = UNITS[u][0]
            G = groups(kind)
            more, mixed = n + 1 < len(us), kind == "a0"
            items = [(g, i) for g in range(G) for i in range(len(b_items(kind, g)))]
            N = len(items)
            also = {}
            if n:
                for k in range(turned(us[n - 1])):
                    also.setdefault(1 + k, []).append(("post", us[n - 1], k))
                if not mixed:
                    also.setdefault(AT_ONT * N // 16, []).append(("ont", us[n - 1], 0))
                    also.setdefault(AT_WO * N // 16, []).append(("wo", us[n - 1], 0))
            if n + 2 < len(us):
                also.setdefault(AT_XT * N // 16, []).append(("xt", us[n + 2], 0))
                also.setdefault(AT_PREP * N // 16, []).append(("prep", us[n + 2], 0))
            if mixed and n == 2:
                also.setdefault(N // 2, []).append(("setup_cross", 0, 0))
            late = N // AFTER
            for k, (g, i) in enumerate(items):
                yield "bexp", u, (g, i)
                if more and k >= late:
                    yield "amax", us[n + 1], (k - late, N - late)
                if i == 1 and g:
                    yield "pv", u, g - 1
                for step in also.get(k, ()):
                    if step[0] == "xt" and UNITS[step[1]][0] == "d1":
                        yield from due(step[1] - B)
                    yield step
                    if step[0] == "wo" and UNITS[step[1]][0] in ("x0", "x1"):
                        steps = expert_steps(step[1] + B)
                        queue += [(n + 1 if j < FIRST_EXPERTS else n + 1 + AT_EXPERTS / 16, st)
                                  for j, st in enumerate(steps)]
                now[0] = n + (k + 1) / (N + 1)
                yield from due()
            if more:
                yield "mneg", us[n + 1], 0
            now[0] = n + 1
            yield from due()
            yield "pv", u, G - 1
            if n + 2 < len(us):
                yield "vprep", us[n + 2], 0
        for k in range(turned(us[-1])):
            yield "post", us[-1], k
            now[0] += 1 / 16
            yield from due()
        for u in us if UNITS[us[0]][0] == "a0" else us[-1:]:
            yield "ont", u, 0
            yield "wo", u, 0
        if UNITS[us[-1]][0] == "x1":
            yield from due(us[-1] + B - 1)
            yield from expert_steps(us[-1] + B)

    for kinds in (("a0",), ("x0", "d1", "x1")):
        yield from chain([u for u, (k, _) in enumerate(UNITS) if k in kinds])


X_COUNT = {u: n + 1 for n, u in enumerate(u for step, u, _ in order() if step in ("wo", "ffn_end"))}


def part_of(u, part):
    n, m = part
    items = len(a_items(UNITS[u][0]))
    return items * n // m, items * (n + 1) // m


class Banks:

    def __init__(self, ctx, nc):
        self.full = [ctx.enter_context(nc.semaphore(f"bank{i}_full")) for i in range(8)]
        self.free = [ctx.enter_context(nc.semaphore(f"bank{i}_free")) for i in range(8)]
        self.uses = [0] * 8
        self.place = {}
        self.turn = {}

    def take(self, pe, key, pool):
        t = self.turn.get(pool, 0)
        self.turn[pool] = t + 1
        i = pool[t % len(pool)]
        n = self.uses[i]
        self.uses[i] = n + 1
        self.place[key] = (i, n)
        if n:
            pe.wait_ge(self.free[i], n)
        return i

    def await_full(self, eng, key):
        i, n = self.place[key]
        eng.wait_ge(self.full[i], n + 1)
        return i

    def await_read(self, eng, key):
        i, n = self.place[key]
        eng.wait_ge(self.free[i], n + 1)


POOL_A, POOL_B, POOL_O, POOL_M = (0, 1), (2, 3), (4, 5), (6, 7)


def decoder(nc, I, out):
    with ExitStack() as ctx:
        def sb(name, shape, dt=F32):
            return ctx.enter_context(nc.sbuf_tensor(name, shape, dt))

        def sem(name):
            return ctx.enter_context(nc.semaphore(name))

        banks = Banks(ctx, nc)
        PS = ctx.enter_context(nc.psum_tensor("PS", [P, 8, 512], F32))
        scr = nc.dram_tensor("parts_scratch", (4, 3, 2 * P, TC + T), BF16).ap()
        mix = nc.dram_tensor("mix_scratch", (H, B, T, HD), F32)
        ext_d = nc.dram_tensor("bias_scratch", (1, 512), F32)

        X = sb("X", [P, B, QT, D])
        C = sb("C", [TC, B, D])
        ctxT = sb("ctxT", [P, B, TC])
        ident = sb("ident", [P, P])
        identb = sb("identb", [P, P], BF16)
        flip = sb("flip", [P, P])
        W = {}
        for n, w in (("a0_q", D), ("a0_k", D), ("a0_v", D), ("a0_o", D), ("x0_q", D), ("x0_k", D), ("x0_v", D),
                     ("x0_o", D), ("d1_q", 2 * D), ("d1_k", 2 * D), ("d1_v", D), ("d1_o", D), ("x1_q", D),
                     ("x1_k", D), ("x1_v", D), ("x1_o", D), ("f0_r", E), ("f1_r", E)):
            W[n] = sb("w_" + n, [P, w])
        FW = sb("FW", [P, 2 * (E + 1) * HID])
        w1 = FW[:, 0:E * HID].rearrange("p (e i) -> p e i", i=HID)
        w2 = FW[:, E * HID:2 * E * HID].rearrange("p (e t d) -> p e t d", t=HH, d=D)
        wg = FW[:, 0:(E + 1) * HID].rearrange("p (e i) -> p e i", i=HID)
        wu = FW[:, (E + 1) * HID:2 * (E + 1) * HID].rearrange("p (e i) -> p e i", i=HID)
        wd = sb("wd", [P, E + 1, HH, D])
        cols = {n: sb("c_" + n, [P, 1]) for n in ("a0_q", "a0_k", "x0_q", "x0_k")}
        rows = {n: sb("r_" + n, [P, D]) for n in ("a0_v", "a0_o", "x0_v", "x0_o", "d1_g", "d1_b", "x1_g",
                                                   "x1_b", "x1_o")}
        rbias = sb("rbias", [P, E])
        gate_t = sb("gate_t", [P, H])
        gates = sb("gates", [P, 2])
        lam4 = sb("lam4", [P, 4, HD])
        lam = sb("lam", [P, 8])
        neghalf = sb("neghalf", [P, 2])
        iota8 = sb("iota8", [P, E])
        ones3 = sb("ones3", [MROWS, 512], BF16)

        PR = sb("PR", [P, 12, 512])
        win = PR[:, 0, :].rearrange("p (q t) -> p q t", t=T)
        bias_n = PR[:, 1, :]
        bias_t = PR[:, 2, :]
        fs = PR[:, 4, :].rearrange("p (b q t) -> p b q t", b=B, t=TC)
        fm = PR[:, 5, :].rearrange("p (b q t) -> p b q t", b=B, t=TC)
        fst = PR[0:TC, 10:12, :].rearrange("p x (b t) -> p (x b) t", t=T)
        hid = [sb(f"hid{i}", [P, 3 * QT * T // 2]) for i in range(2)]
        bias_np, bias_tp = (h[:, :].bitcast(BF16).rearrange("p (c t) -> p c t", c=3) for h in hid)
        sig = sb("sig", [P, 3 * B * QT * TC // 2])
        fsp = sig[:, :].bitcast(BF16).rearrange("p (b c t) -> p b c t", b=B, c=3)
        fstp = sb("fstp", [TC, B, 3, T], BF16)

        xT = sb("xT", [P, B, T])
        ctx0 = sb("ctx0", [P, B, P])
        qf = sb("qf", [P, 2 * T])
        kf = sb("kf", [P, 2 * T])
        rf = sb("rf", [P, 2 * T])
        vf = sb("vf", [P, 2 * T])
        hs = [h[:, 0:HH * T] for h in hid]
        sg = [sig[:, 0:HH * T], vf[:, :]]
        qp = sb("qp", [P, 3, 2 * T], BF16)
        kp = sb("kp", [P, 3, 2 * T], BF16)
        QS = sb("QS", [P, 2, 2 * H, T], BF16)
        KS = sb("KS", [P, 2, 2 * H * T], BF16)
        VX = sb("VX", [P, 2, 3, H, STRIP])
        v0 = sb("v0", [P, B, D])
        mx = sb("mx", [P, 2, 2 * H])
        mf = sb("mf", [2 * H, T])
        mr = sb("mr", [2 * H, T])
        mp = sb("mp", [2 * H, 3, T], BF16)
        OR = sb("OR", [P, 8, T])
        on = sb("on", [P, QT, D])
        cm = sb("cm", [P, QT, D])
        onb = sb("onb", [P, QT, D], BF16)
        tmp = sb("tmp", [P, H, HD])
        rs = sb("rs", [P, H])
        OT = sb("OT", [P, QT, P])
        y = sb("y", [P, QT, D])
        st = sb("st", [P, 6])
        mv = sb("mv", [P, QT, 2])
        ve = sb("ve", [P, QT])
        rstd = sb("rstd", [P, QT])
        acc = sb("acc", [P, QT, D])
        lg = sb("lg", [P, QT, E])
        le = sb("le", [P, QT, E])
        top = sb("top", [P, QT, 8])
        topi = sb("topi", [P, QT, 8], U32)
        topf = sb("topf", [P, QT, 8])
        gt = sb("gt", [P, QT, 8])
        gate = sb("gate", [P, B, QT, E])

        in_first = sem("in_first")
        in_a0 = sem("in_a0")
        in_cross = sem("in_cross")
        in_rest = sem("in_rest")
        late_in = sem("late_in")
        ext_done = sem("ext_done")
        win_in = sem("win_in")
        consts = sem("consts")
        zeroed = sem("zeroed")
        cleared = sem("cleared")
        ones_in = sem("ones_in")
        bias_sum = sem("bias_sum")
        setup_v = sem("setup_v")
        lam_sums = sem("lam_sums")
        act_set = sem("act_set")
        v_chain = sem("v_chain")
        p_chain = sem("p_chain")
        x_new = sem("x_new")
        q_ready = sem("q_ready")
        k_ready = sem("k_ready")
        qp_ready = sem("qp_ready")
        kp_ready = sem("kp_ready")
        qp_out = sem("qp_out")
        kp_out = sem("kp_out")
        qs_in = sem("qs_in")
        ks_in = sem("ks_in")
        mp_ready = sem("mp_ready")
        m_in = sem("m_in")
        on_ready = sem("on_ready")
        mix_out = sem("mix_out")
        mix_in = sem("mix_in")
        var_ready = sem("var_ready")
        rstd_ready = sem("rstd_ready")
        rt_in = sem("rt_in")
        rt_exp = sem("rt_exp")
        stored = sem("stored")

        ks_view = [KS[:, par, :] for par in range(2)]

        def kstack(u):
            kind, _ = UNITS[u]
            n = KEYS[kind]
            return ks_view[ORDER_A[u] % 2][:, 0:HEADS[kind] * n].rearrange("p (s t) -> p s t", t=n)

        AU = ORDER_A
        groups_before = {}
        pbanks_before = {}
        gsum = psum_ = 0
        for u in ATT:
            groups_before[u], pbanks_before[u] = gsum, psum_
            for g in range(groups(UNITS[u][0])):
                gsum += 1
                psum_ += len(b_items(UNITS[u][0], g))

        def p_slot(u, g, i):
            return ((groups_before[u] + g) % 2) * 6 + i

        def p_count(u, g):
            return pbanks_before[u] + sum(len(b_items(UNITS[u][0], x)) for x in range(g + 1))

        f_units = [u for u, (k, _) in enumerate(UNITS) if k[0] == "f"]
        e_before, n = {}, 0
        for u in f_units:
            e_before[u] = n
            n += EXPERTS[UNITS[u][0]]
        flat_e = [(u, e) for u in f_units for e in range(EXPERTS[UNITS[u][0]])]
        widths = {"a0": T, "x0": T, "d1": 2 * T, "x1": T}
        kwidths = {"a0": T, "x0": TC, "d1": 2 * T, "x1": TC + T}
        kdmas, n = {}, 0
        for u in ATT:
            n += 1
            kdmas[u] = 16 * NPROD * n

        def ks_count(u):
            return kdmas[u]

        def last_b(u):
            g = groups(UNITS[u][0]) - 1
            return ("b", u, g, len(b_items(UNITS[u][0], g)) - 1)

        def prev(u, k=1):
            return ATT[AU[u] - k] if AU[u] >= k else None

        def sent_dmas(u):
            return sum(3 * (HEADS[UNITS[v][0]] // H) for v in ATT if v <= u)

        def last_t(u):
            return ("t", u, QT - 1, groups(UNITS[u][0]) // 4 - 1)

        block = ctx.enter_context(nc.Block())
        def weight(*names):
            return [(W[n][:, :], I["w_" + n]) for n in names]

        def column(*names):
            return [(cols[n][:, :], I["c_" + n]) for n in names]

        def row(*names):
            return [(rows[n][:, :], I["r_" + n].partition_broadcast(P)) for n in names]

        load_first = [(X[:, :, :, :], I["x"].rearrange("b (t p) d -> p b t d", p=P))] + \
            weight("a0_q", "a0_k") + column("a0_q", "a0_k") + \
            [(gates[:, 0:1], I["et_gate"].partition_broadcast(P)), (gates[:, 1:2], I["is_gate"].partition_broadcast(P))]
        load_a0 = weight("a0_v", "a0_o") + row("a0_v", "a0_o")
        load_cross = [
            (C[:, :, :], I["ctx_1024"].rearrange("b t d -> t b d")),
            (fs[:, :, :, :], I["fside_BxSxS2_0"].rearrange("b (t p) k -> p b t k", p=P)),
            (fm[:, :, :, :], I["mask_BxSxS2_ff0"].rearrange("b (t p) k -> p b t k", p=P)),
        ] + weight("x0_q", "x0_k", "x0_v", "x0_o") + column("x0_q", "x0_k") + row("x0_v", "x0_o")
        load_rest = weight("f0_r") + [(w1[:, :, :], I["w1"].rearrange("e h i -> h e i")),
                                      (w2[:, :, :, :], I["w2"].rearrange("e (t p) d -> p e t d", p=P))]
        load_rest += weight("d1_q", "d1_k", "d1_v", "d1_o", "x1_q", "x1_k", "x1_v", "x1_o", "f1_r")
        load_rest += row("d1_g", "d1_b", "x1_g", "x1_b", "x1_o")
        load_rest += [(rbias[:, :], I["rbias"].partition_broadcast(P)), (gate_t[:, :], I["gate"].partition_broadcast(P))]
        load_rest += [(lam4[:, i, :], I[n].partition_broadcast(P)) for i, n in enumerate(("lq1", "lk1", "lq2", "lk2"))]
        load_rest += [(wd[:, 0:E, :, :], I["wd"].rearrange("e (t p) d -> p e t d", p=P)),
                      (wd[:, E, :, :], I["sd"].rearrange("(t p) d -> p t d", p=P))]
        N_FIRST, N_A0, N_CROSS, N_REST = (16 * len(x) for x in (load_first, load_a0, load_cross, load_rest))
        late = [(wg[:, 0:E, :], I["wg"].rearrange("e h i -> h e i")), (wg[:, E, :], I["sg"]),
                (wu[:, 0:E, :], I["wu"].rearrange("e h i -> h e i")), (wu[:, E, :], I["su"])]

        @block.tensor
        def _(pe):
            def mm(o, l, r, start, stop):
                return pe.matmul(o, l, r, start=start, stop=stop, skip_group_check=True)

            pe.wait_ge(in_first, N_FIRST)
            pe.wait_ge(consts, 1)

            def setup_bias():
                pe.wait_ge(win_in, 16 * QT)
                i = banks.take(pe, "bn", POOL_M)
                for qt in range(QT):
                    last = mm(PS[:, i, qt * T:(qt + 1) * T], flip[:, :], win[:, qt, :], True, True)
                last.then_inc(banks.full[i], 1)
                i = banks.take(pe, "bt", POOL_M)
                for kt in range(QT):
                    for qt in range(QT):
                        last = mm(PS[:, i, kt * T + qt * P:kt * T + (qt + 1) * P], win[:, qt, kt * P:(kt + 1) * P],
                                  flip[:, :], True, True)
                last.then_inc(banks.full[i], 1)

            def setup_cross():
                pe.wait_ge(in_cross, N_CROSS)
                i = banks.take(pe, "ctxT", POOL_M)
                for b in range(B):
                    last = pe.transpose(PS[:, i, b * TC:(b + 1) * TC], C[:, b, :], ident[0:TC, 0:TC])
                last.then_inc(banks.full[i], 1)
                pe.wait_ge(bias_sum, 1)
                for h in range(2):
                    i = banks.take(pe, ("ft", h), POOL_M)
                    for b2 in range(2):
                        for qt in range(QT):
                            last = pe.transpose(PS[0:TC, i, b2 * T + qt * P:b2 * T + (qt + 1) * P],
                                                fs[:, 2 * h + b2, qt, :], ident[:, :])
                    last.then_inc(banks.full[i], 1)

            def tokens(u):
                kind, b = UNITS[u]
                if kind != "a0":
                    pe.wait_ge(x_new, X_COUNT[u - B])
                i = banks.take(pe, ("xt", u), POOL_M)
                for qt in range(QT):
                    last = pe.transpose(PS[:, i, qt * P:(qt + 1) * P], X[:, b, qt, :], ident[:, :])
                last.then_inc(banks.full[i], 1)

            def prep(u):
                kind, b = UNITS[u]
                if kind == "x0" and b == 0:
                    pe.wait_ge(setup_v, 2)
                elif kind == "d1" and b == 0:
                    pe.wait_ge(in_rest, N_REST)
                x = xT[:, b, :]
                banks.await_read(pe, ("xt", u))
                nq = HEADS[kind] // H
                i = banks.take(pe, ("q", u), POOL_M)
                for c in range(nq):
                    last = mm(PS[:, i, c * T:(c + 1) * T], W[kind + "_q"][:, c * D:(c + 1) * D], x, True, True)
                last.then_inc(banks.full[i], 1)
                i = banks.take(pe, ("k", u), POOL_M)
                at = 0
                if kind in ("x0", "x1"):
                    last = mm(PS[:, i, 0:TC], W[kind + "_k"][:, :], ctxT[:, b, :], True, True)
                    at = TC
                if kind != "x0":
                    for c in range(nq):
                        last = mm(PS[:, i, at + c * T:at + (c + 1) * T], W[kind + "_k"][:, c * D:(c + 1) * D], x,
                                  True, True)
                last.then_inc(banks.full[i], 1)

            def vprep(u):
                kind, b = UNITS[u]
                x = xT[:, b, :]
                if u == 0:
                    pe.wait_ge(in_a0, N_A0)
                i = banks.take(pe, ("v", u), POOL_M)
                w = W[kind + "_v"][:, :]
                if kind != "x0":
                    for qt in range(QT):
                        last = mm(PS[:, i, qt * D:(qt + 1) * D], x[:, qt * P:(qt + 1) * P], w, True, True)
                if kind == "x0":
                    last = mm(PS[0:TC, i, 0:D], ctxT[:, b, :], w, True, True)
                if kind == "x1":
                    mm(PS[0:TC - 1, i, 2 * D:3 * D], ctxT[:, b, 1:TC], w, True, True)
                    last = mm(PS[:, i, 3 * D:4 * D], ctx0[:, b, :], w, True, True)
                last.then_inc(banks.full[i], 1)

            def amax(u, lo, hi):
                kind, b = UNITS[u]
                items = a_items(kind)
                if kind == "a0" and b == 0:
                    pe.wait_ge(setup_v, 1)
                if lo == 0 and hi:
                    pe.wait_ge(qs_in, 16 * NPROD * (AU[u] + 1))
                    pe.wait_ge(ks_in, ks_count(u))
                q, k = QS[0:SROWS, AU[u] % 2], kstack(u)[0:SROWS]
                for it in range(lo, hi):
                    s, qt1 = items[it]
                    i = banks.take(pe, ("a", u, it), POOL_A)
                    if kind == "x1":
                        last = mm(PS[:, i, 0:TC + T - 1], q[:, s, qt1 * P:(qt1 + 1) * P], k[:, s, 1:TC + T], True, True)
                    elif kind == "x0":
                        for p in range(3):
                            r = fsp[:, b, p, :].unsqueeze(1).to_broadcast([P, G4, QT * TC])
                            mm(PS[:, i, :], identb[:, :], r, p == 0, False)
                        for j in range(G4):
                            for qt in range(QT):
                                o = (j * QT + qt) * TC
                                last = mm(PS[:, i, o:o + TC], q[:, G4 * s + j, qt * P:(qt + 1) * P],
                                          k[:, G4 * s + j, :], False, j == G4 - 1 and qt == QT - 1)
                    else:
                        if kind == "a0":
                            for p in range(3):
                                mm(PS[:, i, :], identb[:, :], bias_np[:, p, :], p == 0, False)
                        for qt in range(QT):
                            last = mm(PS[:, i, qt * T:(qt + 1) * T], q[:, s, qt * P:(qt + 1) * P], k[:, s, :],
                                      kind == "d1", True)
                    last.then_inc(banks.full[i], 1)

            def mneg(u):
                n = HEADS[UNITS[u][0]]
                banks.await_read(pe, ("a", u, len(a_items(UNITS[u][0])) - 1))
                i = banks.take(pe, ("m", u), POOL_M)
                for qt in range(QT):
                    last = pe.transpose(PS[0:n, i, qt * P:(qt + 1) * P], mx[:, qt, 0:n], ident[:, :])
                last.then_inc(banks.full[i], 1)

            def bexp(u, g, n):
                kind, b = UNITS[u]
                if g == 0 and n == 0:
                    pe.wait_ge(m_in, 16 * MROWS * (AU[u] + 1))
                    pe.wait_ge(ones_in, 32)
                q, k = QS[:, AU[u] % 2], kstack(u)
                off = TC if kind == "x1" else 0
                c0 = 1 if kind == "x1" else 0
                what, s = b_items(kind, g)[n]
                i = banks.take(pe, ("b", u, g, n), POOL_B)
                if what == "c":
                    if kind == "x0":
                        for p in range(3):
                            r = fstp[:, b, p, :].unsqueeze(1).to_broadcast([TC, 2, T])
                            mm(PS[0:TC, i, :], identb[0:TC, 0:TC], r, p == 0, False)
                    for j in range(2):
                        last = mm(PS[0:TC - c0, i, j * T:(j + 1) * T], k[:, s + j, c0:TC], q[:, s + j, :],
                                  kind == "x1", True)
                else:
                    if kind == "a0":
                        for p in range(3):
                            mm(PS[:, i, :], identb[:, :], bias_tp[:, p, :], p == 0, False)
                    for kt in range(QT):
                        last = mm(PS[:, i, kt * T:(kt + 1) * T], k[:, s, off + kt * P:off + (kt + 1) * P],
                                  q[:, s, :], kind != "a0", True)
                last.then_inc(banks.full[i], 1)

            def pv(u, g):
                kind, b = UNITS[u]
                for n in range(len(b_items(kind, g))):
                    banks.await_read(pe, ("b", u, g, n))
                if g == 0:
                    banks.await_read(pe, ("v", u))
                i = banks.take(pe, ("o", u, g), POOL_O)
                V = VX[:, AU[u] % 2]
                terms = []
                nc0 = 2 if kind in ("x0", "x1") else 0
                if nc0:
                    rowsc = TC - (kind == "x1")
                    terms.append([(V[0:rowsc, 2], PR[0:rowsc, p_slot(u, g, j // 2), (j % 2) * T:(j % 2 + 1) * T])
                                  for j in range(G4)])
                if kind != "x0":
                    for kt in range(QT):
                        terms.append([(V[:, kt], PR[:, p_slot(u, g, nc0 + j), kt * T:(kt + 1) * T])
                                      for j in range(G4)])
                for n, term in enumerate(terms):
                    for j, (v, p) in enumerate(term):
                        s = G4 * g + j
                        h = s // 2 if kind == "d1" else s
                        last = mm(PS[STRIP * j:STRIP * (j + 1), i, 0:T], v[:, h, :], p, n == 0, n == len(terms) - 1)
                last.then_inc(banks.full[i], 1)

            def post(u, k):
                kind, b = UNITS[u]
                gs = groups(kind)
                if k == 0:
                    for g in range(gs):
                        banks.await_read(pe, ("o", u, g))
                qt, half = divmod(k, gs // 4)
                i = banks.take(pe, ("t", u, qt, half), POOL_M)
                for g in range(4):
                    last = pe.transpose(PS[:, i, g * P:(g + 1) * P], OR[:, 4 * half + g, qt * P:(qt + 1) * P],
                                        ident[:, :])
                last.then_inc(banks.full[i], 1)

            def ont(u):
                kind, b = UNITS[u]
                if kind == "a0":
                    pe.wait_ge(mix_in, 16 * (u + 1))
                else:
                    pe.wait_ge(on_ready, AU[u] + 1)
                src = cm if kind == "a0" else on
                i = banks.take(pe, ("ont", u), POOL_M)
                for qt in range(QT):
                    last = pe.transpose(PS[:, i, qt * P:(qt + 1) * P], src[:, qt, :], ident[:, :])
                last.then_inc(banks.full[i], 1)

            def wo(u):
                kind, b = UNITS[u]
                banks.await_read(pe, ("ont", u))
                i = banks.take(pe, ("wo", u), POOL_M)
                for qt in range(QT):
                    last = mm(PS[:, i, qt * D:(qt + 1) * D], OT[:, qt, :], W[kind + "_o"][:, :], True, True)
                last.then_inc(banks.full[i], 1)

            def route(u):
                kind, b = UNITS[u]
                tokens(u)
                banks.await_read(pe, ("xt", u))
                x = xT[:, b, :]
                if kind == "f0":
                    pe.wait_ge(in_rest, N_REST)
                i = banks.take(pe, ("r", u), POOL_M)
                for qt in range(QT):
                    last = mm(PS[:, i, qt * E:(qt + 1) * E], x[:, qt * P:(qt + 1) * P], W[kind + "_r"][:, :], True, True)
                last.then_inc(banks.full[i], 1)

            def up(u, e):
                kind, b = UNITS[u]
                x = xT[:, b, :]
                if kind == "f1":
                    pe.wait_ge(late_in, 16 * len(late))
                for j, (name, w) in enumerate([("h", w1)] if kind == "f0" else [("g", wg), ("u", wu)]):
                    i = banks.take(pe, (name, u, e), (POOL_A, POOL_B)[j])
                    for t in range(HH):
                        last = mm(PS[:, i, t * T:(t + 1) * T], w[:, e, t * P:(t + 1) * P], x, True, True)
                    last.then_inc(banks.full[i], 1)

            def down(u, e):
                kind, b = UNITS[u]
                w = w2 if kind == "f0" else wd
                ne = e_before[u] + e
                banks.await_read(pe, ("h" if kind == "f0" else "u", u, e))
                i = banks.take(pe, ("y", u, e), POOL_O)
                for qt in range(QT):
                    for t in range(HH):
                        last = mm(PS[:, i, qt * D:(qt + 1) * D],
                                  hs[ne % 2][:, t * T + qt * P:t * T + (qt + 1) * P], w[:, e, t, :],
                                  t == 0, t == HH - 1)
                last.then_inc(banks.full[i], 1)

            for step, u, a in order():
                if step == "setup_bias":
                    setup_bias()
                elif step == "setup_cross":
                    setup_cross()
                elif step == "route":
                    route(u)
                elif step == "prep":
                    prep(u)
                elif step == "vprep":
                    vprep(u)
                elif step == "amax":
                    lo, hi = part_of(u, a)
                    amax(u, lo, hi)
                elif step == "mneg":
                    mneg(u)
                elif step == "bexp":
                    bexp(u, *a)
                elif step == "pv":
                    pv(u, a)
                elif step == "post":
                    post(u, a)
                elif step == "ont":
                    ont(u)
                elif step == "wo":
                    wo(u)
                elif step == "xt":
                    tokens(u)
                elif step == "ffn":
                    up(u, a)
                    if a:
                        down(u, a - 1)
                elif step == "ffn_end":
                    down(u, EXPERTS[UNITS[u][0]] - 1)

        @block.scalar
        def _(act):
            act.wait_ge(in_first, N_FIRST)
            act.activation(lam[:, 4:5], gates[:, 0:1], ACT.Exp, scale=-1.0).then_inc(act_set, 1)

            def setup_rest():
                act.wait_ge(in_rest, N_REST)
                act.activation(gate_t[:, :], gate_t[:, :], ACT.Tanh).then_inc(act_set, 1)
                act.wait_ge(lam_sums, 1)
                act.activation(lam[:, 2:4], lam[:, 0:2], ACT.Exp).then_inc(act_set, 1)

            def bexp(u, g, n):
                kind, b = UNITS[u]
                if n == 0 and groups_before[u] + g >= 2:
                    u2, g2 = (u, g - 2) if g >= 2 else (prev(u), groups(UNITS[prev(u)][0]) + g - 2)
                    banks.await_full(act, ("o", u2, g2))
                what, s = b_items(kind, g)[n]
                i = banks.await_full(act, ("b", u, g, n))
                pr = P if what == "s" else TC - (kind == "x1")
                act.activation(PR[0:pr, p_slot(u, g, n), :], PS[0:pr, i, :], ACT.Exp).then_inc(banks.free[i], 1)

            def pv(u, g):
                if g == 0 and prev(u) is not None:
                    banks.await_full(act, last_t(prev(u)))
                i = banks.await_full(act, ("o", u, g))
                act.copy(OR[:, g, :], PS[:, i, 0:T]).then_inc(banks.free[i], 1)

            def ont(u):
                i = banks.await_full(act, ("ont", u))
                act.copy(OT[:, :, :], PS[:, i, 0:QT * P].rearrange("p (q t) -> p q t", t=P)).then_inc(banks.free[i], 1)

            def route(u):
                kind, b = UNITS[u]
                act.wait_ge(rt_in, f_units.index(u) + 1)
                if kind == "f0":
                    act.activation(gt[:, :, 1], gt[:, :, 0], ACT.Tanh, scale=0.5).then_inc(rt_exp, 1)
                else:
                    act.activation(le[:, :, :], lg[:, :, :], ACT.Exp, scale=-1.0).then_inc(rt_exp, 1)

            def ffn(u, e):
                kind, b = UNITS[u]
                ne = e_before[u] + e
                if kind == "f0":
                    i = banks.await_full(act, ("h", u, e))
                    if ne >= 2:
                        banks.await_full(act, ("y",) + flat_e[ne - 2])
                    act.activation(hs[ne % 2], PS[:, i, :], ACT.Gelu).then_inc(banks.free[i], 1)
                else:
                    i = banks.await_full(act, ("g", u, e))
                    if UNITS[flat_e[ne - 2][0]][0] == "f1":
                        banks.await_read(act, ("u",) + flat_e[ne - 2])
                    act.activation(sg[ne % 2], PS[:, i, :], ACT.Silu).then_inc(banks.free[i], 1)

            def mneg(u):
                n = HEADS[UNITS[u][0]]
                act.wait_ge(mp_ready, AU[u] + 1)
                if AU[u] < 2:
                    act.wait_ge(zeroed, 1)
                    act.wait_ge(cleared, 3)
                for p in range(MROWS):
                    act.dma_start(QS[SROWS + p:SROWS + p + 1, AU[u] % 2, 0:n, :], mp[0:n, p, :]).then_inc(m_in, 16)

            for step, u, a in order():
                if step == "mneg":
                    mneg(u)
                if step == "prep" and UNITS[u] == ("d1", 0):
                    setup_rest()
                if step in ("xt", "route"):
                    i = banks.await_full(act, ("xt", u))
                    act.copy(xT[:, UNITS[u][1], :], PS[:, i, 0:T]).then_inc(banks.free[i], 1)
                if step == "route":
                    route(u)
                if step == "bexp":
                    bexp(u, *a)
                elif step == "pv":
                    pv(u, a)
                elif step == "ont":
                    ont(u)
                elif step == "ffn":
                    ffn(u, a)

        @block.gpsimd
        def _(pool):
            nlink = [0]

            def link(ins):
                nlink[0] += 1
                ins.then_inc(p_chain, 1)
                pool.wait_ge(p_chain, nlink[0])

            link(pool.memset(ident[:, :], 0.0))
            link(pool.affine_select(out=ident[:, :], in_=ident[:, :], compare_op=ALU.not_equal, fill=1.0, base=0,
                                    pattern=[[-1, P]], channel_multiplier=1))
            link(pool.memset(flip[:, :], 0.0))
            link(pool.affine_select(out=flip[:, :], in_=flip[:, :], compare_op=ALU.not_equal, fill=1.0,
                                    base=1 - P, pattern=[[1, P]], channel_multiplier=1))
            link(pool.tensor_copy(identb[:, :], ident[:, :]))
            link(pool.iota(iota8[:, :], pattern=[[1, E]], base=0, channel_multiplier=0,
                           allow_small_or_imprecise_dtypes=True))
            link(pool.memset(ones3[:, :], 1.0))
            pool.memset(neghalf[:, :], -0.5).then_inc(consts, 1)
            pool.memset(QS[:, 0, :, :].bitcast(F32), 0.0).then_inc(zeroed, 1)

            def parts(u, src, dst, w, ready, done, sent):
                n = AU[u]
                pool.wait_ge(ready, n + 1)
                if n:
                    pool.wait_ge(sent, 16 * sent_dmas(prev(u)))
                x = src[:, 0:w]
                link(pool.tensor_copy(dst[:, 0, 0:w], x))
                link(pool.tensor_tensor(rf[:, 0:w], x, dst[:, 0, 0:w], ALU.subtract))
                link(pool.tensor_copy(dst[:, 1, 0:w], rf[:, 0:w]))
                pool.tensor_tensor(dst[:, 2, 0:w], rf[:, 0:w], dst[:, 1, 0:w], ALU.subtract).then_inc(done, 1)
                pool.wait_ge(done, n + 1)

            npow = [0]

            def power():
                npow[0] += 1
                pool.wait_ge(var_ready, npow[0])
                pool.tensor_tensor(rstd[:, :], ve[:, :], neghalf[:, :], ALU.pow).then_inc(rstd_ready, 1)

            for step, u, a in order():
                kind, b = UNITS[u]
                if step == "prep":
                    parts(u, qf, qp, widths[kind], q_ready, qp_ready, qp_out)
                    parts(u, kf, kp, kwidths[kind], k_ready, kp_ready, kp_out)
                elif step == "post" and kind == "x1" and a == turned(u) - 1 or step == "wo" and kind == "d1":
                    power()
                if step in ("wo", "ffn_end"):
                    power()

        @block.sync
        def _(sp):
            for dst, src in load_first:
                sp.dma_start(dst, src).then_inc(in_first, 16)
            off = T - 1 - TB // 2
            tb, ext = I["time_bias"].tensor, ext_d
            sp.dma_start(bass.AP(tensor=ext, offset=0, ap=[[1, off], [1, 1]]),
                         bass.AP(tensor=tb, offset=0, ap=[[0, off], [1, 1]])).then_inc(ext_done, 16)
            sp.dma_start(bass.AP(tensor=ext, offset=off, ap=[[1, 1], [1, TB]]),
                         bass.AP(tensor=tb, offset=0, ap=[[1, 1], [1, TB]])).then_inc(ext_done, 16)
            end = 2 * T - off - TB
            sp.dma_start(bass.AP(tensor=ext, offset=off + TB, ap=[[1, end], [1, 1]]),
                         bass.AP(tensor=tb, offset=TB - 1, ap=[[0, end], [1, 1]])).then_inc(ext_done, 16)
            sp.wait_ge(ext_done, 48)
            for qt in range(QT):
                sp.dma_start(win[:, qt, :], bass.AP(tensor=ext, offset=P - P * qt, ap=[[1, P], [1, T]])).then_inc(win_in, 16)
            for group, done in ((load_a0, in_a0), (load_cross, in_cross)):
                for dst, src in group:
                    sp.dma_start(dst, src).then_inc(done, 16)
            sp.wait_ge(zeroed, 1)
            sp.wait_ge(cleared, 1)

            def send(u, par, parts_sb, ready, out_sem, which, in_sem, tiles):
                sp.wait_ge(ready, AU[u] + 1)
                if AU[u] >= 2:
                    sp.wait_ge(in_sem, 16 * NPROD * (AU[u] - 1))
                d = scr[2 * par + which]
                for (t0, tn, row, col) in tiles:
                    for p in range(3):
                        sp.dma_start(d[p, row:row + P, col:col + tn], parts_sb[:, p, t0:t0 + tn]).then_inc(out_sem, 16)

            def stack(u, par, out_sem, dst, which, in_sem, n, c0):
                d = scr[2 * par + which]
                sp.wait_ge(out_sem, 16 * sent_dmas(u))
                for j, p in enumerate((QPART, KPART)[which]):
                    src = d[p, 0:n * HD, 0:c0].rearrange("(s d) t -> d s t", d=HD)
                    sp.dma_start(dst[j * HD:(j + 1) * HD], src).then_inc(in_sem, 16)

            for step, u, a in order():
                kind, b = UNITS[u]
                if step == "vprep" and u == 0:
                    for par in range(2):
                        sp.wait_ge(zeroed, 1)
                        sp.wait_ge(cleared, 3)
                        sp.dma_start(KS[SROWS:SROWS + MROWS, par, :].rearrange("p (n w) -> p n w", w=512),
                                     ones3[:, :].unsqueeze(1).to_broadcast([MROWS, 2 * H * T // 512, 512])).then_inc(ones_in, 16)
                    for dst, src in load_rest:
                        sp.dma_start(dst, src).then_inc(in_rest, 16)
                if step == "prep":
                    par, n = AU[u] % 2, HEADS[kind]
                    tiles = [(c * T, T, c * P, 0) for c in range(n // H)]
                    send(u, par, qp, qp_ready, qp_out, 0, qs_in, tiles)
                    if kind == "x0":
                        tiles = [(0, TC, 0, 0)]
                    elif kind == "x1":
                        tiles = [(0, TC + T, 0, 0)]
                    send(u, par, kp, kp_ready, kp_out, 1, ks_in, tiles)
                    if AU[u] >= 2:
                        banks.await_full(sp, last_b(prev(u, 2)))
                    stack(u, par, qp_out, QS[:, par, 0:n, :], 0, qs_in, n, T)
                    stack(u, par, kp_out, kstack(u), 1, ks_in, n, KEYS[kind])
                elif step == "post" and kind == "a0" and a == turned(u) - 1:
                    sp.wait_ge(on_ready, AU[u] + 1)
                    for qt in range(QT):
                        sp.dma_start(bass.AP(tensor=mix, offset=(b * T + qt * P) * HD, ap=[[HD, P], [B * T * HD, H], [1, HD]]),
                                     on[:, qt, :].rearrange("p (h d) -> p h d", d=HD)).then_inc(mix_out, 16)
                elif step == "ont" and kind == "a0":
                    sp.wait_ge(mix_out, 16 * QT * B)
                    if u:
                        banks.await_full(sp, ("ont", u - 1))
                    sp.dma_start(cm[:, :, :], bass.AP(tensor=mix, offset=u * T * D, ap=[[D, P], [P * D, QT], [1, D]])).then_inc(mix_in, 16)
                elif step == "ffn_end" and (kind == "f1" or b == B - 1):
                    sp.wait_ge(x_new, X_COUNT[u])
                    if kind == "f1":
                        sp.dma_start(out[b].rearrange("(t p) d -> p t d", p=P), X[:, b, :, :]).then_inc(stored, 16)
                    else:
                        for dst, src in late:
                            sp.dma_start(dst, src).then_inc(late_in, 16)
            sp.wait_ge(stored, 16 * B)

        @block.vector
        def _(dve):
            nlink = [0]

            def link(ins):
                nlink[0] += 1
                ins.then_inc(v_chain, 1)
                dve.wait_ge(v_chain, nlink[0])

            def parts(src, dst, tmp_, last=None):
                link(dve.tensor_copy(dst[0], src))
                link(dve.tensor_tensor(tmp_, src, dst[0], ALU.subtract))
                link(dve.tensor_copy(dst[1], tmp_))
                ins = dve.tensor_tensor(dst[2], tmp_, dst[1], ALU.subtract)
                if last is None:
                    link(ins)
                else:
                    ins.then_inc(last, 1)

            side = [iter(())]
            dve.memset(KS[:, 0, :].bitcast(F32), 0.0).then_inc(cleared, 1)
            dve.wait_ge(in_first, N_FIRST)

            def setup_bias():
                dve.memset(KS[:, 1, :].bitcast(F32), 0.0).then_inc(cleared, 1)
                dve.memset(QS[:, 1, :, :].bitcast(F32), 0.0).then_inc(cleared, 1)
                link(dve.memset(VX[:, :, :, :, :], 1.0))
                dve.wait_ge(act_set, 1)
                link(dve.tensor_scalar(lam[:, 6:7], lam[:, 4:5], 1.0, None, ALU.add))
                link(dve.reciprocal(lam[:, 6:7], lam[:, 6:7]))
                for key, raw, p3 in (("bn", bias_n, bias_np), ("bt", bias_t, bias_tp)):
                    i = banks.await_full(dve, key)
                    dve.tensor_scalar(raw[:, :], PS[:, i, :], lam[:, 6:7], gates[:, 1:2], ALU.mult, ALU.add).then_inc(banks.free[i], 1)
                    banks.await_read(dve, key)
                    parts(raw[:, :], [p3[:, p, :] for p in range(3)], vf[:, :], setup_v if key == "bt" else None)
                dve.wait_ge(setup_v, 1)

            def setup_cross():
                dve.wait_ge(in_cross, N_CROSS)
                i = banks.await_full(dve, "ctxT")
                dve.tensor_copy(ctxT[:, :, :], PS[:, i, 0:B * TC].rearrange("p (b t) -> p b t", t=TC)).then_inc(banks.free[i], 1)
                banks.await_read(dve, "ctxT")
                link(dve.tensor_copy(ctx0[:, :, :], ctxT[:, :, 0:1].to_broadcast([P, B, P])))
                dve.tensor_tensor(fs[:, :, :, :], fs[:, :, :, :], fm[:, :, :, :], ALU.add).then_inc(bias_sum, 1)
                dve.wait_ge(bias_sum, 1)
                for h in range(2):
                    i = banks.await_full(dve, ("ft", h))
                    dve.tensor_copy(fst[:, 2 * h:2 * h + 2, :], PS[0:TC, i, :].rearrange("p (b t) -> p b t", t=T)).then_inc(banks.free[i], 1)
                banks.await_read(dve, ("ft", 1))
                parts(fs[:, :, :, :].rearrange("p b q t -> p b (q t)"), [fsp[:, :, p, :] for p in range(3)],
                      vf[:, :].rearrange("p (b t) -> p b t", b=B))
                for h in range(2):
                    parts(fst[:, 2 * h:2 * h + 2, :], [fstp[:, 2 * h:2 * h + 2, p, :] for p in range(3)],
                          vf[0:TC, :].rearrange("p (b t) -> p b t", t=T), setup_v if h else None)
                dve.wait_ge(setup_v, 2)

            def setup_rest():
                dve.wait_ge(in_rest, N_REST)
                link(dve.tensor_tensor(lam4[:, 0, :], lam4[:, 0, :], lam4[:, 1, :], ALU.mult))
                link(dve.tensor_tensor(lam4[:, 2, :], lam4[:, 2, :], lam4[:, 3, :], ALU.mult))
                dve.tensor_reduce(lam[:, 0:2], lam4[:, 0:4:2, :], AX.X, ALU.add).then_inc(lam_sums, 1)
                dve.wait_ge(act_set, 3)
                link(dve.tensor_scalar(lam[:, 5:6], lam[:, 3:4], -LAMBDA_INIT, None, ALU.add))
                link(dve.tensor_tensor(lam[:, 5:6], lam[:, 5:6], lam[:, 2:3], ALU.subtract))

            def prep(u):
                kind, b = UNITS[u]
                par, n = AU[u] % 2, AU[u]
                for which, dst, w, ready, taken in (("q", qf, widths[kind], q_ready, qp_ready),
                                                    ("k", kf, kwidths[kind], k_ready, kp_ready)):
                    i = banks.await_full(dve, (which, u))
                    if n:
                        dve.wait_ge(taken, n)
                    bias = cols[kind + "_" + which][:, 0:1] if kind in ("a0", "x0") else 0.0
                    dve.tensor_scalar(dst[:, 0:w], PS[:, i, 0:w], bias, SCALE if which == "q" else 1.0,
                                      ALU.add, ALU.mult).then_inc(ready, 1)
                    dve.wait_ge(ready, n + 1)
                    dve.sem_inc(banks.free[i], 1)

            def vprep(u):
                kind, b = UNITS[u]
                par, n = AU[u] % 2, AU[u]
                i = banks.await_full(dve, ("v", u))
                if n >= 2:
                    u2 = prev(u, 2)
                    banks.await_full(dve, ("o", u2, groups(UNITS[u2][0]) - 1))

                def to_vx(rows_, kt, c):
                    o = VX[0:rows_, par, kt, :, 0:HD]
                    src = PS[0:rows_, i, c * D:(c + 1) * D].rearrange("p (h d) -> p h d", d=HD)
                    if kind in ("a0", "x0"):
                        return dve.tensor_tensor(o, src, rows[kind + "_v"][0:rows_, :].rearrange("p (h d) -> p h d", d=HD),
                                                 ALU.add)
                    return dve.tensor_copy(o, src)
                if kind == "x0":
                    last = to_vx(TC, 2, 0)
                else:
                    for kt in range(QT):
                        last = to_vx(P, kt, kt)
                if kind == "x1":
                    to_vx(TC - 1, 2, 2)
                    last = dve.tensor_tensor(v0[:, b, :].rearrange("p (h d) -> p h d", d=HD),
                                             PS[:, i, 3 * D:4 * D].rearrange("p (h d) -> p h d", d=HD),
                                             gate_t[:, :].unsqueeze(2).to_broadcast([P, H, HD]), ALU.mult)
                last.then_inc(banks.free[i], 1)

            def amax(u, lo, hi):
                kind, b = UNITS[u]
                items = a_items(kind)
                if lo == 0 and hi and AU[u]:
                    banks.await_full(dve, ("m", prev(u)))
                for it in range(lo, hi):
                    s, qt = items[it]
                    i = banks.await_full(dve, ("a", u, it))
                    if kind == "x1":
                        o, src = mx[:, qt, s:s + 1], PS[:, i, 0:TC + T - 1]
                    elif kind == "x0":
                        o = mx[:, :, G4 * s:G4 * s + G4].rearrange("p q s -> p s q")
                        src = PS[:, i, :].rearrange("p (s q t) -> p s q t", q=QT, t=TC)
                    else:
                        o, src = mx[:, :, s], PS[:, i, :].rearrange("p (q t) -> p q t", t=T)
                    dve.tensor_reduce(o, src, AX.X, ALU.max).then_inc(banks.free[i], 1)
                    for _ in range(2):
                        next(side[0], None)

            def mneg(u):
                n = HEADS[UNITS[u][0]]
                i = banks.await_full(dve, ("m", u))
                if AU[u]:
                    dve.wait_ge(m_in, 16 * MROWS * AU[u])
                dve.tensor_scalar(mf[0:n, :], PS[0:n, i, 0:T], -1.0, TOP, ALU.mult, ALU.add).then_inc(banks.free[i], 1)
                banks.await_read(dve, ("m", u))
                parts(mf[0:n, :], [mp[0:n, p, :] for p in range(3)], mr[0:n, :], mp_ready)
                dve.wait_ge(mp_ready, AU[u] + 1)

            nvar = [0]

            def hold(ins):
                nlink[0] += 1
                n = nlink[0]
                ins.then_inc(v_chain, 1)
                yield
                dve.wait_ge(v_chain, n)

            def norm(src, dst, gain=None, offset=None, done=None, add=None):
                for qt in range(QT):
                    yield from hold(dve.bn_stats(st[:, :], src[qt]))
                    yield from hold(dve.bn_aggr(mv[:, qt, :], st[:, :]))
                nvar[0] += 1
                dve.tensor_scalar(ve[:, :], mv[:, :, 1], EPS, None, ALU.add).then_inc(var_ready, 1)
                n = nvar[0]
                yield
                yield
                dve.wait_ge(rstd_ready, n)
                for qt in range(QT):
                    ins = dve.tensor_scalar(dst[qt], src[qt], mv[:, qt, 0:1], rstd[:, qt:qt + 1], ALU.subtract, ALU.mult)
                    if gain is not None:
                        yield from hold(ins)
                        yield from hold(dve.tensor_tensor(dst[qt], dst[qt], gain, ALU.mult))
                        ins = dve.tensor_tensor(dst[qt], dst[qt], offset, ALU.add)
                    if qt == QT - 1 and done is not None:
                        ins.then_inc(done, 1)
                    else:
                        yield from hold(ins)

            def post(u, k):
                kind, b = UNITS[u]
                gs = groups(kind)
                if k == 0 and AU[u] and kind == "a0":
                    dve.wait_ge(mix_out, 16 * QT * AU[u])
                elif k == 0 and kind != "a0":
                    banks.await_full(dve, ("ont", prev(u)))
                qt, half = divmod(k, gs // 4)
                key = ("t", u, qt, half)
                i = banks.await_full(dve, key)
                t = PS[:, i, :].rearrange("p (s w) -> p s w", w=STRIP)
                yield from hold(dve.reciprocal(rs[:, :], t[:, :, HD]))
                if kind == "d1":
                    yield from hold(dve.tensor_scalar(rs[:, 1:H:2], rs[:, 1:H:2], lam[:, 5:6], None, ALU.mult))
                    o = tmp[:, :, :]
                else:
                    o = on[:, qt, :].rearrange("p (h d) -> p h d", d=HD)
                dve.tensor_tensor(o, t[:, :, 0:HD], rs[:, :].unsqueeze(2).to_broadcast([P, H, HD]),
                                  ALU.mult).then_inc(banks.free[i], 1)
                yield
                banks.await_read(dve, key)
                if kind == "d1":
                    yield from hold(dve.tensor_tensor(on[:, qt, half * D // 2:(half + 1) * D // 2].rearrange("p (h d) -> p h d", d=HD),
                                           tmp[:, 0:H:2, :], tmp[:, 1:H:2, :], ALU.add))
                if k < turned(u) - 1:
                    return
                if kind == "x1":
                    for qt in range(QT):
                        yield from hold(dve.tensor_tensor(onb[:, qt, :], on[:, qt, :], v0[:, b, :], ALU.add))
                    yield from norm([onb[:, qt, :] for qt in range(QT)], [on[:, qt, :] for qt in range(QT)],
                         rows["x1_g"][:, :], rows["x1_b"][:, :], on_ready)
                    yield
                    dve.wait_ge(on_ready, AU[u] + 1)
                else:
                    dve.sem_inc(on_ready, 1)

            def finish(u):
                kind, b = UNITS[u]
                i = banks.await_full(dve, ("wo", u))
                x = X[:, b, :, :]
                ps = PS[:, i, 0:QT * D].rearrange("p (q d) -> p q d", d=D)
                yq = [y[:, qt, :] for qt in range(QT)]
                xq = [x[:, qt, :] for qt in range(QT)]
                if kind == "d1":
                    dve.tensor_copy(y[:, :, :], ps).then_inc(banks.free[i], 1)
                    yield
                    banks.await_read(dve, ("wo", u))
                    yield from norm(yq, yq, rows["d1_g"][:, :], rows["d1_b"][:, :])
                    yield from hold(dve.tensor_tensor(y[:, :, :], y[:, :, :], x, ALU.add))
                else:
                    dve.tensor_tensor(y[:, :, :], ps, x, ALU.add).then_inc(banks.free[i], 1)
                    yield
                    banks.await_read(dve, ("wo", u))
                    yield from hold(dve.tensor_tensor(y[:, :, :], y[:, :, :],
                                           rows[kind + "_o"][:, :].unsqueeze(1).to_broadcast([P, QT, D]), ALU.add))
                yield from norm(yq, xq, done=x_new)
                yield
                dve.wait_ge(x_new, X_COUNT[u])

            def route(u):
                kind, b = UNITS[u]
                nf = f_units.index(u)
                i = banks.await_full(dve, ("r", u))
                ps = PS[:, i, 0:QT * E].rearrange("p (q e) -> p q e", e=E)
                if kind == "f0":
                    dve.tensor_copy(lg[:, :, :], ps).then_inc(banks.free[i], 1)
                    banks.await_read(dve, ("r", u))
                else:
                    dve.tensor_tensor(lg[:, :, :], ps, rbias[:, :].unsqueeze(1).to_broadcast([P, QT, E]),
                                      ALU.add).then_inc(rt_in, 1)
                    dve.wait_ge(rt_in, nf + 1)
                    dve.sem_inc(banks.free[i], 1)
                    dve.wait_ge(rt_exp, nf + 1)
                    link(dve.tensor_scalar(le[:, :, :], le[:, :, :], 1.0, None, ALU.add))
                    link(dve.reciprocal(lg[:, :, :], le[:, :, :]))
                for qt in range(QT):
                    link(dve.max(top[:, qt, :], lg[:, qt, :]))
                    link(dve.max_index(topi[:, qt, :], top[:, qt, :], lg[:, qt, :]))
                link(dve.tensor_copy(topf[:, :, 0:2], topi[:, :, 0:2]))
                if kind == "f0":
                    dve.tensor_tensor(gt[:, :, 0], top[:, :, 0], top[:, :, 1], ALU.subtract).then_inc(rt_in, 1)
                    dve.wait_ge(rt_exp, nf + 1)
                    link(dve.tensor_scalar(gt[:, :, 2], gt[:, :, 1], 0.5, 0.5, ALU.mult, ALU.add))
                    link(dve.tensor_scalar(gt[:, :, 3], gt[:, :, 1], -0.5, 0.5, ALU.mult, ALU.add))
                else:
                    link(dve.tensor_tensor(gt[:, :, 0], top[:, :, 0], top[:, :, 1], ALU.add))
                    link(dve.reciprocal(gt[:, :, 1], gt[:, :, 0]))
                    link(dve.tensor_tensor(gt[:, :, 2], top[:, :, 0], gt[:, :, 1], ALU.mult))
                    link(dve.tensor_tensor(gt[:, :, 3], top[:, :, 1], gt[:, :, 1], ALU.mult))
                for qt in range(QT):
                    link(dve.tensor_scalar(gate[:, b, qt, :], iota8[:, :], topf[:, qt, 0:1], gt[:, qt, 2:3], ALU.is_equal, ALU.mult))
                    link(dve.tensor_scalar(le[:, qt, :], iota8[:, :], topf[:, qt, 1:2], gt[:, qt, 3:4], ALU.is_equal, ALU.mult))
                    link(dve.tensor_tensor(gate[:, b, qt, :], gate[:, b, qt, :], le[:, qt, :], ALU.add))

            def add_expert(u, e):
                kind, b = UNITS[u]
                i = banks.await_full(dve, ("y", u, e))
                for qt in range(QT):
                    ps, a_ = PS[:, i, qt * D:(qt + 1) * D], acc[:, qt, :]
                    if e == 0:
                        ins = dve.tensor_scalar(a_, ps, gate[:, b, qt, 0:1], None, ALU.mult)
                    elif e < E:
                        ins = dve.scalar_tensor_tensor(out=a_, in0=ps, scalar=gate[:, b, qt, e:e + 1], in1=a_,
                                                       op0=ALU.mult, op1=ALU.add)
                    else:
                        ins = dve.tensor_tensor(a_, ps, a_, ALU.add)
                ins.then_inc(banks.free[i], 1)
                banks.await_read(dve, ("y", u, e))

            def ffn(u, e):
                if UNITS[u][0] == "f1":
                    ne = e_before[u] + e
                    i = banks.await_full(dve, ("u", u, e))
                    banks.await_read(dve, ("g", u, e))
                    banks.await_full(dve, ("y",) + flat_e[ne - 2])
                    dve.tensor_tensor(hs[ne % 2], PS[:, i, :], sg[ne % 2], ALU.mult).then_inc(banks.free[i], 1)
                if e:
                    add_expert(u, e - 1)

            def ffn_end(u):
                kind, b = UNITS[u]
                add_expert(u, EXPERTS[kind] - 1)
                link(dve.tensor_tensor(y[:, :, :], acc[:, :, :], X[:, b, :, :], ALU.add))
                for _ in norm([y[:, qt, :] for qt in range(QT)], [X[:, b, qt, :] for qt in range(QT)], done=x_new):
                    pass
                dve.wait_ge(x_new, X_COUNT[u])

            for step, u, a in order():
                if step not in ("amax", "bexp", "pv", "ffn"):
                    for _ in side[0]:
                        pass
                if step == "prep" and UNITS[u] == ("d1", 0):
                    setup_rest()
                if step == "setup_bias":
                    setup_bias()
                elif step == "setup_cross":
                    setup_cross()
                elif step == "route":
                    route(u)
                elif step == "prep":
                    prep(u)
                elif step == "vprep":
                    vprep(u)
                elif step == "amax":
                    amax(u, *part_of(u, a))
                elif step == "mneg":
                    mneg(u)
                elif step == "post":
                    side[0] = post(u, a)
                elif step == "wo":
                    side[0] = finish(u)
                elif step == "ffn":
                    ffn(u, a)
                    for _ in range(2):
                        next(side[0], None)
                elif step == "ffn_end":
                    ffn_end(u)


def kernel(**inputs):
    import numpy as np
    import concourse.bacc as bacc
    from concourse.bass_utils import run_bass_kernel_spmd as run

    g = {k: np.asarray(v) for k, v in inputs.items()}
    t = np.transpose
    a = {
        "x": g["x"], "ctx_1024": g["ctx_1024"], "fside_BxSxS2_0": g["fside_BxSxS2_0"],
        "mask_BxSxS2_ff0": g["mask_BxSxS2_ff0"],
        "w_a0_q": g["L0_attn_Wq"].T, "w_a0_k": g["L0_attn_Wk"].T, "w_a0_v": g["L0_attn_Wv"].T,
        "w_a0_o": g["L0_attn_Wo"].T, "w_x0_q": g["L0_xattn_Wq"], "w_x0_k": g["L0_xattn_Wk"],
        "w_x0_v": g["L0_xattn_Wv"], "w_x0_o": g["L0_xattn_Wo"], "w_d1_q": g["L1_attn_Wq"],
        "w_d1_k": g["L1_attn_Wk"], "w_d1_v": g["L1_attn_Wv"], "w_d1_o": g["L1_attn_Wo"],
        "w_x1_q": g["L1_xattn_Wq"].T, "w_x1_k": g["L1_xattn_Wk"].T, "w_x1_v": g["L1_xattn_Wv"].T,
        "w_x1_o": g["L1_xattn_Wp"].T, "w_f0_r": g["L0_ffn_router_w"].T, "w_f1_r": g["L1_ffn_router_w"].T,
        "c_a0_q": g["L0_attn_bq"].reshape(D, 1), "c_a0_k": g["L0_attn_bk"].reshape(D, 1),
        "c_x0_q": g["L0_xattn_bq"].reshape(D, 1), "c_x0_k": g["L0_xattn_bk"].reshape(D, 1),
        "r_a0_v": g["L0_attn_bv"], "r_a0_o": g["L0_attn_bo"], "r_x0_v": g["L0_xattn_bv"], "r_x0_o": g["L0_xattn_bo"],
        "r_d1_g": g["L1_attn_gamma"], "r_d1_b": g["L1_attn_beta"], "r_x1_g": g["L1_xattn_ln_g"],
        "r_x1_b": g["L1_xattn_ln_b"], "r_x1_o": g["L1_xattn_bp"], "rbias": g["L1_ffn_routing_bias"],
        "gate": g["L1_xattn_gate"].reshape(H), "et_gate": g["L0_attn_et_gate"].reshape(1),
        "is_gate": g["L0_attn_is_gate"].reshape(1), "time_bias": g["L0_attn_time_bias"].reshape(1, TB),
        "lq1": g["L1_attn_lambda_q1"], "lk1": g["L1_attn_lambda_k1"], "lq2": g["L1_attn_lambda_q2"],
        "lk2": g["L1_attn_lambda_k2"], "w1": t(g["L0_ffn_w1"], (0, 2, 1)), "w2": t(g["L0_ffn_w2"], (0, 2, 1)),
        "wg": t(g["L1_ffn_wg"], (0, 2, 1)), "wu": t(g["L1_ffn_wu"], (0, 2, 1)), "wd": t(g["L1_ffn_wd"], (0, 2, 1)),
        "sg": g["L1_ffn_sg_w"].T, "su": g["L1_ffn_su_w"].T, "sd": g["L1_ffn_sd_w"].T,
    }
    nc = bacc.Bacc("TRN2", target_bir_lowering=False, num_devices=1)
    arrays, I = {}, {}
    for name, v in a.items():
        v = np.ascontiguousarray(v)
        arrays["in_" + name] = v
        I[name] = nc.dram_tensor("in_" + name, v.shape, mybir.dt.from_np(v.dtype), kind="ExternalInput").ap()
    out = nc.dram_tensor("out_0", (B, T, D), F32, kind="ExternalOutput").ap()
    decoder(nc, I, out)
    r = run(nc, [arrays], core_ids=[0])
    return r.results[0]["out_0"]
```

```python
from contextlib import ExitStack

import concourse.bass as bass
from concourse import mybir

F32 = mybir.dt.float32
BF16 = mybir.dt.bfloat16
U32 = mybir.dt.uint32
ACT = mybir.ActivationFunctionType
ALU = mybir.AluOpType
AX = mybir.AxisListType

P = 128
B, T, D = 4, 256, 128
TC = 64
H, HD = 16, 8
QT = T // P
E, HID = 8, 256
HH = HID // P
STRIP = 32
G4 = P // STRIP
NPROD = 6
KPART = (0, 0, 1, 0, 2, 1)
QPART = (0, 1, 0, 2, 0, 1)
SROWS = NPROD * HD
MROWS = 3
SCALE = float(HD) ** -0.5
EXPERTS = {"f0": E, "f1": E + 1}
LAMBDA_INIT = 0.8 - 0.6 * 2.718281828459045 ** (-0.3 * 11)
EPS = 1e-5
TB = 500
TOP = -1.0
LOWEST = -3.4e38

KINDS = ("a0", "x0", "f0", "d1", "x1", "f1")
UNITS = [(kind, b) for kind in KINDS for b in range(B)]
HEADS = {"a0": H, "x0": H, "d1": 2 * H, "x1": H}
KEYS = {"a0": T, "x0": TC, "d1": T, "x1": TC + T}
ATT = [u for u, (k, _) in enumerate(UNITS) if k[0] != "f"]
ORDER_A = {u: n for n, u in enumerate(ATT)}


def a_items(kind):
    if kind == "x0":
        return [(g, 0) for g in range(H // G4)]
    if kind == "x1":
        return [(s, qt) for s in range(H) for qt in range(QT)]
    return [(s, 0) for s in range(HEADS[kind])]


def b_items(kind, g):
    s0 = G4 * g
    if kind == "x0":
        return [("c", s0), ("c", s0 + 2)]
    if kind == "x1":
        return [("c", s0), ("c", s0 + 2)] + [("s", s0 + j) for j in range(G4)]
    return [("s", s0 + j) for j in range(G4)]


def groups(kind):
    return HEADS[kind] // G4


def turned(u):
    return QT * groups(UNITS[u][0]) // 4


AT_ONT, AT_WO, AT_XT, AT_PREP = 5, 6, 8, 8
A_FROM, A_TO = 3 / 16, 7 / 8


def expert_steps(u):
    return [("route", u, 0)] + [("ffn", u, e) for e in range(EXPERTS[UNITS[u][0]])] + [("ffn_end", u, 0)]


def start(u):
    return [("xt", u, 0), ("qprep", u, 0), ("kprep", u, 0), ("qstack", u, 0), ("kstack", u, 0)]


def order():
    first = [u for u in ATT if UNITS[u][0] == "a0"]
    rest = [u for u in ATT if UNITS[u][0] != "a0"]
    yield from start(0)
    yield "setup_bias", 0, 0
    yield from start(1)
    yield "amax", 0, (0, 1)
    yield "mneg", 0, 0
    yield "vprep", 0, 0
    yield "vprep", 1, 0
    yield from chain(first)
    v0, v1 = rest[:2]
    yield "kprep", v1, 0
    for k in range(turned(first[-1])):
        yield "post", first[-1], k
    for n, u in enumerate(first):
        yield "ont", u, 0
        if n == 0:
            yield "kstack", v1, 0
        yield "wo", u, 0
        if n < 2:
            yield "xt", rest[n], 0
            yield "qprep", rest[n], 0
            yield "qstack", rest[n], 0
    yield "vprep", v0, 0
    yield "vprep", v1, 0
    yield "amax", v0, (0, 1)
    yield "mneg", v0, 0
    yield from chain(rest)
    for k in range(turned(rest[-1])):
        yield "post", rest[-1], k
    yield "ont", rest[-1], 0
    yield "wo", rest[-1], 0
    for step in expert_steps(rest[-1] + B):
        yield step


def chain(us):
    for n, u in enumerate(us):
        kind = UNITS[u][0]
        G = groups(kind)
        more, mixed = n + 1 < len(us), kind == "a0"
        items = [(g, i) for g in range(G) for i in range(len(b_items(kind, g)))]
        N = len(items)
        also = {}
        if n:
            for k in range(turned(us[n - 1])):
                also.setdefault(1 + k, []).append(("post", us[n - 1], k))
            if not mixed:
                also.setdefault(AT_ONT * N // 16, []).append(("ont", us[n - 1], 0))
                also.setdefault(AT_WO * N // 16, []).append(("wo", us[n - 1], 0))
        if n + 2 < len(us):
            for step, at in (("xt", AT_XT), ("qprep", AT_PREP), ("kprep", AT_PREP)):
                also.setdefault(at * N // 16, []).append((step, us[n + 2], 0))
        if mixed and n == 2:
            also.setdefault(N // 2, []).append(("setup_cross", 0, 0))
        if mixed and n == 3:
            also.setdefault(N // 2, []).extend([("kprep", B, 0), ("kstack", B, 0)])
        lo, hi = int(N * A_FROM), int(N * A_TO)
        for k, (g, i) in enumerate(items):
            yield "bexp", u, (g, i)
            if more and lo <= k < hi:
                yield "amax", us[n + 1], (k - lo, hi - lo)
            if i == 1 and g:
                yield "pv", u, g - 1
            yield from also.get(k, ())
            if more and k == min(hi, N - 1):
                yield "mneg", us[n + 1], 0
        yield "pv", u, G - 1
        if n + 2 < len(us):
            yield "qstack", us[n + 2], 0
            yield "kstack", us[n + 2], 0
        if n and UNITS[us[n - 1]][0] in ("x0", "x1"):
            yield from expert_steps(us[n - 1] + B)
        if n + 2 < len(us):
            yield "vprep", us[n + 2], 0


X_COUNT = {u: n + 1 for n, u in enumerate(u for step, u, _ in order() if step in ("wo", "ffn_end"))}


def part_of(u, part):
    n, m = part
    items = len(a_items(UNITS[u][0]))
    return items * n // m, items * (n + 1) // m


class Banks:

    def __init__(self, ctx, nc):
        self.full = [ctx.enter_context(nc.semaphore(f"bank{i}_full")) for i in range(8)]
        self.free = [ctx.enter_context(nc.semaphore(f"bank{i}_free")) for i in range(8)]
        self.uses = [0] * 8
        self.place = {}
        self.turn = {}

    def take(self, pe, key, pool):
        t = self.turn.get(pool, 0)
        self.turn[pool] = t + 1
        i = pool[t % len(pool)]
        n = self.uses[i]
        self.uses[i] = n + 1
        self.place[key] = (i, n)
        if n:
            pe.wait_ge(self.free[i], n)
        return i

    def await_full(self, eng, key):
        i, n = self.place[key]
        eng.wait_ge(self.full[i], n + 1)
        return i

    def await_read(self, eng, key):
        i, n = self.place[key]
        eng.wait_ge(self.free[i], n + 1)


POOL_A = POOL_B = (0, 1, 2, 3, 4)
POOL_O = POOL_M = (5, 6, 7)


def decoder(nc, I, out):
    with ExitStack() as ctx:
        def sb(name, shape, dt=F32):
            return ctx.enter_context(nc.sbuf_tensor(name, shape, dt))

        def sem(name):
            return ctx.enter_context(nc.semaphore(name))

        banks = Banks(ctx, nc)
        PS = ctx.enter_context(nc.psum_tensor("PS", [P, 8, 512], F32))
        scr = nc.dram_tensor("parts_scratch", (4, 3, 2 * P, TC + T), BF16).ap()
        mix = nc.dram_tensor("mix_scratch", (H, B, T, HD), F32)
        ext_d = nc.dram_tensor("bias_scratch", (1, 512), F32)

        X = sb("X", [P, B, QT, D])
        C = sb("C", [TC, B, D])
        ctxT = sb("ctxT", [P, B, TC])
        ident = sb("ident", [P, P])
        identb = sb("identb", [P, P], BF16)
        flip = sb("flip", [P, P])
        W = {}
        for n, w in (("a0_q", D), ("a0_k", D), ("a0_v", D), ("a0_o", D), ("x0_q", D), ("x0_k", D), ("x0_v", D),
                     ("x0_o", D), ("d1_q", 2 * D), ("d1_k", 2 * D), ("d1_v", D), ("d1_o", D), ("x1_q", D),
                     ("x1_k", D), ("x1_v", D), ("x1_o", D), ("f0_r", E), ("f1_r", E)):
            W[n] = sb("w_" + n, [P, w])
        FW = sb("FW", [P, 2 * (E + 1) * HID])
        w1 = FW[:, 0:E * HID].rearrange("p (e i) -> p e i", i=HID)
        w2 = FW[:, E * HID:2 * E * HID].rearrange("p (e t d) -> p e t d", t=HH, d=D)
        wg = FW[:, 0:(E + 1) * HID].rearrange("p (e i) -> p e i", i=HID)
        wu = FW[:, (E + 1) * HID:2 * (E + 1) * HID].rearrange("p (e i) -> p e i", i=HID)
        wd = sb("wd", [P, E + 1, HH, D])
        cols = {n: sb("c_" + n, [P, 1]) for n in ("a0_q", "a0_k", "x0_q", "x0_k")}
        rows = {n: sb("r_" + n, [P, D]) for n in ("a0_v", "a0_o", "x0_v", "x0_o", "d1_g", "d1_b", "x1_g",
                                                   "x1_b", "x1_o")}
        rbias = sb("rbias", [P, E])
        gate_t = sb("gate_t", [P, H])
        gates = sb("gates", [P, 2])
        lam4 = sb("lam4", [P, 4, HD])
        lam = sb("lam", [P, 8])
        neghalf = sb("neghalf", [P, 2])
        iota8 = sb("iota8", [P, E])
        ones3 = sb("ones3", [MROWS, 512], BF16)

        PR = sb("PR", [P, 12, 512])
        win = PR[:, 0, :].rearrange("p (q t) -> p q t", t=T)
        bias_t = PR[:, 2, :]
        cm = PR[:, 0:2, :].rearrange("p x (n d) -> p (x n) d", d=D)
        fs = PR[:, 4, :].rearrange("p (b q t) -> p b q t", b=B, t=TC)
        fm = PR[:, 5, :].rearrange("p (b q t) -> p b q t", b=B, t=TC)
        fst = PR[0:TC, 10:12, :].rearrange("p x (b t) -> p (x b) t", t=T)
        hid = [sb(f"hid{i}", [P, 3 * QT * T // 2]) for i in range(2)]
        bias_n = hid[0][:, 0:QT * T]
        bias_tp = hid[1][:, :].bitcast(BF16).rearrange("p (c t) -> p c t", c=3)
        sig = sb("sig", [P, 3 * B * QT * TC // 2])
        fsp = sig[:, :].bitcast(BF16).rearrange("p (b c t) -> p b c t", b=B, c=3)
        fstp = sb("fstp", [TC, B, 3, T], BF16)

        xT = sb("xT", [P, B, T])
        ctx0 = sb("ctx0", [P, B, P])
        qf = sb("qf", [P, 2 * T])
        kf = sb("kf", [P, 2 * T])
        vf = sb("vf", [P, 2 * T])
        hs = [h[:, 0:HH * T] for h in hid]
        sg = [sig[:, 0:HH * T], vf[:, :]]
        qp = sb("qp", [P, 3, 2 * T], BF16)
        kp = sb("kp", [P, 3, 2 * T], BF16)
        QS = sb("QS", [P, 2, 2 * H, T], BF16)
        KS = sb("KS", [P, 2, 2 * H * T], BF16)
        VX = sb("VX", [P, 2, 3, H, STRIP])
        v0 = sb("v0", [P, B, D])
        mx = sb("mx", [P, 2, 2 * H])
        mf = sb("mf", [2 * H, T])
        mr = sb("mr", [2 * H, T])
        mp = sb("mp", [2 * H, 3, T], BF16)
        OR = sb("OR", [P, 8, T])
        on = sb("on", [P, QT, D])
        onb = sb("onb", [P, QT, D], BF16)
        tmp = sb("tmp", [P, H, HD])
        rs = sb("rs", [P, H])
        OT = sb("OT", [P, QT, P])
        y = sb("y", [P, QT, D])
        st = sb("st", [P, QT, 6])
        mv = sb("mv", [P, QT, 2])
        ve = sb("ve", [P, QT])
        rstd = sb("rstd", [P, QT])
        acc = sb("acc", [P, QT, D])
        lg = sb("lg", [P, QT, E])
        le = sb("le", [P, QT, E])
        top = sb("top", [P, QT, 8])
        topi = sb("topi", [P, QT, 8], U32)
        topf = sb("topf", [P, QT, 8])
        gt = sb("gt", [P, QT, 8])
        gate = sb("gate", [P, B, QT, E])

        in_first = sem("in_first")
        in_a0 = sem("in_a0")
        in_cross = sem("in_cross")
        in_rest = sem("in_rest")
        late_in = sem("late_in")
        ext_done = sem("ext_done")
        win_in = sem("win_in")
        consts = sem("consts")
        zeroed = sem("zeroed")
        cleared = sem("cleared")
        ones_in = sem("ones_in")
        bias_sum = sem("bias_sum")
        setup_v = sem("setup_v")
        lam_sums = sem("lam_sums")
        act_set = sem("act_set")
        v_chain = sem("v_chain")
        p_chain = sem("p_chain")
        x_new = sem("x_new")
        k_ready = sem("k_ready")
        qp_ready = sem("qp_ready")
        kp_ready = sem("kp_ready")
        qp_out = sem("qp_out")
        kp_out = sem("kp_out")
        qs_in = [sem(f"qs{i}_in") for i in range(2)]
        ks_in = [sem(f"ks{i}_in") for i in range(2)]
        mp_ready = sem("mp_ready")
        m_in = sem("m_in")
        on_ready = sem("on_ready")
        mix_out = sem("mix_out")
        mix_in = sem("mix_in")
        var_ready = sem("var_ready")
        rstd_ready = sem("rstd_ready")
        rt_in = sem("rt_in")
        rt_exp = sem("rt_exp")
        stored = sem("stored")

        ks_view = [KS[:, par, :] for par in range(2)]

        def kstack(u):
            kind, _ = UNITS[u]
            n = KEYS[kind]
            return ks_view[ORDER_A[u] % 2][:, 0:HEADS[kind] * n].rearrange("p (s t) -> p s t", t=n)

        AU = ORDER_A
        groups_before = {}
        gsum = 0
        for u in ATT:
            groups_before[u] = gsum
            gsum += groups(UNITS[u][0])

        def p_slot(u, g, i):
            return ((groups_before[u] + g) % 2) * 6 + i

        f_units = [u for u, (k, _) in enumerate(UNITS) if k[0] == "f"]
        e_before, n = {}, 0
        for u in f_units:
            e_before[u] = n
            n += EXPERTS[UNITS[u][0]]
        flat_e = [(u, e) for u in f_units for e in range(EXPERTS[UNITS[u][0]])]
        widths = {"a0": T, "x0": T, "d1": 2 * T, "x1": T}
        kwidths = {"a0": T, "x0": TC, "d1": 2 * T, "x1": TC + T}

        def rows_in(u):
            return 16 * NPROD * (AU[u] // 2 + 1)

        def last_b(u):
            g = groups(UNITS[u][0]) - 1
            return ("b", u, g, len(b_items(UNITS[u][0], g)) - 1)

        def prev(u, k=1):
            return ATT[AU[u] - k] if AU[u] >= k else None

        def sent_dmas(u):
            return sum(3 * (HEADS[UNITS[v][0]] // H) for v in ATT if v <= u)

        def last_t(u):
            return ("t", u, QT - 1, groups(UNITS[u][0]) // 4 - 1)

        block = ctx.enter_context(nc.Block())
        def weight(*names):
            return [(W[n][:, :], I["w_" + n]) for n in names]

        def column(*names):
            return [(cols[n][:, :], I["c_" + n]) for n in names]

        def row(*names):
            return [(rows[n][:, :], I["r_" + n].partition_broadcast(P)) for n in names]

        load_first = [(X[:, :, :, :], I["x"].rearrange("b (t p) d -> p b t d", p=P))] + \
            weight("a0_q", "a0_k") + column("a0_q", "a0_k") + \
            [(gates[:, 0:1], I["et_gate"].partition_broadcast(P)), (gates[:, 1:2], I["is_gate"].partition_broadcast(P))]
        load_a0 = weight("a0_v", "a0_o") + row("a0_v", "a0_o")
        load_cross = [
            (C[:, :, :], I["ctx_1024"].rearrange("b t d -> t b d")),
            (fs[:, :, :, :], I["fside_BxSxS2_0"].rearrange("b (t p) k -> p b t k", p=P)),
            (fm[:, :, :, :], I["mask_BxSxS2_ff0"].rearrange("b (t p) k -> p b t k", p=P)),
        ] + weight("x0_q", "x0_k", "x0_v", "x0_o") + column("x0_q", "x0_k") + row("x0_v", "x0_o")
        load_rest = weight("f0_r") + [(w1[:, :, :], I["w1"].rearrange("e h i -> h e i")),
                                      (w2[:, :, :, :], I["w2"].rearrange("e (t p) d -> p e t d", p=P))]
        load_rest += weight("d1_q", "d1_k", "d1_v", "d1_o", "x1_q", "x1_k", "x1_v", "x1_o", "f1_r")
        load_rest += row("d1_g", "d1_b", "x1_g", "x1_b", "x1_o")
        load_rest += [(rbias[:, :], I["rbias"].partition_broadcast(P)), (gate_t[:, :], I["gate"].partition_broadcast(P))]
        load_rest += [(lam4[:, i, :], I[n].partition_broadcast(P)) for i, n in enumerate(("lq1", "lk1", "lq2", "lk2"))]
        load_rest += [(wd[:, 0:E, :, :], I["wd"].rearrange("e (t p) d -> p e t d", p=P)),
                      (wd[:, E, :, :], I["sd"].rearrange("(t p) d -> p t d", p=P))]
        N_FIRST, N_A0, N_CROSS, N_REST = (16 * len(x) for x in (load_first, load_a0, load_cross, load_rest))
        late = [(wg[:, 0:E, :], I["wg"].rearrange("e h i -> h e i")), (wg[:, E, :], I["sg"]),
                (wu[:, 0:E, :], I["wu"].rearrange("e h i -> h e i")), (wu[:, E, :], I["su"])]

        @block.tensor
        def _(pe):
            def mm(o, l, r, start, stop):
                return pe.matmul(o, l, r, start=start, stop=stop, skip_group_check=True)

            pe.wait_ge(in_first, N_FIRST)
            pe.wait_ge(consts, 1)

            def setup_bias():
                pe.wait_ge(win_in, 16 * QT)
                i = banks.take(pe, "bn", POOL_M)
                for qt in range(QT):
                    last = mm(PS[:, i, qt * T:(qt + 1) * T], flip[:, :], win[:, qt, :], True, True)
                last.then_inc(banks.full[i], 1)
                i = banks.take(pe, "bt", POOL_M)
                for kt in range(QT):
                    for qt in range(QT):
                        last = mm(PS[:, i, kt * T + qt * P:kt * T + (qt + 1) * P], win[:, qt, kt * P:(kt + 1) * P],
                                  flip[:, :], True, True)
                last.then_inc(banks.full[i], 1)

            def setup_cross():
                pe.wait_ge(in_cross, N_CROSS)
                i = banks.take(pe, "ctxT", POOL_M)
                for b in range(B):
                    last = pe.transpose(PS[:, i, b * TC:(b + 1) * TC], C[:, b, :], ident[0:TC, 0:TC])
                last.then_inc(banks.full[i], 1)
                pe.wait_ge(bias_sum, 1)
                for h in range(2):
                    i = banks.take(pe, ("ft", h), POOL_M)
                    for b2 in range(2):
                        for qt in range(QT):
                            last = pe.transpose(PS[0:TC, i, b2 * T + qt * P:b2 * T + (qt + 1) * P],
                                                fs[:, 2 * h + b2, qt, :], ident[:, :])
                    last.then_inc(banks.full[i], 1)

            def tokens(u):
                kind, b = UNITS[u]
                if kind != "a0":
                    pe.wait_ge(x_new, X_COUNT[u - B])
                i = banks.take(pe, ("xt", u), POOL_M)
                for qt in range(QT):
                    last = pe.transpose(PS[:, i, qt * P:(qt + 1) * P], X[:, b, qt, :], ident[:, :])
                last.then_inc(banks.full[i], 1)

            def qprep(u):
                kind, b = UNITS[u]
                if kind == "d1" and b == 0:
                    pe.wait_ge(in_rest, N_REST)
                banks.await_read(pe, ("xt", u))
                i = banks.take(pe, ("q", u), POOL_M)
                for c in range(HEADS[kind] // H):
                    last = mm(PS[:, i, c * T:(c + 1) * T], W[kind + "_q"][:, c * D:(c + 1) * D], xT[:, b, :], True, True)
                last.then_inc(banks.full[i], 1)

            def kprep(u):
                kind, b = UNITS[u]
                if kind == "x0" and b == 0:
                    pe.wait_ge(setup_v, 2)
                if kind != "x0":
                    banks.await_read(pe, ("xt", u))
                i = banks.take(pe, ("k", u), POOL_M)
                at = 0
                if kind in ("x0", "x1"):
                    last = mm(PS[:, i, 0:TC], W[kind + "_k"][:, :], ctxT[:, b, :], True, True)
                    at = TC
                if kind != "x0":
                    for c in range(HEADS[kind] // H):
                        last = mm(PS[:, i, at + c * T:at + (c + 1) * T], W[kind + "_k"][:, c * D:(c + 1) * D],
                                  xT[:, b, :], True, True)
                last.then_inc(banks.full[i], 1)

            def vprep(u):
                kind, b = UNITS[u]
                x = xT[:, b, :]
                if u == 0:
                    pe.wait_ge(in_a0, N_A0)
                i = banks.take(pe, ("v", u), POOL_M)
                w = W[kind + "_v"][:, :]
                if kind != "x0":
                    for qt in range(QT):
                        last = mm(PS[:, i, qt * D:(qt + 1) * D], x[:, qt * P:(qt + 1) * P], w, True, True)
                if kind == "x0":
                    last = mm(PS[0:TC, i, 0:D], ctxT[:, b, :], w, True, True)
                if kind == "x1":
                    mm(PS[0:TC - 1, i, 2 * D:3 * D], ctxT[:, b, 1:TC], w, True, True)
                    last = mm(PS[:, i, 3 * D:4 * D], ctx0[:, b, :], w, True, True)
                last.then_inc(banks.full[i], 1)

            def amax(u, lo, hi):
                kind, b = UNITS[u]
                items = a_items(kind)
                if lo == 0 and hi:
                    pe.wait_ge(qs_in[AU[u] % 2], rows_in(u))
                    pe.wait_ge(ks_in[AU[u] % 2], rows_in(u))
                q, k = QS[0:SROWS, AU[u] % 2], kstack(u)[0:SROWS]
                for it in range(lo, hi):
                    s, qt1 = items[it]
                    i = banks.take(pe, ("a", u, it), POOL_A)
                    if kind == "x1":
                        last = mm(PS[:, i, 0:TC + T - 1], q[:, s, qt1 * P:(qt1 + 1) * P], k[:, s, 1:TC + T], True, True)
                    elif kind == "x0":
                        for p in range(3):
                            r = fsp[:, b, p, :].unsqueeze(1).to_broadcast([P, G4, QT * TC])
                            mm(PS[:, i, :], identb[:, :], r, p == 0, False)
                        for j in range(G4):
                            for qt in range(QT):
                                o = (j * QT + qt) * TC
                                last = mm(PS[:, i, o:o + TC], q[:, G4 * s + j, qt * P:(qt + 1) * P],
                                          k[:, G4 * s + j, :], False, j == G4 - 1 and qt == QT - 1)
                    else:
                        for qt in range(QT):
                            last = mm(PS[:, i, qt * T:(qt + 1) * T], q[:, s, qt * P:(qt + 1) * P], k[:, s, :],
                                      True, True)
                    last.then_inc(banks.full[i], 1)

            def mneg(u):
                n = HEADS[UNITS[u][0]]
                banks.await_read(pe, ("a", u, len(a_items(UNITS[u][0])) - 1))
                i = banks.take(pe, ("m", u), POOL_M)
                for qt in range(QT):
                    last = pe.transpose(PS[0:n, i, qt * P:(qt + 1) * P], mx[:, qt, 0:n], ident[:, :])
                last.then_inc(banks.full[i], 1)

            def bexp(u, g, n):
                kind, b = UNITS[u]
                if u == 0 and g == 0 and n == 0:
                    pe.wait_ge(setup_v, 1)
                if g == 0 and n == 0:
                    pe.wait_ge(m_in, 16 * MROWS * (AU[u] + 1))
                    pe.wait_ge(ones_in, 32)
                q, k = QS[:, AU[u] % 2], kstack(u)
                off = TC if kind == "x1" else 0
                c0 = 1 if kind == "x1" else 0
                what, s = b_items(kind, g)[n]
                i = banks.take(pe, ("b", u, g, n), POOL_B)
                if what == "c":
                    if kind == "x0":
                        for p in range(3):
                            r = fstp[:, b, p, :].unsqueeze(1).to_broadcast([TC, 2, T])
                            mm(PS[0:TC, i, :], identb[0:TC, 0:TC], r, p == 0, False)
                    for j in range(2):
                        last = mm(PS[0:TC - c0, i, j * T:(j + 1) * T], k[:, s + j, c0:TC], q[:, s + j, :],
                                  kind == "x1", True)
                else:
                    if kind == "a0":
                        for p in range(3):
                            mm(PS[:, i, :], identb[:, :], bias_tp[:, p, :], p == 0, False)
                    for kt in range(QT):
                        last = mm(PS[:, i, kt * T:(kt + 1) * T], k[:, s, off + kt * P:off + (kt + 1) * P],
                                  q[:, s, :], kind != "a0", True)
                last.then_inc(banks.full[i], 1)

            def pv(u, g):
                kind, b = UNITS[u]
                for n in range(len(b_items(kind, g))):
                    banks.await_read(pe, ("b", u, g, n))
                if g == 0:
                    banks.await_read(pe, ("v", u))
                i = banks.take(pe, ("o", u, g), POOL_O)
                V = VX[:, AU[u] % 2]
                terms = []
                nc0 = 2 if kind in ("x0", "x1") else 0
                if nc0:
                    rowsc = TC - (kind == "x1")
                    terms.append([(V[0:rowsc, 2], PR[0:rowsc, p_slot(u, g, j // 2), (j % 2) * T:(j % 2 + 1) * T])
                                  for j in range(G4)])
                if kind != "x0":
                    for kt in range(QT):
                        terms.append([(V[:, kt], PR[:, p_slot(u, g, nc0 + j), kt * T:(kt + 1) * T])
                                      for j in range(G4)])
                for n, term in enumerate(terms):
                    for j, (v, p) in enumerate(term):
                        s = G4 * g + j
                        h = s // 2 if kind == "d1" else s
                        last = mm(PS[STRIP * j:STRIP * (j + 1), i, 0:T], v[:, h, :], p, n == 0, n == len(terms) - 1)
                last.then_inc(banks.full[i], 1)

            def post(u, k):
                kind, b = UNITS[u]
                gs = groups(kind)
                if k == 0:
                    for g in range(gs):
                        banks.await_read(pe, ("o", u, g))
                qt, half = divmod(k, gs // 4)
                i = banks.take(pe, ("t", u, qt, half), POOL_M)
                for g in range(4):
                    last = pe.transpose(PS[:, i, g * P:(g + 1) * P], OR[:, 4 * half + g, qt * P:(qt + 1) * P],
                                        ident[:, :])
                last.then_inc(banks.full[i], 1)

            def ont(u):
                kind, b = UNITS[u]
                if kind == "a0":
                    pe.wait_ge(mix_in, 16)
                else:
                    pe.wait_ge(on_ready, AU[u] + 1)
                src = cm[:, b * QT:(b + 1) * QT, :] if kind == "a0" else on
                i = banks.take(pe, ("ont", u), POOL_M)
                for qt in range(QT):
                    last = pe.transpose(PS[:, i, qt * P:(qt + 1) * P], src[:, qt, :], ident[:, :])
                last.then_inc(banks.full[i], 1)

            def wo(u):
                kind, b = UNITS[u]
                banks.await_read(pe, ("ont", u))
                i = banks.take(pe, ("wo", u), POOL_M)
                for qt in range(QT):
                    last = mm(PS[:, i, qt * D:(qt + 1) * D], OT[:, qt, :], W[kind + "_o"][:, :], True, True)
                last.then_inc(banks.full[i], 1)

            def route(u):
                kind, b = UNITS[u]
                tokens(u)
                banks.await_read(pe, ("xt", u))
                x = xT[:, b, :]
                if kind == "f0":
                    pe.wait_ge(in_rest, N_REST)
                i = banks.take(pe, ("r", u), POOL_M)
                for qt in range(QT):
                    last = mm(PS[:, i, qt * E:(qt + 1) * E], x[:, qt * P:(qt + 1) * P], W[kind + "_r"][:, :], True, True)
                last.then_inc(banks.full[i], 1)

            def up(u, e):
                kind, b = UNITS[u]
                x = xT[:, b, :]
                if kind == "f1":
                    pe.wait_ge(late_in, 16 * len(late))
                for j, (name, w) in enumerate([("h", w1)] if kind == "f0" else [("g", wg), ("u", wu)]):
                    i = banks.take(pe, (name, u, e), (POOL_A, POOL_B)[j])
                    for t in range(HH):
                        last = mm(PS[:, i, t * T:(t + 1) * T], w[:, e, t * P:(t + 1) * P], x, True, True)
                    last.then_inc(banks.full[i], 1)

            def down(u, e):
                kind, b = UNITS[u]
                w = w2 if kind == "f0" else wd
                ne = e_before[u] + e
                banks.await_read(pe, ("h" if kind == "f0" else "u", u, e))
                i = banks.take(pe, ("y", u, e), POOL_O)
                for qt in range(QT):
                    for t in range(HH):
                        last = mm(PS[:, i, qt * D:(qt + 1) * D],
                                  hs[ne % 2][:, t * T + qt * P:t * T + (qt + 1) * P], w[:, e, t, :],
                                  t == 0, t == HH - 1)
                last.then_inc(banks.full[i], 1)

            for step, u, a in order():
                if step == "setup_bias":
                    setup_bias()
                elif step == "setup_cross":
                    setup_cross()
                elif step == "route":
                    route(u)
                elif step == "qprep":
                    qprep(u)
                elif step == "kprep":
                    kprep(u)
                elif step == "vprep":
                    vprep(u)
                elif step == "amax":
                    lo, hi = part_of(u, a)
                    amax(u, lo, hi)
                elif step == "mneg":
                    mneg(u)
                elif step == "bexp":
                    bexp(u, *a)
                elif step == "pv":
                    pv(u, a)
                elif step == "post":
                    post(u, a)
                elif step == "ont":
                    ont(u)
                elif step == "wo":
                    wo(u)
                elif step == "xt":
                    tokens(u)
                elif step == "ffn":
                    up(u, a)
                    if a:
                        down(u, a - 1)
                elif step == "ffn_end":
                    down(u, EXPERTS[UNITS[u][0]] - 1)

        @block.scalar
        def _(act):
            act.wait_ge(in_first, N_FIRST)
            act.activation(lam[:, 4:5], gates[:, 0:1], ACT.Exp, scale=-1.0).then_inc(act_set, 1)

            def setup_rest():
                act.wait_ge(in_rest, N_REST)
                act.activation(gate_t[:, :], gate_t[:, :], ACT.Tanh).then_inc(act_set, 1)
                act.wait_ge(lam_sums, 1)
                act.activation(lam[:, 2:4], lam[:, 0:2], ACT.Exp).then_inc(act_set, 1)

            def bexp(u, g, n):
                kind, b = UNITS[u]
                if n == 0 and groups_before[u] + g >= 2:
                    u2, g2 = (u, g - 2) if g >= 2 else (prev(u), groups(UNITS[prev(u)][0]) + g - 2)
                    banks.await_full(act, ("o", u2, g2))
                what, s = b_items(kind, g)[n]
                i = banks.await_full(act, ("b", u, g, n))
                pr = P if what == "s" else TC - (kind == "x1")
                act.activation(PR[0:pr, p_slot(u, g, n), :], PS[0:pr, i, :], ACT.Exp).then_inc(banks.free[i], 1)

            def pv(u, g):
                if g == 0 and prev(u) is not None:
                    banks.await_full(act, last_t(prev(u)))
                i = banks.await_full(act, ("o", u, g))
                act.copy(OR[:, g, :], PS[:, i, 0:T]).then_inc(banks.free[i], 1)

            def ont(u):
                i = banks.await_full(act, ("ont", u))
                act.copy(OT[:, :, :], PS[:, i, 0:QT * P].rearrange("p (q t) -> p q t", t=P)).then_inc(banks.free[i], 1)

            def route(u):
                kind, b = UNITS[u]
                act.wait_ge(rt_in, f_units.index(u) + 1)
                if kind == "f0":
                    act.activation(gt[:, :, 1], gt[:, :, 0], ACT.Tanh, scale=0.5).then_inc(rt_exp, 1)
                else:
                    act.activation(le[:, :, :], lg[:, :, :], ACT.Exp, scale=-1.0).then_inc(rt_exp, 1)

            def ffn(u, e):
                kind, b = UNITS[u]
                ne = e_before[u] + e
                if kind == "f0":
                    i = banks.await_full(act, ("h", u, e))
                    if ne >= 2:
                        banks.await_full(act, ("y",) + flat_e[ne - 2])
                    act.activation(hs[ne % 2], PS[:, i, :], ACT.Gelu).then_inc(banks.free[i], 1)
                else:
                    i = banks.await_full(act, ("g", u, e))
                    if UNITS[flat_e[ne - 2][0]][0] == "f1":
                        banks.await_read(act, ("u",) + flat_e[ne - 2])
                    act.activation(sg[ne % 2], PS[:, i, :], ACT.Silu).then_inc(banks.free[i], 1)

            for step, u, a in order():
                if step == "qprep" and UNITS[u] == ("d1", 0):
                    setup_rest()
                if step in ("xt", "route"):
                    i = banks.await_full(act, ("xt", u))
                    act.copy(xT[:, UNITS[u][1], :], PS[:, i, 0:T]).then_inc(banks.free[i], 1)
                if step == "route":
                    route(u)
                if step == "bexp":
                    bexp(u, *a)
                elif step == "pv":
                    pv(u, a)
                elif step == "ont":
                    ont(u)
                elif step == "ffn":
                    ffn(u, a)

        @block.gpsimd
        def _(pool):
            nlink = [0]

            def link(ins):
                nlink[0] += 1
                ins.then_inc(p_chain, 1)
                pool.wait_ge(p_chain, nlink[0])

            link(pool.memset(ident[:, :], 0.0))
            link(pool.affine_select(out=ident[:, :], in_=ident[:, :], compare_op=ALU.not_equal, fill=1.0, base=0,
                                    pattern=[[-1, P]], channel_multiplier=1))
            link(pool.memset(flip[:, :], 0.0))
            link(pool.affine_select(out=flip[:, :], in_=flip[:, :], compare_op=ALU.not_equal, fill=1.0,
                                    base=1 - P, pattern=[[1, P]], channel_multiplier=1))
            link(pool.tensor_copy(identb[:, :], ident[:, :]))
            link(pool.iota(iota8[:, :], pattern=[[1, E]], base=0, channel_multiplier=0,
                           allow_small_or_imprecise_dtypes=True))
            link(pool.memset(ones3[:, :], 1.0))
            pool.memset(neghalf[:, :], -0.5).then_inc(consts, 1)
            pool.memset(QS[:, 0, :, :].bitcast(F32), 0.0).then_inc(zeroed, 1)

            def kprep(u):
                n = AU[u]
                pool.wait_ge(k_ready, n + 1)
                if n:
                    pool.wait_ge(kp_out, 16 * sent_dmas(prev(u)))
                w = kwidths[UNITS[u][0]]
                x, part = kf[:, 0:w], [kp[:, p, 0:w] for p in range(3)]
                link(pool.tensor_copy(part[0], x))
                link(pool.tensor_tensor(x, x, part[0], ALU.subtract))
                link(pool.tensor_copy(part[1], x))
                pool.tensor_tensor(part[2], x, part[1], ALU.subtract).then_inc(kp_ready, 1)
                pool.wait_ge(kp_ready, n + 1)
                if n == 0:
                    pool.memset(QS[:, 1, :, :].bitcast(F32), 0.0).then_inc(zeroed, 1)
                    pool.memset(KS[:, 1, :].bitcast(F32), 0.0).then_inc(zeroed, 1)

            npow = [0]

            def power():
                npow[0] += 1
                pool.wait_ge(var_ready, npow[0])
                pool.tensor_tensor(rstd[:, :], ve[:, :], neghalf[:, :], ALU.pow).then_inc(rstd_ready, 1)

            for step, u, a in order():
                kind, b = UNITS[u]
                if step == "kprep":
                    kprep(u)
                elif step == "post" and kind == "x1" and a == turned(u) - 1 or step == "wo" and kind == "d1":
                    power()
                if step in ("wo", "ffn_end"):
                    power()

        @block.sync
        def _(sp):
            for dst, src in load_first:
                sp.dma_start(dst, src).then_inc(in_first, 16)
            off = T - 1 - TB // 2
            tb, ext = I["time_bias"].tensor, ext_d
            sp.dma_start(bass.AP(tensor=ext, offset=0, ap=[[1, off], [1, 1]]),
                         bass.AP(tensor=tb, offset=0, ap=[[0, off], [1, 1]])).then_inc(ext_done, 16)
            sp.dma_start(bass.AP(tensor=ext, offset=off, ap=[[1, 1], [1, TB]]),
                         bass.AP(tensor=tb, offset=0, ap=[[1, 1], [1, TB]])).then_inc(ext_done, 16)
            end = 2 * T - off - TB
            sp.dma_start(bass.AP(tensor=ext, offset=off + TB, ap=[[1, end], [1, 1]]),
                         bass.AP(tensor=tb, offset=TB - 1, ap=[[0, end], [1, 1]])).then_inc(ext_done, 16)
            sp.wait_ge(ext_done, 48)
            for qt in range(QT):
                sp.dma_start(win[:, qt, :], bass.AP(tensor=ext, offset=P - P * qt, ap=[[1, P], [1, T]])).then_inc(win_in, 16)
            for dst, src in load_a0:
                sp.dma_start(dst, src).then_inc(in_a0, 16)

            def send(u, par, parts_sb, ready, out_sem, which, tiles):
                sp.wait_ge(ready, AU[u] + 1)
                if AU[u] >= 2:
                    sp.wait_ge((qs_in, ks_in)[which][par], rows_in(prev(u, 2)))
                d = scr[2 * par + which]
                for (t0, tn, row, col) in tiles:
                    for p in range(3):
                        sp.dma_start(d[p, row:row + P, col:col + tn], parts_sb[:, p, t0:t0 + tn]).then_inc(out_sem, 16)

            def stack(u, par, out_sem, dst, which, in_sem, n, c0):
                d = scr[2 * par + which]
                sp.wait_ge(out_sem, 16 * sent_dmas(u))
                for j, p in enumerate((QPART, KPART)[which]):
                    src = d[p, 0:n * HD, 0:c0].rearrange("(s d) t -> d s t", d=HD)
                    sp.dma_start(dst[j * HD:(j + 1) * HD], src).then_inc(in_sem, 16)

            for step, u, a in order():
                kind, b = UNITS[u]
                if step == "vprep" and u == 0:
                    for dst, src in load_cross:
                        sp.dma_start(dst, src).then_inc(in_cross, 16)
                    for dst, src in load_rest:
                        sp.dma_start(dst, src).then_inc(in_rest, 16)
                par = AU.get(u, 0) % 2
                if step == "qprep":
                    send(u, par, qp, qp_ready, qp_out, 0, [(c * T, T, c * P, 0) for c in range(HEADS[kind] // H)])
                elif step == "kprep":
                    if kind == "x0":
                        tiles = [(0, TC, 0, 0)]
                    elif kind == "x1":
                        tiles = [(0, TC + T, 0, 0)]
                    else:
                        tiles = [(c * T, T, c * P, 0) for c in range(HEADS[kind] // H)]
                    send(u, par, kp, kp_ready, kp_out, 1, tiles)
                elif step in ("qstack", "kstack"):
                    n = HEADS[kind]
                    if AU[u] >= 2:
                        banks.await_full(sp, last_b(prev(u, 2)))
                    else:
                        sp.wait_ge(zeroed, 1 + 2 * AU[u])
                        sp.wait_ge(cleared, 1)
                    if step == "qstack":
                        stack(u, par, qp_out, QS[:, par, 0:n, :], 0, qs_in[par], n, T)
                    else:
                        stack(u, par, kp_out, kstack(u), 1, ks_in[par], n, KEYS[kind])
                        if AU[u] < 2:
                            sp.dma_start(KS[SROWS:SROWS + MROWS, par, :].rearrange("p (n w) -> p n w", w=512),
                                         ones3[:, :].unsqueeze(1).to_broadcast([MROWS, 2 * H * T // 512, 512])).then_inc(ones_in, 16)
                elif step == "mneg":
                    n = HEADS[kind]
                    sp.wait_ge(mp_ready, AU[u] + 1)
                    for p in range(MROWS):
                        sp.dma_start(QS[SROWS + p:SROWS + p + 1, par, 0:n, :], mp[0:n, p, :]).then_inc(m_in, 16)
                elif step == "post" and kind == "a0" and a == turned(u) - 1:
                    sp.wait_ge(on_ready, AU[u] + 1)
                    for qt in range(QT):
                        sp.dma_start(bass.AP(tensor=mix, offset=(b * T + qt * P) * HD, ap=[[HD, P], [B * T * HD, H], [1, HD]]),
                                     on[:, qt, :].rearrange("p (h d) -> p h d", d=HD)).then_inc(mix_out, 16)
                elif step == "ont" and u == 0:
                    sp.wait_ge(mix_out, 16 * QT * B)
                    sp.dma_start(cm, bass.AP(tensor=mix, offset=0, ap=[[D, P], [P * D, B * QT], [1, D]])).then_inc(mix_in, 16)
                elif step == "ffn_end" and (kind == "f1" or b == B - 1):
                    sp.wait_ge(x_new, X_COUNT[u])
                    if kind == "f1":
                        sp.dma_start(out[b].rearrange("(t p) d -> p t d", p=P), X[:, b, :, :]).then_inc(stored, 16)
                    else:
                        for dst, src in late:
                            sp.dma_start(dst, src).then_inc(late_in, 16)
            sp.wait_ge(stored, 16 * B)

        @block.vector
        def _(dve):
            nlink = [0]

            def link(ins):
                nlink[0] += 1
                ins.then_inc(v_chain, 1)
                dve.wait_ge(v_chain, nlink[0])

            def parts(src, dst, tmp_, last=None):
                link(dve.tensor_copy(dst[0], src))
                link(dve.tensor_tensor(tmp_, src, dst[0], ALU.subtract))
                link(dve.tensor_copy(dst[1], tmp_))
                ins = dve.tensor_tensor(dst[2], tmp_, dst[1], ALU.subtract)
                if last is None:
                    link(ins)
                else:
                    ins.then_inc(last, 1)

            side = [iter(())]
            dve.memset(KS[:, 0, :].bitcast(F32), 0.0).then_inc(cleared, 1)
            dve.wait_ge(in_first, N_FIRST)

            def setup_bias():
                dve.wait_ge(act_set, 1)
                link(dve.tensor_scalar(lam[:, 6:7], lam[:, 4:5], 1.0, None, ALU.add))
                link(dve.reciprocal(lam[:, 6:7], lam[:, 6:7]))
                for key, raw in (("bn", bias_n), ("bt", bias_t)):
                    i = banks.await_full(dve, key)
                    dve.tensor_scalar(raw[:, :], PS[:, i, :], lam[:, 6:7], gates[:, 1:2], ALU.mult, ALU.add).then_inc(banks.free[i], 1)
                    banks.await_read(dve, key)
                parts(bias_t[:, :], [bias_tp[:, p, :] for p in range(3)], vf[:, :], setup_v)
                link(dve.memset(VX[:, :, :, :, :], 1.0))
                dve.wait_ge(setup_v, 1)

            def setup_cross():
                dve.wait_ge(in_cross, N_CROSS)
                i = banks.await_full(dve, "ctxT")
                dve.tensor_copy(ctxT[:, :, :], PS[:, i, 0:B * TC].rearrange("p (b t) -> p b t", t=TC)).then_inc(banks.free[i], 1)
                banks.await_read(dve, "ctxT")
                link(dve.tensor_copy(ctx0[:, :, :], ctxT[:, :, 0:1].to_broadcast([P, B, P])))
                dve.tensor_tensor(fs[:, :, :, :], fs[:, :, :, :], fm[:, :, :, :], ALU.add).then_inc(bias_sum, 1)
                dve.wait_ge(bias_sum, 1)
                for h in range(2):
                    i = banks.await_full(dve, ("ft", h))
                    dve.tensor_copy(fst[:, 2 * h:2 * h + 2, :], PS[0:TC, i, :].rearrange("p (b t) -> p b t", t=T)).then_inc(banks.free[i], 1)
                banks.await_read(dve, ("ft", 1))
                parts(fs[:, :, :, :].rearrange("p b q t -> p b (q t)"), [fsp[:, :, p, :] for p in range(3)],
                      vf[:, :].rearrange("p (b t) -> p b t", b=B))
                for h in range(2):
                    parts(fst[:, 2 * h:2 * h + 2, :], [fstp[:, 2 * h:2 * h + 2, p, :] for p in range(3)],
                          vf[0:TC, :].rearrange("p (b t) -> p b t", t=T), setup_v if h else None)
                dve.wait_ge(setup_v, 2)

            def setup_rest():
                dve.wait_ge(in_rest, N_REST)
                link(dve.tensor_tensor(lam4[:, 0, :], lam4[:, 0, :], lam4[:, 1, :], ALU.mult))
                link(dve.tensor_tensor(lam4[:, 2, :], lam4[:, 2, :], lam4[:, 3, :], ALU.mult))
                dve.tensor_reduce(lam[:, 0:2], lam4[:, 0:4:2, :], AX.X, ALU.add).then_inc(lam_sums, 1)
                dve.wait_ge(act_set, 3)
                link(dve.tensor_scalar(lam[:, 5:6], lam[:, 3:4], -LAMBDA_INIT, None, ALU.add))
                link(dve.tensor_tensor(lam[:, 5:6], lam[:, 5:6], lam[:, 2:3], ALU.subtract))

            def qprep(u):
                kind, b = UNITS[u]
                w = widths[kind]
                i = banks.await_full(dve, ("q", u))
                bias = cols[kind + "_q"][:, 0:1] if kind in ("a0", "x0") else 0.0
                dve.tensor_scalar(qf[:, 0:w], PS[:, i, 0:w], bias, SCALE, ALU.add, ALU.mult).then_inc(banks.free[i], 1)
                banks.await_read(dve, ("q", u))
                if AU[u]:
                    dve.wait_ge(qp_out, 16 * sent_dmas(prev(u)))
                parts(qf[:, 0:w], [qp[:, p, 0:w] for p in range(3)], qf[:, 0:w], qp_ready)
                dve.wait_ge(qp_ready, AU[u] + 1)

            def kprep(u):
                kind, b = UNITS[u]
                n, w = AU[u], kwidths[kind]
                i = banks.await_full(dve, ("k", u))
                if n:
                    dve.wait_ge(kp_ready, n)
                bias = cols[kind + "_k"][:, 0:1] if kind in ("a0", "x0") else 0.0
                dve.tensor_scalar(kf[:, 0:w], PS[:, i, 0:w], bias, None, ALU.add).then_inc(banks.free[i], 1)
                banks.await_read(dve, ("k", u))
                dve.sem_inc(k_ready, 1)

            def vprep(u):
                kind, b = UNITS[u]
                par, n = AU[u] % 2, AU[u]
                i = banks.await_full(dve, ("v", u))
                if n >= 2:
                    u2 = prev(u, 2)
                    banks.await_full(dve, ("o", u2, groups(UNITS[u2][0]) - 1))

                def to_vx(rows_, kt, c):
                    o = VX[0:rows_, par, kt, :, 0:HD]
                    src = PS[0:rows_, i, c * D:(c + 1) * D].rearrange("p (h d) -> p h d", d=HD)
                    if kind in ("a0", "x0"):
                        return dve.tensor_tensor(o, src, rows[kind + "_v"][0:rows_, :].rearrange("p (h d) -> p h d", d=HD),
                                                 ALU.add)
                    return dve.tensor_copy(o, src)
                if kind == "x0":
                    last = to_vx(TC, 2, 0)
                else:
                    for kt in range(QT):
                        last = to_vx(P, kt, kt)
                if kind == "x1":
                    to_vx(TC - 1, 2, 2)
                    last = dve.tensor_tensor(v0[:, b, :].rearrange("p (h d) -> p h d", d=HD),
                                             PS[:, i, 3 * D:4 * D].rearrange("p (h d) -> p h d", d=HD),
                                             gate_t[:, :].unsqueeze(2).to_broadcast([P, H, HD]), ALU.mult)
                last.then_inc(banks.free[i], 1)

            sums = ((vf[:, 0:T], vf[:, T:2 * T]), (acc[:, :, :].rearrange("p q d -> p (q d)"), y[:, :, :].rearrange("p q d -> p (q d)")))

            def amax(u, lo, hi):
                kind, b = UNITS[u]
                items = a_items(kind)
                if lo == 0 and hi and AU[u]:
                    banks.await_full(dve, ("m", prev(u)))
                for it in range(lo, hi):
                    s, qt = items[it]
                    i = banks.await_full(dve, ("a", u, it))
                    if kind == "a0":
                        ago = AU[u] * len(items) + it - 2
                        if ago >= 0:
                            banks.await_read(dve, ("a", ATT[ago // len(items)], ago % len(items)))
                        for q in range(QT):
                            last = dve.tensor_tensor_reduce(out=sums[it % 2][q], in0=PS[:, i, q * T:(q + 1) * T],
                                                            in1=bias_n[:, q * T:(q + 1) * T], scale=1.0, scalar=LOWEST,
                                                            op0=ALU.add, op1=ALU.max, accum_out=mx[:, q, s:s + 1])
                        last.then_inc(banks.free[i], 1)
                        continue
                    if kind == "x1":
                        o, src = mx[:, qt, s:s + 1], PS[:, i, 0:TC + T - 1]
                    elif kind == "x0":
                        o = mx[:, :, G4 * s:G4 * s + G4].rearrange("p q s -> p s q")
                        src = PS[:, i, :].rearrange("p (s q t) -> p s q t", q=QT, t=TC)
                    else:
                        o, src = mx[:, :, s], PS[:, i, :].rearrange("p (q t) -> p q t", t=T)
                    dve.tensor_reduce(o, src, AX.X, ALU.max).then_inc(banks.free[i], 1)
                    for _ in range(2):
                        next(side[0], None)

            def mneg(u):
                n = HEADS[UNITS[u][0]]
                i = banks.await_full(dve, ("m", u))
                if AU[u]:
                    dve.wait_ge(m_in, 16 * MROWS * AU[u])
                dve.tensor_scalar(mf[0:n, :], PS[0:n, i, 0:T], -1.0, TOP, ALU.mult, ALU.add).then_inc(banks.free[i], 1)
                banks.await_read(dve, ("m", u))
                parts(mf[0:n, :], [mp[0:n, p, :] for p in range(3)], mr[0:n, :], mp_ready)
                dve.wait_ge(mp_ready, AU[u] + 1)

            nvar = [0]

            def hold(ins):
                nlink[0] += 1
                n = nlink[0]
                ins.then_inc(v_chain, 1)
                yield
                dve.wait_ge(v_chain, n)

            def norm(src, dst, gain=None, offset=None, done=None):
                for qt in range(QT):
                    last = dve.bn_stats(st[:, qt, :], src[:, qt, :])
                yield from hold(last)
                for qt in range(QT):
                    last = dve.bn_aggr(mv[:, qt, :], st[:, qt, :])
                yield from hold(last)
                nvar[0] += 1
                dve.tensor_scalar(ve[:, :], mv[:, :, 1], EPS, None, ALU.add).then_inc(var_ready, 1)
                n = nvar[0]
                yield
                yield
                dve.wait_ge(rstd_ready, n)
                for qt in range(QT):
                    last = dve.tensor_scalar(dst[:, qt, :], src[:, qt, :], mv[:, qt, 0:1], rstd[:, qt:qt + 1],
                                             ALU.subtract, ALU.mult)
                if gain is not None:
                    yield from hold(last)
                    yield from hold(dve.tensor_tensor(dst, dst, gain.unsqueeze(1).to_broadcast([P, QT, D]), ALU.mult))
                    last = dve.tensor_tensor(dst, dst, offset.unsqueeze(1).to_broadcast([P, QT, D]), ALU.add)
                if done is not None:
                    last.then_inc(done, 1)
                else:
                    yield from hold(last)

            def post(u, k):
                kind, b = UNITS[u]
                gs = groups(kind)
                if k == 0 and AU[u] and kind == "a0":
                    dve.wait_ge(mix_out, 16 * QT * AU[u])
                elif k == 0 and kind != "a0":
                    banks.await_full(dve, ("ont", prev(u)))
                qt, half = divmod(k, gs // 4)
                key = ("t", u, qt, half)
                i = banks.await_full(dve, key)
                t = PS[:, i, :].rearrange("p (s w) -> p s w", w=STRIP)
                yield from hold(dve.reciprocal(rs[:, :], t[:, :, HD]))
                if kind == "d1":
                    yield from hold(dve.tensor_scalar(rs[:, 1:H:2], rs[:, 1:H:2], lam[:, 5:6], None, ALU.mult))
                    o = tmp[:, :, :]
                else:
                    o = on[:, qt, :].rearrange("p (h d) -> p h d", d=HD)
                dve.tensor_tensor(o, t[:, :, 0:HD], rs[:, :].unsqueeze(2).to_broadcast([P, H, HD]),
                                  ALU.mult).then_inc(banks.free[i], 1)
                yield
                banks.await_read(dve, key)
                if kind == "d1":
                    yield from hold(dve.tensor_tensor(on[:, qt, half * D // 2:(half + 1) * D // 2].rearrange("p (h d) -> p h d", d=HD),
                                           tmp[:, 0:H:2, :], tmp[:, 1:H:2, :], ALU.add))
                if k < turned(u) - 1:
                    return
                if kind == "x1":
                    yield from hold(dve.tensor_tensor(onb[:, :, :], on[:, :, :], v0[:, b:b + 1, :].to_broadcast([P, QT, D]),
                                                      ALU.add))
                    yield from norm(onb[:, :, :], on[:, :, :], rows["x1_g"][:, :], rows["x1_b"][:, :], on_ready)
                    yield
                    dve.wait_ge(on_ready, AU[u] + 1)
                else:
                    dve.sem_inc(on_ready, 1)

            def finish(u):
                kind, b = UNITS[u]
                i = banks.await_full(dve, ("wo", u))
                x = X[:, b, :, :]
                ps = PS[:, i, 0:QT * D].rearrange("p (q d) -> p q d", d=D)
                if kind == "d1":
                    dve.tensor_copy(y[:, :, :], ps).then_inc(banks.free[i], 1)
                    yield
                    banks.await_read(dve, ("wo", u))
                    yield from norm(y[:, :, :], y[:, :, :], rows["d1_g"][:, :], rows["d1_b"][:, :])
                    yield from hold(dve.tensor_tensor(y[:, :, :], y[:, :, :], x, ALU.add))
                else:
                    dve.tensor_tensor(y[:, :, :], ps, x, ALU.add).then_inc(banks.free[i], 1)
                    yield
                    banks.await_read(dve, ("wo", u))
                    yield from hold(dve.tensor_tensor(y[:, :, :], y[:, :, :],
                                           rows[kind + "_o"][:, :].unsqueeze(1).to_broadcast([P, QT, D]), ALU.add))
                yield from norm(y[:, :, :], x, done=x_new)
                yield
                dve.wait_ge(x_new, X_COUNT[u])

            def route(u):
                kind, b = UNITS[u]
                nf = f_units.index(u)
                i = banks.await_full(dve, ("r", u))
                ps = PS[:, i, 0:QT * E].rearrange("p (q e) -> p q e", e=E)
                if kind == "f0":
                    dve.tensor_copy(lg[:, :, :], ps).then_inc(banks.free[i], 1)
                    banks.await_read(dve, ("r", u))
                else:
                    dve.tensor_tensor(lg[:, :, :], ps, rbias[:, :].unsqueeze(1).to_broadcast([P, QT, E]),
                                      ALU.add).then_inc(rt_in, 1)
                    dve.wait_ge(rt_in, nf + 1)
                    dve.sem_inc(banks.free[i], 1)
                    dve.wait_ge(rt_exp, nf + 1)
                    link(dve.tensor_scalar(le[:, :, :], le[:, :, :], 1.0, None, ALU.add))
                    link(dve.reciprocal(lg[:, :, :], le[:, :, :]))
                for qt in range(QT):
                    link(dve.max(top[:, qt, :], lg[:, qt, :]))
                    link(dve.max_index(topi[:, qt, :], top[:, qt, :], lg[:, qt, :]))
                link(dve.tensor_copy(topf[:, :, 0:2], topi[:, :, 0:2]))
                if kind == "f0":
                    dve.tensor_tensor(gt[:, :, 0], top[:, :, 0], top[:, :, 1], ALU.subtract).then_inc(rt_in, 1)
                    dve.wait_ge(rt_exp, nf + 1)
                    link(dve.tensor_scalar(gt[:, :, 2], gt[:, :, 1], 0.5, 0.5, ALU.mult, ALU.add))
                    link(dve.tensor_scalar(gt[:, :, 3], gt[:, :, 1], -0.5, 0.5, ALU.mult, ALU.add))
                else:
                    link(dve.tensor_tensor(gt[:, :, 0], top[:, :, 0], top[:, :, 1], ALU.add))
                    link(dve.reciprocal(gt[:, :, 1], gt[:, :, 0]))
                    link(dve.tensor_tensor(gt[:, :, 2], top[:, :, 0], gt[:, :, 1], ALU.mult))
                    link(dve.tensor_tensor(gt[:, :, 3], top[:, :, 1], gt[:, :, 1], ALU.mult))
                for qt in range(QT):
                    link(dve.tensor_scalar(gate[:, b, qt, :], iota8[:, :], topf[:, qt, 0:1], gt[:, qt, 2:3], ALU.is_equal, ALU.mult))
                    link(dve.tensor_scalar(le[:, qt, :], iota8[:, :], topf[:, qt, 1:2], gt[:, qt, 3:4], ALU.is_equal, ALU.mult))
                    link(dve.tensor_tensor(gate[:, b, qt, :], gate[:, b, qt, :], le[:, qt, :], ALU.add))

            def add_expert(u, e):
                kind, b = UNITS[u]
                i = banks.await_full(dve, ("y", u, e))
                for qt in range(QT):
                    ps, a_ = PS[:, i, qt * D:(qt + 1) * D], acc[:, qt, :]
                    if e == 0:
                        ins = dve.tensor_scalar(a_, ps, gate[:, b, qt, 0:1], None, ALU.mult)
                    elif e < E:
                        ins = dve.scalar_tensor_tensor(out=a_, in0=ps, scalar=gate[:, b, qt, e:e + 1], in1=a_,
                                                       op0=ALU.mult, op1=ALU.add)
                    else:
                        ins = dve.tensor_tensor(a_, ps, a_, ALU.add)
                ins.then_inc(banks.free[i], 1)
                banks.await_read(dve, ("y", u, e))

            def ffn(u, e):
                if UNITS[u][0] == "f1":
                    ne = e_before[u] + e
                    i = banks.await_full(dve, ("u", u, e))
                    banks.await_read(dve, ("g", u, e))
                    banks.await_full(dve, ("y",) + flat_e[ne - 2])
                    dve.tensor_tensor(hs[ne % 2], PS[:, i, :], sg[ne % 2], ALU.mult).then_inc(banks.free[i], 1)
                if e:
                    add_expert(u, e - 1)

            def ffn_end(u):
                kind, b = UNITS[u]
                add_expert(u, EXPERTS[kind] - 1)
                link(dve.tensor_tensor(y[:, :, :], acc[:, :, :], X[:, b, :, :], ALU.add))
                for _ in norm(y[:, :, :], X[:, b, :, :], done=x_new):
                    pass
                dve.wait_ge(x_new, X_COUNT[u])

            for step, u, a in order():
                if step not in ("amax", "bexp", "pv", "ffn", "xt", "qstack", "kstack"):
                    for _ in side[0]:
                        pass
                if step == "qprep" and UNITS[u] == ("d1", 0):
                    setup_rest()
                if step == "setup_bias":
                    setup_bias()
                elif step == "setup_cross":
                    setup_cross()
                elif step == "route":
                    route(u)
                elif step == "qprep":
                    qprep(u)
                elif step == "kprep":
                    kprep(u)
                elif step == "vprep":
                    vprep(u)
                elif step == "amax":
                    amax(u, *part_of(u, a))
                elif step == "mneg":
                    mneg(u)
                elif step == "post":
                    side[0] = post(u, a)
                elif step == "wo":
                    side[0] = finish(u)
                elif step == "ffn":
                    ffn(u, a)
                    for _ in range(2):
                        next(side[0], None)
                elif step == "ffn_end":
                    ffn_end(u)


def kernel(**inputs):
    import numpy as np
    import concourse.bacc as bacc
    from concourse.bass_utils import run_bass_kernel_spmd as run

    g = {k: np.asarray(v) for k, v in inputs.items()}
    t = np.transpose
    a = {
        "x": g["x"], "ctx_1024": g["ctx_1024"], "fside_BxSxS2_0": g["fside_BxSxS2_0"],
        "mask_BxSxS2_ff0": g["mask_BxSxS2_ff0"],
        "w_a0_q": g["L0_attn_Wq"].T, "w_a0_k": g["L0_attn_Wk"].T, "w_a0_v": g["L0_attn_Wv"].T,
        "w_a0_o": g["L0_attn_Wo"].T, "w_x0_q": g["L0_xattn_Wq"], "w_x0_k": g["L0_xattn_Wk"],
        "w_x0_v": g["L0_xattn_Wv"], "w_x0_o": g["L0_xattn_Wo"], "w_d1_q": g["L1_attn_Wq"],
        "w_d1_k": g["L1_attn_Wk"], "w_d1_v": g["L1_attn_Wv"], "w_d1_o": g["L1_attn_Wo"],
        "w_x1_q": g["L1_xattn_Wq"].T, "w_x1_k": g["L1_xattn_Wk"].T, "w_x1_v": g["L1_xattn_Wv"].T,
        "w_x1_o": g["L1_xattn_Wp"].T, "w_f0_r": g["L0_ffn_router_w"].T, "w_f1_r": g["L1_ffn_router_w"].T,
        "c_a0_q": g["L0_attn_bq"].reshape(D, 1), "c_a0_k": g["L0_attn_bk"].reshape(D, 1),
        "c_x0_q": g["L0_xattn_bq"].reshape(D, 1), "c_x0_k": g["L0_xattn_bk"].reshape(D, 1),
        "r_a0_v": g["L0_attn_bv"], "r_a0_o": g["L0_attn_bo"], "r_x0_v": g["L0_xattn_bv"], "r_x0_o": g["L0_xattn_bo"],
        "r_d1_g": g["L1_attn_gamma"], "r_d1_b": g["L1_attn_beta"], "r_x1_g": g["L1_xattn_ln_g"],
        "r_x1_b": g["L1_xattn_ln_b"], "r_x1_o": g["L1_xattn_bp"], "rbias": g["L1_ffn_routing_bias"],
        "gate": g["L1_xattn_gate"].reshape(H), "et_gate": g["L0_attn_et_gate"].reshape(1),
        "is_gate": g["L0_attn_is_gate"].reshape(1), "time_bias": g["L0_attn_time_bias"].reshape(1, TB),
        "lq1": g["L1_attn_lambda_q1"], "lk1": g["L1_attn_lambda_k1"], "lq2": g["L1_attn_lambda_q2"],
        "lk2": g["L1_attn_lambda_k2"], "w1": t(g["L0_ffn_w1"], (0, 2, 1)), "w2": t(g["L0_ffn_w2"], (0, 2, 1)),
        "wg": t(g["L1_ffn_wg"], (0, 2, 1)), "wu": t(g["L1_ffn_wu"], (0, 2, 1)), "wd": t(g["L1_ffn_wd"], (0, 2, 1)),
        "sg": g["L1_ffn_sg_w"].T, "su": g["L1_ffn_su_w"].T, "sd": g["L1_ffn_sd_w"].T,
    }
    nc = bacc.Bacc("TRN2", target_bir_lowering=False, num_devices=1)
    arrays, I = {}, {}
    for name, v in a.items():
        v = np.ascontiguousarray(v)
        arrays["in_" + name] = v
        I[name] = nc.dram_tensor("in_" + name, v.shape, mybir.dt.from_np(v.dtype), kind="ExternalInput").ap()
    out = nc.dram_tensor("out_0", (B, T, D), F32, kind="ExternalOutput").ap()
    decoder(nc, I, out)
    r = run(nc, [arrays], core_ids=[0])
    return r.results[0]["out_0"]
```
